# Optimizing a Trainium2 kernel written in Bass

```python
import numpy as np
import jax
import jax.numpy as jnp

def _softmax(x, axis=-1):
    return jax.nn.softmax(x, axis=axis)

def _gelu(x):
    return jax.nn.gelu(x, approximate=True)

def _silu(x):
    return jax.nn.silu(x)

def _sigmoid(x):
    return jax.nn.sigmoid(x)

def _layernorm(x, axis=-1, eps=1e-05):
    m = jnp.mean(x, axis=axis, keepdims=True)
    v = jnp.var(x, axis=axis, keepdims=True)
    return (x - m) / jnp.sqrt(v + eps)

def _scatter_add(tgt, idx, src, axis=0):
    return tgt.at[idx].add(src)

def _segment_sum(src, seg, n):
    return jax.ops.segment_sum(src, seg, n)
kernel_name = 'mk_early_fusion_d1_tok_img1024_r4_0d92e9'

def setup_inputs(seed: int=0):
    np.random.seed(seed)
    _w = jnp.asarray

    def _rec_inputs():
        import jax
        import jax.numpy as jnp
        _rk = jax.random.key(seed)
        x = -0.00016672 + 0.999947 * jax.random.normal(jax.random.fold_in(_rk, 1), (32, 3, 96, 96), jnp.float32)
        txt = 0.00140885 + 1.4139 * jax.random.normal(jax.random.fold_in(_rk, 2), (32, 77, 256), jnp.float32)
        return (x, txt)
    x, txt = _rec_inputs()

    def _L0_tok_setup():
        import jax, jax.numpy as jnp
        import numpy as np
        B, C, H, W = (64, 3, 96, 96)
        P = 16
        NP = H // P * (W // P)
        PD = C * P * P
        ED = 256
        NCLS = 1

        def _layernorm(x, g, b, eps=1e-05):
            mu = jnp.mean(x, axis=-1, keepdims=True)
            var = jnp.mean(jnp.square(x - mu), axis=-1, keepdims=True)
            return (x - mu) * jax.lax.rsqrt(var + eps) * g + b
        key = jax.random.key(seed)
        ks = jax.random.split(key, 8)
        x = jax.random.normal(ks[0], (B, C, H, W), dtype=jnp.float32)
        ln1_g = jnp.ones((PD,), jnp.float32)
        ln1_b = jnp.zeros((PD,), jnp.float32)
        W_proj = jax.random.normal(ks[1], (PD, ED), jnp.float32) / np.sqrt(PD)
        b_proj = jnp.zeros((ED,), jnp.float32)
        ln2_g = jnp.ones((ED,), jnp.float32)
        ln2_b = jnp.zeros((ED,), jnp.float32)
        cls_token = jax.random.normal(ks[2], (1, NCLS, ED), jnp.float32)
        pos_emb = jax.random.normal(ks[3], (1, NP + NCLS, ED), jnp.float32)
        return {'x': x, 'ln1_g': ln1_g, 'ln1_b': ln1_b, 'W_proj': W_proj, 'b_proj': b_proj, 'ln2_g': ln2_g, 'ln2_b': ln2_b, 'cls_token': cls_token, 'pos_emb': pos_emb}
    _L0_tok_all = _L0_tok_setup()
    _L0_tok_in = {k: v for k, v in _L0_tok_all.items() if k in ('ln1_g', 'ln1_b', 'W_proj', 'b_proj', 'ln2_g', 'ln2_b', 'cls_token', 'pos_emb')}
    del _L0_tok_all

    def _L0_attn_setup():
        import jax, jax.numpy as jnp
        import numpy as np
        B, N, D, H = (2, 512, 256, 8)
        HD = D // H
        EPS = 1e-06

        def _interleave(a, b):
            return jnp.stack([a, b], axis=2).reshape(a.shape[0], 2 * a.shape[1], a.shape[2], a.shape[3])

        def _l2norm(x):
            return x / jnp.sqrt(jnp.sum(x * x, axis=-1, keepdims=True) + EPS)

        def _dense_rnn(x, Wq, Wk, Wv, Wf1, Wf2, Wbeta, Wog1, Wog2, norm_w, Wo):
            b, n, d = x.shape
            q = jax.nn.silu(x @ Wq)
            k = jax.nn.silu(x @ Wk)
            v = jax.nn.silu(x @ Wv)
            f = x @ Wf1 @ Wf2
            log_f = jax.nn.log_sigmoid(f)
            beta = jax.nn.sigmoid(x @ Wbeta) * 2.0
            shp = (b, n, H, HD)
            q, k, v, log_f = (t.reshape(shp) for t in (q, k, v, log_f))
            k = _l2norm(k)
            k_ = -beta[..., None] * k
            zero = jnp.zeros(shp, x.dtype)
            gk = _interleave(log_f, zero)
            a = _interleave(k_ * jnp.exp(log_f), k_)
            bb = _interleave(k, k)
            kk = _interleave(zero, k)
            vv = _interleave(zero, v)
            qq = _interleave(zero, q)
            seq = tuple((jnp.moveaxis(t, 1, 0) for t in (gk, a, bb, kk, vv, qq)))
            S0 = jnp.zeros((b, H, HD, HD), x.dtype)

            def step(S, inp):
                g, a_t, b_t, k_t, v_t, q_t = inp
                bS = jnp.einsum('bhk,bhkv->bhv', b_t, S)
                S = jnp.exp(g)[..., None] * S + a_t[..., None] * bS[:, :, None, :] + k_t[..., None] * v_t[:, :, None, :]
                o = jnp.einsum('bhk,bhkv->bhv', q_t, S)
                return (S, o)
            _, o = jax.lax.scan(step, S0, seq)
            o = jnp.moveaxis(o, 0, 1)[:, 1::2]
            out = o.reshape(b, n, d)
            gate = x @ Wog1 @ Wog2
            y = out * jax.nn.sigmoid(gate)
            yh = y.reshape(b, n, H, HD)
            yh = yh / jnp.sqrt(jnp.mean(yh * yh, axis=-1, keepdims=True) + EPS)
            y = yh.reshape(b, n, d) * norm_w
            return y @ Wo
        key = jax.random.key(seed)
        ks = jax.random.split(key, 11)
        std = 0.02
        w = lambda k, shape: jax.random.normal(k, shape, dtype=jnp.float32) * std
        return {'x': jax.random.normal(ks[0], (B, N, D), dtype=jnp.float32), 'Wq': w(ks[1], (D, D)), 'Wk': w(ks[2], (D, D)), 'Wv': w(ks[3], (D, D)), 'Wf1': w(ks[4], (D, HD)), 'Wf2': w(ks[5], (HD, D)), 'Wbeta': w(ks[6], (D, H)), 'Wog1': w(ks[7], (D, HD)), 'Wog2': w(ks[8], (HD, D)), 'norm_w': jnp.ones((D,), dtype=jnp.float32), 'Wo': w(ks[9], (D, D))}
    _L0_attn_all = _L0_attn_setup()
    _L0_attn_in = {k: v for k, v in _L0_attn_all.items() if k in ('Wq', 'Wk', 'Wv', 'Wf1', 'Wf2', 'Wbeta', 'Wog1', 'Wog2', 'norm_w', 'Wo')}
    del _L0_attn_all

    def _L0_ffn_setup():
        import jax, jax.numpy as jnp
        import numpy as np
        T, Z, D_DIM = (8, 512, 256)
        N_EXP, P_SLOT, H = (64, 32, 256)
        LN_EPS = 1e-05
        key = jax.random.key(seed)
        k = jax.random.split(key, 5)
        s = 0.02
        return {'x': jax.random.normal(k[0], (T, Z, D_DIM), dtype=jnp.float32), 'phi_w': jax.random.normal(k[1], (N_EXP * P_SLOT, D_DIM), dtype=jnp.float32) * s, 'phi_b': jax.random.normal(k[2], (N_EXP * P_SLOT,), dtype=jnp.float32) * s, 'expert_w': jax.random.normal(k[3], (N_EXP, D_DIM, H), dtype=jnp.float32) * s, 'expert_b': jax.random.normal(k[4], (N_EXP, H), dtype=jnp.float32) * s}
    _L0_ffn_all = _L0_ffn_setup()
    _L0_ffn_in = {k: v for k, v in _L0_ffn_all.items() if k in ('phi_w', 'phi_b', 'expert_w', 'expert_b')}
    del _L0_ffn_all
    return {'x': x, 'txt': txt, 'L0_tok_ln1_g': _L0_tok_in['ln1_g'], 'L0_tok_ln1_b': _L0_tok_in['ln1_b'], 'L0_tok_W_proj': _L0_tok_in['W_proj'], 'L0_tok_b_proj': _L0_tok_in['b_proj'], 'L0_tok_ln2_g': _L0_tok_in['ln2_g'], 'L0_tok_ln2_b': _L0_tok_in['ln2_b'], 'L0_tok_cls_token': _L0_tok_in['cls_token'], 'L0_tok_pos_emb': _L0_tok_in['pos_emb'], 'L0_attn_Wq': _L0_attn_in['Wq'], 'L0_attn_Wk': _L0_attn_in['Wk'], 'L0_attn_Wv': _L0_attn_in['Wv'], 'L0_attn_Wf1': _L0_attn_in['Wf1'], 'L0_attn_Wf2': _L0_attn_in['Wf2'], 'L0_attn_Wbeta': _L0_attn_in['Wbeta'], 'L0_attn_Wog1': _L0_attn_in['Wog1'], 'L0_attn_Wog2': _L0_attn_in['Wog2'], 'L0_attn_norm_w': _L0_attn_in['norm_w'], 'L0_attn_Wo': _L0_attn_in['Wo'], 'L0_ffn_phi_w': _L0_ffn_in['phi_w'], 'L0_ffn_phi_b': _L0_ffn_in['phi_b'], 'L0_ffn_expert_w': _L0_ffn_in['expert_w'], 'L0_ffn_expert_b': _L0_ffn_in['expert_b']}

def reference(x, txt, L0_tok_ln1_g, L0_tok_ln1_b, L0_tok_W_proj, L0_tok_b_proj, L0_tok_ln2_g, L0_tok_ln2_b, L0_tok_cls_token, L0_tok_pos_emb, L0_attn_Wq, L0_attn_Wk, L0_attn_Wv, L0_attn_Wf1, L0_attn_Wf2, L0_attn_Wbeta, L0_attn_Wog1, L0_attn_Wog2, L0_attn_norm_w, L0_attn_Wo, L0_ffn_phi_w, L0_ffn_phi_b, L0_ffn_expert_w, L0_ffn_expert_b):
    import jax
    import jax.numpy as jnp

    def _L0_tok_ref(x, ln1_g, ln1_b, W_proj, b_proj, ln2_g, ln2_b, cls_token, pos_emb):
        import jax, jax.numpy as jnp
        import numpy as np
        B, C, H, W = (64, 3, 96, 96)
        P = 16
        NP = H // P * (W // P)
        PD = C * P * P
        ED = 256
        NCLS = 1

        def _layernorm(x, g, b, eps=1e-05):
            mu = jnp.mean(x, axis=-1, keepdims=True)
            var = jnp.mean(jnp.square(x - mu), axis=-1, keepdims=True)
            return (x - mu) * jax.lax.rsqrt(var + eps) * g + b
        b = x.shape[0]
        h, w = (H // P, W // P)
        patches = x.reshape(b, C, h, P, w, P)
        patches = patches.transpose(0, 2, 4, 3, 5, 1).reshape(b, h * w, P * P * C)
        z = _layernorm(patches, ln1_g, ln1_b)
        z = jnp.einsum('bnp,pe->bne', z, W_proj) + b_proj
        z = _layernorm(z, ln2_g, ln2_b)
        cls = jnp.broadcast_to(cls_token, (b, NCLS, ED))
        z = jnp.concatenate([cls, z], axis=1)
        z = z + pos_emb
        return z

    def _L0_attn_ref(x, Wq, Wk, Wv, Wf1, Wf2, Wbeta, Wog1, Wog2, norm_w, Wo):
        import jax, jax.numpy as jnp
        import numpy as np
        B, N, D, H = (2, 512, 256, 8)
        HD = D // H
        EPS = 1e-06

        def _interleave(a, b):
            return jnp.stack([a, b], axis=2).reshape(a.shape[0], 2 * a.shape[1], a.shape[2], a.shape[3])

        def _l2norm(x):
            return x / jnp.sqrt(jnp.sum(x * x, axis=-1, keepdims=True) + EPS)

        def _dense_rnn(x, Wq, Wk, Wv, Wf1, Wf2, Wbeta, Wog1, Wog2, norm_w, Wo):
            b, n, d = x.shape
            q = jax.nn.silu(x @ Wq)
            k = jax.nn.silu(x @ Wk)
            v = jax.nn.silu(x @ Wv)
            f = x @ Wf1 @ Wf2
            log_f = jax.nn.log_sigmoid(f)
            beta = jax.nn.sigmoid(x @ Wbeta) * 2.0
            shp = (b, n, H, HD)
            q, k, v, log_f = (t.reshape(shp) for t in (q, k, v, log_f))
            k = _l2norm(k)
            k_ = -beta[..., None] * k
            zero = jnp.zeros(shp, x.dtype)
            gk = _interleave(log_f, zero)
            a = _interleave(k_ * jnp.exp(log_f), k_)
            bb = _interleave(k, k)
            kk = _interleave(zero, k)
            vv = _interleave(zero, v)
            qq = _interleave(zero, q)
            seq = tuple((jnp.moveaxis(t, 1, 0) for t in (gk, a, bb, kk, vv, qq)))
            S0 = jnp.zeros((b, H, HD, HD), x.dtype)

            def step(S, inp):
                g, a_t, b_t, k_t, v_t, q_t = inp
                bS = jnp.einsum('bhk,bhkv->bhv', b_t, S)
                S = jnp.exp(g)[..., None] * S + a_t[..., None] * bS[:, :, None, :] + k_t[..., None] * v_t[:, :, None, :]
                o = jnp.einsum('bhk,bhkv->bhv', q_t, S)
                return (S, o)
            _, o = jax.lax.scan(step, S0, seq)
            o = jnp.moveaxis(o, 0, 1)[:, 1::2]
            out = o.reshape(b, n, d)
            gate = x @ Wog1 @ Wog2
            y = out * jax.nn.sigmoid(gate)
            yh = y.reshape(b, n, H, HD)
            yh = yh / jnp.sqrt(jnp.mean(yh * yh, axis=-1, keepdims=True) + EPS)
            y = yh.reshape(b, n, d) * norm_w
            return y @ Wo
        return _dense_rnn(x, Wq, Wk, Wv, Wf1, Wf2, Wbeta, Wog1, Wog2, norm_w, Wo)

    def _L0_ffn_ref(x, phi_w, phi_b, expert_w, expert_b):
        import jax, jax.numpy as jnp
        import numpy as np
        T, Z, D_DIM = (8, 512, 256)
        N_EXP, P_SLOT, H = (64, 32, 256)
        LN_EPS = 1e-05
        t, z, d = x.shape
        n = expert_w.shape[0]
        p = phi_w.shape[0] // n
        logits = (jnp.einsum('tzd,ed->tze', x, phi_w) + phi_b).reshape(t, z, n, p)
        D = jax.nn.softmax(logits, axis=3)
        C = jax.nn.softmax(logits, axis=2)
        X_tilde = jnp.einsum('tznp,tzd->npd', D, x)
        X_tilde = jnp.clip(X_tilde, -33000.0, 65000.0)
        mu = jnp.mean(X_tilde, axis=-1, keepdims=True)
        var = jnp.mean(jnp.square(X_tilde - mu), axis=-1, keepdims=True)
        X_tilde = (X_tilde - mu) * jax.lax.rsqrt(var + LN_EPS)
        X_tilde = jnp.tanh(X_tilde)
        Y_tilde = jnp.einsum('npd,ndH->npH', X_tilde, expert_w) + expert_b[:, None, :]
        Y = jnp.einsum('tznp,npH->tzH', C, Y_tilde)
        return Y
    h = _L0_tok_ref(x, L0_tok_ln1_g, L0_tok_ln1_b, L0_tok_W_proj, L0_tok_b_proj, L0_tok_ln2_g, L0_tok_ln2_b, L0_tok_cls_token, L0_tok_pos_emb)
    h = jnp.concatenate([h, txt], axis=1)
    h = h + _L0_attn_ref(_layernorm(h, axis=-1), L0_attn_Wq, L0_attn_Wk, L0_attn_Wv, L0_attn_Wf1, L0_attn_Wf2, L0_attn_Wbeta, L0_attn_Wog1, L0_attn_Wog2, L0_attn_norm_w, L0_attn_Wo)
    h = h + _L0_ffn_ref(_layernorm(h, axis=-1), L0_ffn_phi_w, L0_ffn_phi_b, L0_ffn_expert_w, L0_ffn_expert_b)
    return h

_drawn_inputs = setup_inputs


def setup_inputs(seed=0):
    import zlib

    import numpy as np

    out = dict(_drawn_inputs(seed))
    spreads = {'L0_tok_ln1_g': (1.0, 0.2),
     'L0_tok_ln1_b': (0.0, 0.1),
     'L0_tok_b_proj': (0.0, 0.1),
     'L0_tok_ln2_g': (1.0, 0.2),
     'L0_tok_ln2_b': (0.0, 0.1),
     'L0_attn_norm_w': (1.0, 0.2)}
    factors = {'L0_attn_Wf1': 8.0,
     'L0_attn_Wf2': 8.0,
     'L0_attn_Wbeta': 23.851,
     'L0_attn_Wog1': 8.0,
     'L0_attn_Wog2': 8.0,
     'L0_ffn_phi_b': 34.346}
    for name, (base, spread) in spreads.items():
        noise = np.random.default_rng([zlib.crc32(name.encode()), seed]).standard_normal(out[name].shape)
        drawn = base * np.exp(spread * noise) if base else spread * noise
        out[name] = jnp.asarray(drawn.astype(out[name].dtype))
    for name, factor in factors.items():
        out[name] = (out[name] * factor).astype(out[name].dtype)
    return out
```

```python
import concourse.bass as bass
from concourse import mybir
from contextlib import ExitStack

F32 = mybir.dt.float32
BF16 = mybir.dt.bfloat16
I32 = mybir.dt.int32
ALU = mybir.AluOpType
ACT = mybir.ActivationFunctionType
AX = mybir.AxisListType

B, NTXT, D = 32, 77, 256
GRID, NPOS = 6, 36
PD = 768
N = 1 + NPOS + NTXT
H, HD = 8, 32
T = 16
NC = 8
NT = NC * T
V = 2 * T
GB = 8
NG = B // GB
LV = 5
W = V + T
NEXP, PS = 64, 32
NS = NEXP * PS
ST = NS // 128
LN_EPS, QK_EPS = 1e-5, 1e-6
UP = [2 * T] + [W // 2] * (LV - 1)
KIN, KOUT, Q_E, A_T = 0, 2 * V, 4 * V, 4 * V + 2 * T
SLAB = 4 * V + 4 * T
LN_EXP, SILU, SIGMOID = "natural_log_exp_and_others", "silu_and_others", "sigmoid_and_others"


class Steps:

    def __init__(self, engine, sem):
        self.engine, self.sem, self.n = engine, sem, 0

    def mark(self, ins):
        self.n += 1
        ins.then_inc(self.sem, 1)
        return self.n

    def wait(self, n=None):
        self.engine.wait_ge(self.sem, self.n if n is None else n)

    def link(self, ins):
        self.mark(ins)
        self.wait()

    def restart(self):
        self.wait()
        self.engine.sem_clear(self.sem)
        self.n = 0


class Memory:
    def __init__(self, nc, ctx):
        self.nc, self.ctx = nc, ctx

    def sb(self, name, shape, dt=F32):
        return self.ctx.enter_context(self.nc.sbuf_tensor(name, shape, dt))

    def ps(self, name, shape=(128, 512), dt=F32):
        return self.ctx.enter_context(self.nc.psum_tensor(name, list(shape), dt))

    def sem(self, name):
        return self.ctx.enter_context(self.nc.semaphore(name))


def hold(engine, sem, value, passed):
    engine.wait_ge(sem, value)
    engine.sem_inc(passed, 1)


def inverse_root(nc, steps, out, x, eps):
    steps.link(nc.scalar.activation(out, x, ACT.Ln, bias=eps))
    return nc.scalar.activation(out, out, ACT.Exp, scale=-0.5)


def tokenizer(nc, a, scratch):
    TILES = B * NPOS // 128
    KT = PD // 128
    with ExitStack() as ctx:
        m = Memory(nc, ctx)
        wp = m.sb("wp", [128, KT, D])
        g1, b1 = m.sb("g1", [128, KT]), m.sb("b1", [128, KT])
        bproj, g2, b2 = m.sb("bproj", [128, D]), m.sb("g2", [128, D]), m.sb("b2", [128, D])
        pos = m.sb("pos", [128, TILES, D])
        cls, pos0 = m.sb("cls", [32, D]), m.sb("pos0", [32, D])
        ident = m.sb("ident_tok", [128, 128])
        patch = m.sb("patch", [128, PD])
        stats, mv, rstd = m.sb("tok_stats", [128, 12]), m.sb("tok_mv", [128, 2]), m.sb("tok_rstd", [128, 1])
        stats2, mv2, rstd2 = m.sb("tok_stats2", [128, 6]), m.sb("tok_mv2", [128, 2]), m.sb("tok_rstd2", [128, 1])
        xn = m.sb("tok_xn", [128, PD])
        xnT = m.sb("tok_xnT", [128, KT, 128])
        z, zo = m.sb("tok_z", [128, D]), m.sb("tok_zo", [128, D])
        pT = [m.ps(f"pT{i}") for i in range(2)]
        pZ = m.ps("pZ")
        consts, loaded, moments, rstds = m.sem("tok_consts"), m.sem("tok_loaded"), m.sem("tok_moments"), m.sem("tok_rstds")
        normed, transposed, evacuated, projected = m.sem("tok_normed"), m.sem("tok_transposed"), m.sem("tok_evacuated"), m.sem("tok_projected")
        z_ready, stored, dve_steps = m.sem("z_ready"), m.sem("tok_stored"), m.sem("tok_dve_steps")
        cls_ready, cls_stored, act_steps, passed_pe = m.sem("cls_ready"), m.sem("cls_stored"), m.sem("tok_act_steps"), m.sem("tok_passed_pe")
        block = ctx.enter_context(nc.Block())
        n_consts = 16 * (9 + 4)

        @block.sync
        def _(sp):
            sp.dma_start(wp[:], a.W_proj.rearrange("(k p) e -> p k e", p=128)).then_inc(consts, 16)
            sp.dma_start(g1[:], a.ln1_g).then_inc(consts, 16)
            sp.dma_start(b1[:], a.ln1_b).then_inc(consts, 16)
            sp.dma_start(bproj[:], a.b_proj.partition_broadcast(128)).then_inc(consts, 16)
            sp.dma_start(g2[:], a.ln2_g.partition_broadcast(128)).then_inc(consts, 16)
            sp.dma_start(b2[:], a.ln2_b.partition_broadcast(128)).then_inc(consts, 16)
            sp.dma_start(cls[:], a.cls_token.partition_broadcast(32)).then_inc(consts, 16)
            sp.dma_start(pos0[:], a.pos_emb[0].partition_broadcast(32)).then_inc(consts, 16)
            sp.dma_start(ident[:], a.ident).then_inc(consts, 16)
            by_tile = a.pos_emb[1:1 + NPOS].rearrange("(j q) e -> q j e", q=4)
            for q in range(4):
                sp.dma_start(pos[32 * q:32 * q + 32], by_tile[q].partition_broadcast(32)).then_inc(consts, 16)
            sp.wait_ge(cls_ready, 1)
            sp.dma_start(scratch.z[:, 0, :], cls[:]).then_inc(cls_stored, 16)
            with sp.Fori(0, TILES) as j:
                sp.wait_ge(normed, j)
                sp.dma_start(patch[:], a.patches[j]).then_inc(loaded, 16)
            sp.wait_ge(cls_stored, 16)

        @block.gpsimd
        def _(pool):
            with pool.Fori(0, TILES) as j:
                pool.wait_ge(z_ready, j + 1)
                for q in range(4):
                    pool.dma_start(scratch.z[:, 1 + 4 * j + q, :], zo[32 * q:32 * q + 32]).then_inc(stored, 16)
            pool.wait_ge(stored, 64 * TILES)

        @block.vector
        def _(dve):
            steps = Steps(dve, dve_steps)
            dve.wait_ge(consts, n_consts)
            nc.vector.tensor_tensor(cls[:], cls[:], pos0[:], ALU.add).then_inc(cls_ready, 1)
            steps.link(nc.vector.tensor_tensor(pos[:], pos[:], b2[:].unsqueeze(1).to_broadcast([128, TILES, D]), ALU.add))
            steps.restart()
            with dve.Fori(0, TILES) as j:
                dve.wait_ge(loaded, 16 * (j + 1))
                for i in range(2):
                    steps.mark(nc.vector.bn_stats(stats[:, 6 * i:6 * i + 6], patch[:, 384 * i:384 * i + 384]))
                steps.wait()
                nc.vector.bn_aggr(mv[:], stats[:]).then_inc(moments, 1)
                dve.wait_ge(rstds, 2 * j + 1)
                dve.wait_ge(transposed, j)
                nc.vector.tensor_scalar(xn[:], patch[:], mv[:, 0:1], rstd[:], ALU.subtract, ALU.mult).then_inc(normed, 1)
                dve.wait_ge(projected, j + 1)
                steps.link(nc.vector.tensor_tensor(z[:], pZ[:, 0:D], bproj[:], ALU.add))
                steps.link(nc.vector.bn_stats(stats2[:], z[:]))
                nc.vector.bn_aggr(mv2[:], stats2[:]).then_inc(moments, 1)
                dve.wait_ge(rstds, 2 * j + 2)
                steps.link(nc.vector.tensor_scalar(z[:], z[:], mv2[:, 0:1], rstd2[:], ALU.subtract, ALU.mult))
                steps.link(nc.vector.tensor_tensor(z[:], z[:], g2[:], ALU.mult))
                dve.wait_ge(stored, 64 * j)
                nc.vector.tensor_tensor(zo[:], z[:], pos[:, j, :], ALU.add).then_inc(z_ready, 1)
                steps.restart()

        @block.tensor
        def _(pe):
            pe.wait_ge(consts, n_consts)
            with pe.Fori(0, TILES) as j:
                hold(pe, normed, j + 1, passed_pe)
                hold(pe, evacuated, j, passed_pe)
                for k in range(KT):
                    last = nc.tensor.transpose(pT[k // 4][:, 128 * (k % 4):128 * (k % 4) + 128], xn[:, 128 * k:128 * k + 128], ident[:])
                last.then_inc(transposed, 1)
                hold(pe, evacuated, j + 1, passed_pe)
                hold(pe, moments, 2 * j, passed_pe)
                for k in range(KT):
                    last = nc.tensor.matmul(pZ[:, 0:D], xnT[:, k, :], wp[:, k, :], start=k == 0, stop=k == KT - 1)
                last.then_inc(projected, 1)

        @block.scalar
        def _(act):
            steps = Steps(act, act_steps)
            act.wait_ge(consts, n_consts)
            nc.scalar.preload_act_table_set(LN_EXP)
            with act.Fori(0, TILES) as j:
                act.wait_ge(moments, 2 * j + 1)
                inverse_root(nc, steps, rstd[:], mv[:, 1:2], LN_EPS).then_inc(rstds, 1)
                act.wait_ge(transposed, j + 1)
                act.wait_ge(projected, j)
                for k in range(KT):
                    last = nc.scalar.activation(xnT[:, k, :], pT[k // 4][:, 128 * (k % 4):128 * (k % 4) + 128],
                                                ACT.Identity, bias=b1[:, k:k + 1], scale=g1[:, k:k + 1])
                last.then_inc(evacuated, 1)
                act.wait_ge(moments, 2 * j + 2)
                inverse_root(nc, steps, rstd2[:], mv2[:, 1:2], LN_EPS).then_inc(rstds, 1)
                steps.restart()


def attention(nc, a, scratch):
    with ExitStack() as ctx:
        m = Memory(nc, ctx)
        wq, wk, wv = m.sb("wq", [128, 2, D]), m.sb("wk", [128, 2, D]), m.sb("wv", [128, 2, D])
        wfg = m.sb("wfg", [128, 2, 2 * HD])
        wf2, wog2 = m.sb("wf2", [HD, D]), m.sb("wog2", [HD, D])
        wb8, wb = m.sb("wb8", [128, 2, H]), m.sb("wb", [128, 2, D])
        ident, head_ones = m.sb("ident_att", [128, 128]), m.sb("head_ones", [128, 128])
        levels = m.sb("levels", [128, LV, 2 * T], I32)
        in_chunk = m.sb("in_chunk", [128, 2 * NC * V])
        hx = m.sb("hx", [128, D])
        stats, mv, rstd = m.sb("stats", [128, 6]), m.sb("mv", [128, 2]), m.sb("rstd", [128, 1])
        xn, xT = m.sb("xn", [128, D]), m.sb("xT", [128, 2, NT])
        fg = m.sb("fg", [HD, 2, NT])
        q, kraw, k2, k = m.sb("q", [128, D]), m.sb("kraw", [128, D]), m.sb("k2", [128, D]), m.sb("k", [128, D])
        kr, vt, gate = m.sb("kr", [128, D]), m.sb("vt", [128, D]), m.sb("gate", [128, D])
        tanh_beta, tanh_gate = m.sb("tanh_beta", [128, D]), m.sb("tanh_gate", [128, D])
        nbeta, nbk = m.sb("nbeta", [128, D]), m.sb("nbk", [128, D])
        fabs, flog = m.sb("fabs", [128, D]), m.sb("flog", [128, D])
        decay = m.sb("decay", [128, 2 * NC * V])
        L = m.sb("L", [128, 2 * NC * V])
        fac, facin = m.sb("fac", [128, LV + 1, 2 * NC * V]), m.sb("facin", [128, 2 * NC * V])
        diff = fac
        lower = m.sb("lower", [128, LV, 2 * NC, V])
        above = [m.sb(f"above{l}", [128, 2 * NC * UP[l]]) for l in range(LV)]
        kout, koutT = m.sb("kout", [128, 2 * NC * V]), m.sb("koutT", [128, 2 * NC * V])
        PA = m.sb("PA", [128, 2, NC, W])
        kiq, at = m.sb("kiq", [128, NC, A_T]), m.sb("at", [128, NC, SLAB - A_T])
        Pb = m.sb("Pb", [128, V, 128])
        LP = Pb
        X = m.sb("X", [128, V, 128])
        XT = m.sb("XT", [128, NC, 2 * GB * V])
        tmp = m.sb("tmp", [128, 4 * (V - 1) ** 2])
        eg = m.sb("eg", [128, NC, 2 * (B + 1)])
        stage = [m.sb(f"stage{i}", [128, GB, SLAB]) for i in range(2)]
        xst = [m.sb(f"xst{i}", [128, 2 * GB * V]) for i in range(2)]
        vst = [m.sb(f"vst{i}", [128, 512]) for i in range(2)]
        S = [m.sb(f"S{i}", [128, 512]) for i in range(2)]
        tS, R, U, O = m.sb("tS", [128, 512]), m.sb("R", [128, 512]), m.sb("U", [128, 512]), m.sb("O", [128, 512])
        bank = [m.ps(f"bank{i}") for i in range(8)]
        b_x, b_qk, b_vb, b_fg = bank[4:8]
        ring = bank[0:4]

        consts, wb_ready, zeroed = m.sem("consts"), m.sem("wb_ready"), m.sem("zeroed")
        loaded, moments, rstds, normed = m.sem("loaded"), m.sem("moments"), m.sem("rstds"), m.sem("normed")
        pe_x, x_ready, pe_fg, fg_ready = m.sem("pe_x"), m.sem("x_ready"), m.sem("pe_fg"), m.sem("fg_ready")
        pe_proj, act_proj, k2_ready, pe_ss = m.sem("pe_proj"), m.sem("act_proj"), m.sem("k2_ready"), m.sem("pe_ss")
        k_ready, kr_ready, flog_ready = m.sem("k_ready"), m.sem("kr_ready"), m.sem("flog_ready")
        diff_ready, fac_ready, kq_ready = m.sem("diff_ready"), m.sem("fac_ready"), m.sem("kq_ready")
        scores, taken = m.sem("scores"), m.sem("taken")
        v_out, gate_out, kiq_out, at_out = m.sem("v_out"), m.sem("gate_out"), m.sem("kiq_out"), m.sem("at_out")
        gate_ready, nb_ready, pool_done = m.sem("gate_ready"), m.sem("nb_ready"), m.sem("pool_done")
        pa_ready, at_copied, kout_ready, kout_copied = m.sem("pa_ready"), m.sem("at_copied"), m.sem("kout_ready"), m.sem("kout_copied")
        lane_ps, lane_sb, inverted = m.sem("lane_ps"), m.sem("lane_sb"), m.sem("inverted")
        xt_ps, xt_sb = m.sem("xt_ps"), m.sem("xt_sb")
        staged, v_staged = [m.sem("staged0"), m.sem("staged1")], [m.sem("v_staged0"), m.sem("v_staged1")]
        R_ps, R_sb, U_ps, U_sb = m.sem("R_ps"), m.sem("R_sb"), m.sem("U_ps"), m.sem("U_sb")
        S_ps, S_sb, O_ps, O_sb, o_out = m.sem("S_ps"), m.sem("S_sb"), m.sem("O_ps"), m.sem("O_sb"), m.sem("o_out")
        tS_ready, R_copied, S_copied = m.sem("tS_ready"), m.sem("R_copied"), m.sem("S_copied")
        act_steps, dve_steps, pool_steps, passed = m.sem("act_steps"), m.sem("dve_steps"), m.sem("pool_steps"), m.sem("passed")
        block = ctx.enter_context(nc.Block())

        def chunks(x):
            return x.rearrange("p (g c w) -> p g c w", g=2, c=NC)

        def tokens(x):
            return x.rearrange("p (n t) -> p n t", t=T)

        def upper(x, l):
            if l == 0:
                return x.rearrange("p c (t k) -> p c t k", k=3)[:, :, :, 1:]
            return x.rearrange("p c (s u k) -> p c s u k", u=2, k=3 << (l - 1))[:, :, :, 1]

        def fronts(g):
            return GB * (g + 1) + 1

        def groups(first, project, invert, finish, sweep):
            first()
            project(0)
            invert(0)
            finish(0)
            with block_engine[0].Fori(0, NG - 1) as g:
                project(g + 1)
                invert(g + 1)
                sweep(g)
                finish(g + 1)
            sweep(NG - 1)

        block_engine = [None]

        @block.sync
        def _(sp):
            block_engine[0] = sp
            for dst, src in ((wq, a.Wq), (wk, a.Wk), (wv, a.Wv), (wb8, a.Wbeta)):
                sp.dma_start(dst[:], src.rearrange("(t p) n -> p t n", p=128)).then_inc(consts, 16)
            sp.dma_start(wfg[:, :, 0:HD], a.Wf1.rearrange("(t p) n -> p t n", p=128)).then_inc(consts, 16)
            sp.dma_start(wfg[:, :, HD:], a.Wog1.rearrange("(t p) n -> p t n", p=128)).then_inc(consts, 16)
            sp.dma_start(wf2[:], a.Wf2).then_inc(consts, 16)
            sp.dma_start(wog2[:], a.Wog2).then_inc(consts, 16)
            sp.dma_start(ident[:], a.ident).then_inc(consts, 16)
            sp.dma_start(head_ones[:], a.head_ones).then_inc(consts, 16)
            sp.dma_start(levels[:], a.levels.rearrange("p (l w) -> p l w", l=LV)).then_inc(consts, 16)
            sp.dma_start(in_chunk[:], a.in_chunk).then_inc(consts, 16)

            def load(y, at_batch):
                if not (isinstance(y, int) and y == 0):
                    hold(sp, normed, y, passed)
                sp.dma_start(hx[0:1 + NPOS], scratch.z[at_batch]).then_inc(loaded, 16)
                sp.dma_start(hx[1 + NPOS:N], a.txt[at_batch]).then_inc(loaded, 16)

            def store_front(x):
                hold(sp, gate_ready, x + 1, passed)
                hold(sp, act_proj, 3 * x + 3, passed)
                sp.dma_start(scratch.v[x].rearrange("g t w -> t g w"), vt[:].rearrange("p (g w) -> p g w", g=2)).then_inc(v_out, 16)
                sp.dma_start(scratch.gate[x], gate[:]).then_inc(gate_out, 16)
                hold(sp, pool_done, 5 * (x + 1), passed)
                hold(sp, kout_copied, x + 1, passed)
                sp.dma_start(scratch.slab[:, :, x, 0:A_T].rearrange("c p w -> p c w"), kiq[:]).then_inc(kiq_out, 16)

            def first():
                load(0, 0)
                load(1, 1)
                store_front(0)

            def project(g):
                with sp.Fori(0, GB) as b:
                    it = g * GB + b
                    load(it + 2, (it + 2) % B)
                    store_front(it + 1)
                    hold(sp, at_copied, it + 1, passed)
                    sp.dma_start(scratch.slab[:, :, it, A_T:].rearrange("c p w -> p c w"), at[:]).then_inc(at_out, 16)

            values = scratch.v.rearrange("b g (c t) (h w) -> h c t (b g) w", c=NC, h=4)

            def sweep(g):
                hold(sp, v_out, 16 * (fronts(g + 1) if not isinstance(g, int) else fronts(g)), passed)
                hold(sp, kiq_out, 16 * (fronts(g + 1) if not isinstance(g, int) else fronts(g)), passed)
                hold(sp, at_out, 16 * GB * ((g + 2) if not isinstance(g, int) else NG), passed)
                hold(sp, xt_sb, 8 * (g + 1), passed)
                with sp.Fori(0, NC // 2) as c2:
                    for i in range(2):
                        c = c2 * 2 + i
                        n = g * NC + c
                        hold(sp, O_ps, 2 * n, passed)
                        sp.dma_start(stage[i][:], scratch.slab[c, :, bass.ds(g * GB, GB), :]).then_inc(staged[i], 16)
                        sp.dma_start(xst[i][:], XT[:, c, :]).then_inc(staged[i], 16)
                        sp.wait_ge(zeroed, 4)
                        for h in range(4):
                            sp.dma_start(vst[i][32 * h + 1:32 * h + 32:2].rearrange("p (y w) -> p y w", y=2 * GB),
                                         values[h, c, :, bass.ds(g * (2 * GB), 2 * GB), :]).then_inc(v_staged[i], 16)

            groups(first, project, lambda g: None, lambda g: None, sweep)
            sp.wait_ge(gate_out, 16 * (B + 1))
            sp.wait_ge(v_out, 16 * (B + 1))
            sp.wait_ge(kiq_out, 16 * (B + 1))
            sp.wait_ge(at_out, 16 * B)

        @block.tensor
        def _(pe):
            block_engine[0] = pe

            def wait(sem, value):
                if not (isinstance(value, int) and value <= 0):
                    hold(pe, sem, value, passed)

            pe.wait_ge(consts, 16 * 12)
            pe.wait_ge(wb_ready, 1)
            pe.wait_ge(zeroed, 4)
            pe.sem_inc(O_ps, 2)

            def transposes(y):
                wait(normed, y + 1)
                wait(kr_ready, y - 1)
                for t in range(2):
                    last = nc.tensor.transpose(b_x[:, 128 * t:128 * t + N], xn[0:N, 128 * t:128 * t + 128], ident[0:N, 0:N])
                last.then_inc(pe_x, 1)

            def project_qk(x):
                wait(x_ready, x + 1)
                wait(kr_ready, x)
                wait(act_proj, 3 * x)
                for j in range(2):
                    for t in range(2):
                        last = nc.tensor.matmul(b_x[0:HD, 256 + 128 * j:384 + 128 * j], wfg[:, t, HD * j:HD * j + HD], xT[:, t, :], start=t == 0, stop=t == 1)
                last.then_inc(pe_fg, 1)
                for w, at_col in ((wk, D), (wq, 0)):
                    for hg in range(2):
                        for t in range(2):
                            last = nc.tensor.matmul(b_qk[:, at_col + 128 * hg:at_col + 128 * hg + 128], w[:, t, 128 * hg:128 * hg + 128], xT[:, t, :], start=t == 0, stop=t == 1)
                last.then_inc(pe_proj, 1)

            def project_rest(x):
                for t in range(2):
                    nc.tensor.matmul(b_vb[:, 0:D], xT[:, t, :], wv[:, t, :], start=t == 0, stop=t == 1)
                for hg in range(2):
                    for t in range(2):
                        last = nc.tensor.matmul(b_vb[:, D + 128 * hg:D + 128 * hg + 128], wb[:, t, 128 * hg:128 * hg + 128], xT[:, t, :], start=t == 0, stop=t == 1)
                last.then_inc(pe_proj, 1)
                wait(fg_ready, x + 1)
                wait(flog_ready, x)
                for hg in range(2):
                    nc.tensor.matmul(b_fg[:, 128 * hg:128 * hg + 128], wf2[:, 128 * hg:128 * hg + 128], fg[:, 0, :], start=True, stop=True)
                nc.tensor.matmul(b_fg[:, D:], fg[:, 1, :], wog2[:], start=True, stop=True).then_inc(pe_proj, 1)

            def squares(x):
                wait(k2_ready, x + 1)
                nc.tensor.matmul(b_x[:, 0:D], head_ones[:], k2[:], start=True, stop=True).then_inc(pe_ss, 1)

            def score(it, n):
                l, hg = n // 2, n % 2
                if hg == 0:
                    wait(kq_ready, 3 * (LV * it + l + 1))
                wait(taken, 2 * LV * it + max(0, n - 3))
                for c in range(NC):
                    for h in range(4):
                        r = slice(32 * h, 32 * h + 32)
                        last = nc.tensor.matmul(ring[n % 4][r, 32 * c:32 * c + UP[l]], lower[r, l, hg * NC + c, :], above[l][r, UP[l] * (hg * NC + c):UP[l] * (hg * NC + c) + UP[l]], start=True, stop=True)
                last.then_inc(scores, 1)

            def first():
                transposes(0)
                project_qk(0)
                project_rest(0)
                squares(0)
                transposes(1)

            def project(g):
                wait(O_sb, 2 * NC * (g - 1 if not isinstance(g, int) else 0))
                wait(S_sb, 18 * (g - 1 if not isinstance(g, int) else 0))
                wait(xt_sb, 8 * g)
                with pe.Fori(0, GB) as b:
                    it = g * GB + b
                    project_qk(it + 1)
                    score(it, 0)
                    score(it, 1)
                    project_rest(it + 1)
                    score(it, 2)
                    squares(it + 1)
                    for n in range(3, 6):
                        score(it, n)
                    transposes(it + 2)
                    for n in range(6, 2 * LV):
                        score(it, n)
                wait(pa_ready, 2 * GB * (g + 1))
                wait(taken, 2 * LV * GB * (g + 1))
                for n in range(V // 4):
                    if n >= 4:
                        wait(lane_sb, 8 * g + n - 3)
                    for i in range(4):
                        last = nc.tensor.transpose(ring[n % 4][:, 128 * i:128 * i + 128], Pb[:, 4 * n + i, :], ident[:])
                    last.then_inc(lane_ps, 1)

            def finish(g):
                wait(inverted, g + 1)
                wait(lane_sb, 8 * (g + 1))
                wait(R_sb, 2 * NC * g)
                wait(U_sb, 2 * NC * g)
                for n in range(V // 4):
                    if n >= 4:
                        wait(xt_sb, 8 * g + n - 3)
                    for i in range(4):
                        last = nc.tensor.transpose(ring[n % 4][:, 128 * i:128 * i + 128], X[:, 4 * n + i, :], ident[:])
                    last.then_inc(xt_ps, 1)

            def sweep(g):
                wait(xt_sb, 8 * (g + 1))
                wait(lane_sb, 8 * (g + 2 if not isinstance(g, int) else NG))
                x1 = fronts(g + 1) if not isinstance(g, int) else fronts(g)
                wait(act_proj, 3 * x1)
                wait(flog_ready, x1)
                wait(kr_ready, x1)
                wait(x_ready, x1 + 1)
                with pe.Fori(0, NC // 2) as c2:
                    for i in range(2):
                        n = g * NC + c2 * 2 + i
                        st = stage[i]

                        def chain(p, h, at_col, w):
                            return st[32 * h:32 * h + 32, p // 2, at_col + w * (p % 2):at_col + w * (p % 2) + w]

                        wait(staged[i], 32 * (g * (NC // 2) + c2 + 1))
                        for half in range(2):
                            wait(S_sb, 18 * g + 2 * (c2 * 2 + i) + half + 1)
                            for p in range(8 * half, 8 * half + 8):
                                for h in range(4):
                                    r = slice(32 * h, 32 * h + 32)
                                    last = nc.tensor.matmul(bank[half][r, 32 * p:32 * p + 32], chain(p, h, KIN, V), S[i][r, 32 * p:32 * p + 32], start=True, stop=True)
                            last.then_inc(R_ps, 1)
                        for half in range(2):
                            wait(R_sb, 2 * n + half + 1)
                            for p in range(8 * half, 8 * half + 8):
                                for h in range(4):
                                    r = slice(32 * h, 32 * h + 32)
                                    last = nc.tensor.matmul(bank[2 + half][r, 32 * p:32 * p + 32], xst[i][r, 32 * p:32 * p + 32], R[r, 32 * p:32 * p + 32], start=True, stop=True)
                            last.then_inc(U_ps, 1)
                        for half in range(2):
                            wait(U_sb, 2 * n + half + 1)
                            for p in range(8 * half, 8 * half + 8):
                                for h in range(4):
                                    r = slice(32 * h, 32 * h + 32)
                                    last = nc.tensor.matmul(bank[4 + half][r, 32 * p:32 * p + 32], chain(p, h, KOUT, V), U[r, 32 * p:32 * p + 32], start=True, stop=True)
                            last.then_inc(S_ps, 1)
                        for half in range(2):
                            wait(O_sb, 2 * n)
                            for p in range(8 * half, 8 * half + 8):
                                for h in range(4):
                                    r = slice(32 * h, 32 * h + 32)
                                    o = bank[6 + half][32 * h:32 * h + T, 32 * p:32 * p + 32]
                                    nc.tensor.matmul(o, chain(p, h, Q_E, T), S[i][r, 32 * p:32 * p + 32], start=True, stop=False)
                                    last = nc.tensor.matmul(o, chain(p, h, A_T, T), U[r, 32 * p:32 * p + 32], start=False, stop=True)
                            last.then_inc(O_ps, 1)

            groups(first, project, lambda g: None, finish, sweep)

        @block.scalar
        def _(act):
            block_engine[0] = act
            steps = Steps(act, act_steps)
            outs = scratch.o.rearrange("b g (c t) (h w) -> h c t (b g) w", c=NC, h=4)

            def wait(sem, value):
                if not (isinstance(value, int) and value <= 0):
                    act.wait_ge(sem, value)

            def rows_root(y):
                wait(moments, y + 1)
                inverse_root(nc, steps, rstd[0:N], mv[0:N, 1:2], LN_EPS).then_inc(rstds, 1)

            def rows_copy(y):
                wait(pe_x, y + 1)
                wait(pe_proj, 3 * y)
                nc.scalar.activation(xT[:, :, 0:N], b_x[:, 0:256].rearrange("p (t n) -> p t n", t=2)[:, :, 0:N], ACT.Copy).then_inc(x_ready, 1)

            def front(x, y):
                nc.scalar.preload_act_table_set(SILU)
                wait(pe_fg, x + 1)
                wait(pe_proj, 3 * x)
                nc.scalar.activation(fg[:], b_x[0:HD, 256:512].rearrange("p (t n) -> p t n", t=2), ACT.Copy).then_inc(fg_ready, 1)
                wait(pe_proj, 3 * x + 1)
                wait(k_ready, x)
                wait(pe_ss, x)
                wait(kq_ready, 3 * LV * x)
                steps.link(nc.scalar.activation(kraw[:], b_qk[:, D:], ACT.Silu))
                nc.scalar.activation(k2[:], kraw[:], ACT.Square).then_inc(k2_ready, 1)
                wait(pool_done, 5 * x)
                nc.scalar.activation(q[:], b_qk[:, 0:D], ACT.Silu).then_inc(act_proj, 1)
                wait(pe_proj, 3 * x + 2)
                wait(v_out, 16 * x)
                steps.mark(nc.scalar.activation(vt[:], b_vb[:, 0:D], ACT.Silu))
                wait(nb_ready, x)
                nc.scalar.activation(tanh_beta[:], b_vb[:, D:], ACT.Tanh, scale=0.5).then_inc(act_proj, 1)
                wait(pe_proj, 3 * x + 3)
                wait(gate_ready, x)
                steps.mark(nc.scalar.activation(tanh_gate[:], b_fg[:, D:], ACT.Tanh, scale=0.5))
                nc.scalar.preload_act_table_set(LN_EXP)
                wait(flog_ready, x)
                steps.link(nc.scalar.activation(fabs[:], b_fg[:, 0:D], ACT.Abs))
                steps.link(nc.scalar.activation(fabs[:], fabs[:], ACT.Exp, scale=-1.0))
                nc.scalar.activation(flog[:], fabs[:], ACT.Ln, bias=1.0).then_inc(act_proj, 1)
                wait(pe_ss, x + 1)
                steps.link(nc.scalar.activation(kr[:], b_x[:, 0:D], ACT.Ln, bias=QK_EPS))
                nc.scalar.activation(kr[:], kr[:], ACT.Exp, scale=-0.5).then_inc(kr_ready, 1)
                rows_root(y)
                wait(diff_ready, x + 1)
                steps.mark(nc.scalar.activation(facin[:], L[:], ACT.Exp))
                nc.scalar.activation(fac[:], diff[:], ACT.Exp).then_inc(fac_ready, 1)
                rows_copy(y)

            def kout_section(x):
                wait(kout_ready, x + 1)
                wait(kiq_out, 16 * x)
                kt = chunks(koutT[:])
                nc.scalar.activation(kiq[:, :, KOUT:KOUT + 2 * V].rearrange("p c (g w) -> p g c w", g=2), kt, ACT.Copy).then_inc(kout_copied, 1)

            def first():
                nc.scalar.preload_act_table_set(LN_EXP)
                wait(zeroed, 4)
                rows_root(0)
                rows_copy(0)
                front(0, 1)
                kout_section(0)
                steps.restart()

            def project(g):
                with act.Fori(0, GB) as b:
                    it = g * GB + b
                    front(it + 1, it + 2)
                    wait(at_out, 16 * it)
                    wait(pa_ready, 2 * it + 2)
                    nc.scalar.activation(at[:].rearrange("p c (g t) -> p g c t", g=2), PA[:].rearrange("p g c (t k) -> p g c t k", k=3)[:, :, :, :, 2], ACT.Copy).then_inc(at_copied, 1)
                    kout_section(it + 1)
                    steps.restart()
                for n in range(V // 4):
                    act.wait_ge(lane_ps, 8 * g + n + 1)
                    nc.scalar.activation(LP[:, 4 * n:4 * n + 4, :], ring[n % 4][:].rearrange("p (v x) -> p v x", v=4), ACT.Copy).then_inc(lane_sb, 1)

            def finish(g):
                for i in range(2):
                    wait(staged[i], 32 * (NC // 2) * g)
                for n in range(V // 4):
                    act.wait_ge(xt_ps, 8 * g + n + 1)
                    for i in range(4):
                        last = nc.scalar.activation(XT[:, :, 4 * n + i::V], ring[n % 4][:, 128 * i:128 * i + 128].rearrange("p (c x) -> p c x", c=NC), ACT.Copy)
                    last.then_inc(xt_sb, 1)

            def sweep(g):
                act.wait_ge(S_sb, 18 * g + 2)
                with act.Fori(0, NC // 2) as c2:
                    for i in range(2):
                        c = c2 * 2 + i
                        n = g * NC + c
                        parts = (slice(0, 256), slice(256, 512))
                        for half, cols in enumerate(parts):
                            act.wait_ge(R_ps, 2 * n + half + 1)
                            if half == 0:
                                act.wait_ge(U_ps, 2 * n)
                            nc.scalar.activation(R[:, cols], bank[half][:, cols], ACT.Copy).then_inc(R_copied, 1)
                        for half, cols in enumerate(parts):
                            act.wait_ge(U_ps, 2 * n + half + 1)
                            if half == 0:
                                act.wait_ge(O_ps, 2 * n + 2)
                            nc.scalar.activation(U[:, cols], bank[2 + half][:, cols], ACT.Copy).then_inc(U_sb, 1)
                        for half, cols in enumerate(parts):
                            act.wait_ge(S_ps, 2 * n + half + 1)
                            if half == 0:
                                act.wait_ge(tS_ready, n)
                            nc.scalar.activation(S[1 - i][:, cols], bank[4 + half][:, cols], ACT.Copy).then_inc(S_copied, 1)
                        for half, cols in enumerate(parts):
                            act.wait_ge(O_ps, 2 * n + half + 3)
                            if half == 0:
                                act.wait_ge(o_out, 64 * n)
                            nc.scalar.activation(O[:, cols], bank[6 + half][:, cols], ACT.Copy).then_inc(O_sb, 1)
                        act.wait_ge(O_sb, 2 * n + 2)
                        for h in range(4):
                            act.dma_start(outs[h, c, :, bass.ds(g * (2 * GB), 2 * GB), :],
                                          O[32 * h:32 * h + T].rearrange("p (y w) -> p y w", y=2 * GB)).then_inc(o_out, 16)

            groups(first, project, lambda g: None, finish, sweep)
            act.wait_ge(o_out, 64 * NG * NC)

        @block.gpsimd
        def _(pool):
            block_engine[0] = pool

            def wait(sem, value):
                if not (isinstance(value, int) and value <= 0):
                    pool.wait_ge(sem, value)

            def front(x):
                wait(fac_ready, x + 1)
                wait(nb_ready, x + 1)
                wait(kiq_out, 16 * x)
                fin = chunks(facin[:])
                for hg in range(2):
                    kk = nbk[:, 128 * hg:128 * hg + 128].rearrange("p (c t) -> p c t", c=NC).unsqueeze(3).to_broadcast([128, NC, T, 2])
                    pool.tensor_tensor(kiq[:, :, KIN + V * hg:KIN + V * hg + V].rearrange("p c (t a) -> p c t a", a=2),
                                       fin[:, hg].rearrange("p c (t a) -> p c t a", a=2), kk, ALU.mult).then_inc(pool_done, 1)
                    pool.tensor_tensor(kiq[:, :, Q_E + T * hg:Q_E + T * hg + T], fin[:, hg, :, 1:V:2],
                                       q[:, 128 * hg:128 * hg + 128].rearrange("p (c t) -> p c t", c=NC), ALU.mult).then_inc(pool_done, 1)
                pool.tensor_copy(eg[:, :, bass.ds(2 * x, 2)], fin[:, :, :, V - 1].rearrange("p g c -> p c g")).then_inc(pool_done, 1)

            def project(g):
                with pool.Fori(0, GB) as b:
                    front(g * GB + b + 1)

            def sweep(g):
                hold(pool, pool_done, 5 * (fronts(g + 1) if not isinstance(g, int) else fronts(g)), passed)
                hold(pool, S_sb, 18 * g, passed)
                nc.gpsimd.memset(S[0][:, 0:256], 0.0).then_inc(S_sb, 1)
                nc.gpsimd.memset(S[0][:, 256:512], 0.0).then_inc(S_sb, 1)
                with pool.Fori(0, NC // 2) as c2:
                    for i in range(2):
                        c = c2 * 2 + i
                        n = g * NC + c
                        pool.wait_ge(S_sb, 18 * g + 2 * c + 2)
                        pool.tensor_tensor(tS[:].rearrange("p (x w) -> p x w", w=HD), S[i][:].rearrange("p (x w) -> p x w", w=HD),
                                           eg[:, c, bass.ds(g * (2 * GB), 2 * GB)].unsqueeze(2).to_broadcast([128, 2 * GB, HD]), ALU.mult).then_inc(tS_ready, 1)
                        pool.wait_ge(v_staged[i], 64 * (g * (NC // 2) + c2 + 1))
                        for half in range(2):
                            cols = slice(256 * half, 256 * half + 256)
                            pool.wait_ge(R_copied, 2 * n + half + 1)
                            pool.tensor_tensor(R[:, cols], R[:, cols], vst[i][:, cols], ALU.add).then_inc(R_sb, 1)
                        pool.wait_ge(tS_ready, n + 1)
                        for half in range(2):
                            cols = slice(256 * half, 256 * half + 256)
                            pool.wait_ge(S_copied, 2 * n + half + 1)
                            pool.tensor_tensor(S[1 - i][:, cols], S[1 - i][:, cols], tS[:, cols], ALU.add).then_inc(S_sb, 1)

            groups(lambda: front(0), project, lambda g: None, lambda g: None, sweep)

        @block.vector
        def _(dve):
            block_engine[0] = dve
            steps = Steps(dve, dve_steps)

            def wait(sem, value):
                if not (isinstance(value, int) and value <= 0):
                    dve.wait_ge(sem, value)

            dve.wait_ge(consts, 16 * 12)
            nc.vector.tensor_copy(wb[:].rearrange("p t (h w) -> p t h w", h=H), wb8[:].unsqueeze(3).to_broadcast([128, 2, H, HD])).then_inc(wb_ready, 1)
            for x in (xT, vst[0], vst[1], lower):
                nc.vector.memset(x[:], 0.0).then_inc(zeroed, 1)
            steps.mark(nc.vector.memset(decay[:], 0.0))
            steps.mark(nc.vector.memset(PA[:], 0.0))
            steps.link(nc.vector.memset(X[:], 0.0))
            for v in range(V):
                steps.mark(nc.vector.memset(X[:, v, v:128:V], 1.0))
            steps.restart()

            def rows_stats(y):
                wait(rstds, y)
                wait(loaded, 32 * (y + 1))
                steps.link(nc.vector.bn_stats(stats[0:N], hx[0:N]))
                nc.vector.bn_aggr(mv[0:N], stats[0:N]).then_inc(moments, 1)

            def rows_norm(y):
                wait(rstds, y + 1)
                wait(pe_x, y)
                nc.vector.tensor_scalar(xn[0:N], hx[0:N], mv[0:N, 0:1], rstd[0:N], ALU.subtract, ALU.mult).then_inc(normed, 1)

            def decays(x):
                wait(act_proj, 3 * x + 3)
                wait(fac_ready, x)
                nc.vector.scalar_tensor_tensor(out=decay[:, 1::2], in0=b_fg[:, 0:D], scalar=0.0, in1=flog[:], op0=ALU.min, op1=ALU.subtract).then_inc(flog_ready, 1)
                wait(gate_out, 16 * x)
                nc.vector.tensor_scalar(gate[:], tanh_gate[:], 0.5, 0.5, ALU.mult, ALU.add).then_inc(gate_ready, 1)
                wait(flog_ready, x + 1)
                steps.link(nc.vector.tensor_tensor_scan(L[:], in_chunk[:], decay[:], 0.0, ALU.mult, ALU.add))
                for l in range(LV):
                    w = 1 << l
                    s = L[:].rearrange("p (n s w) -> p n s w", s=2, w=w)
                    d = diff[:, l].rearrange("p (n s w) -> p n s w", s=2, w=w)
                    top = s[:, :, 1, 0:1].to_broadcast([128, 2 * NC * V // (2 * w), w])
                    steps.mark(nc.vector.tensor_tensor(d[:, :, 1], s[:, :, 1], top, ALU.subtract))
                    steps.mark(nc.vector.tensor_tensor(d[:, :, 0], top, s[:, :, 0], ALU.subtract))
                s = L[:].rearrange("p (n w) -> p n w", w=V)
                steps.mark(nc.vector.tensor_tensor(diff[:, LV].rearrange("p (n w) -> p n w", w=V), s[:, :, V - 1:V].to_broadcast([128, 2 * NC, V]), s, ALU.subtract))
                steps.wait()
                dve.sem_inc(diff_ready, 1)

            def keys(x):
                wait(kr_ready, x + 1)
                nc.vector.tensor_tensor(k[:], kraw[:], kr[:], ALU.mult).then_inc(k_ready, 1)
                wait(k_ready, x + 1)
                wait(fac_ready, x + 1)

            def pairs_of_keys():
                return tokens(k[:]).unsqueeze(3).to_broadcast([128, 2 * NC, T, 2])

            def factors(x, l):
                wait(scores, 2 * LV * (x - 1) + 2 * l + 2 if not isinstance(x, int) else 0)
                if l == 0:
                    f, up = tokens(fac[:, 0, 1::2]), above[0][:].rearrange("p (n t k) -> p n t k", t=T, k=2)
                    nc.vector.tensor_tensor(lower[:, 0].rearrange("p n (t a) -> p n t a", a=2), fac[:, 0].rearrange("p (n t a) -> p n t a", t=T, a=2),
                                            pairs_of_keys(), ALU.mult).then_inc(kq_ready, 1)
                    nc.vector.tensor_tensor(up[:, :, :, 0], f, tokens(k[:]), ALU.mult).then_inc(kq_ready, 1)
                    nc.vector.tensor_tensor(up[:, :, :, 1], f, tokens(q[:]), ALU.mult).then_inc(kq_ready, 1)
                    return
                w = 1 << (l - 1)
                kb = k[:].rearrange("p (s u w) -> p s u w", u=2, w=w)
                qb = q[:].rearrange("p (s u w) -> p s u w", u=2, w=w)
                f = fac[:, l].rearrange("p (s u w a) -> p s u w a", u=2, w=w, a=2)
                low = lower[:, l].rearrange("p n v -> p (n v)").rearrange("p (s u w a) -> p s u w a", u=2, w=w, a=2)
                up = above[l][:].rearrange("p (s w k) -> p s w k", w=w, k=3)
                both = [128, D // (2 * w), w, 2]
                nc.vector.tensor_tensor(low[:, :, 0], f[:, :, 0], kb[:, :, 0].unsqueeze(3).to_broadcast(both), ALU.mult).then_inc(kq_ready, 1)
                nc.vector.tensor_tensor(up[:, :, :, 0:2], f[:, :, 1], kb[:, :, 1].unsqueeze(3).to_broadcast(both), ALU.mult).then_inc(kq_ready, 1)
                nc.vector.tensor_tensor(up[:, :, :, 2], f[:, :, 1, :, 1], qb[:, :, 1], ALU.mult).then_inc(kq_ready, 1)

            def writes(x):
                steps.link(nc.vector.tensor_tensor(kout[:].rearrange("p (n t a) -> p n t a", t=T, a=2), fac[:, LV].rearrange("p (n t a) -> p n t a", t=T, a=2), pairs_of_keys(), ALU.mult))
                wait(kout_copied, x)
                nc.vector.transpose(koutT[:], kout[:]).then_inc(kout_ready, 1)
                steps.link(nc.vector.tensor_scalar(nbeta[:], tanh_beta[:], -1.0, -1.0, ALU.mult, ALU.add))
                wait(pool_done, 5 * x)
                nc.vector.tensor_tensor(nbk[:], k[:], nbeta[:], ALU.mult).then_inc(nb_ready, 1)

            def take(it, n):
                l, hg = n // 2, n % 2
                hold(dve, scores, 2 * LV * it + n + 1, passed)
                dst = upper(PA[:, hg], l)
                k1, k0 = dst.shape[-2:]
                mask = levels[:, l, 0:UP[l]].rearrange("p (s k) -> p s k", s=k1).unsqueeze(1).to_broadcast([128, NC, k1, k0])
                src = ring[n % 4][:, 0:NC * 32].rearrange("p (c w) -> p c w", w=32)[:, :, 0:UP[l]].rearrange("p c (s k) -> p c s k", s=k1)
                nc.vector.copy_predicated(dst, mask, src).then_inc(taken, 1)
                hold(dve, taken, 2 * LV * it + n + 1, passed)

            def times_beta(b, it):
                pbv = Pb[:].rearrange("p (t a) (c y) -> p c t a y", a=2, c=NC)
                for hg in range(2):
                    nb = nbeta[:, 128 * hg:128 * hg + 128].rearrange("p (c t) -> p c t", c=NC).unsqueeze(3).to_broadcast([128, NC, T, 2])
                    nc.vector.tensor_tensor(pbv[:, :, :, :, 2 * b + hg], PA[:, hg].rearrange("p c (t k) -> p c t k", k=3)[:, :, :, 0:2], nb, ALU.mult).then_inc(pa_ready, 1)

            def first():
                rows_stats(0)
                rows_norm(0)
                rows_stats(1)
                decays(0)
                rows_norm(1)
                keys(0)
                for l in range(LV):
                    factors(0, l)
                writes(0)
                steps.restart()

            def project(g):
                with dve.Fori(0, GB) as b:
                    it = g * GB + b
                    dve.wait_ge(nb_ready, it + 1)
                    dve.wait_ge(at_copied, it)
                    rows_stats(it + 2)
                    for n in range(3):
                        take(it, n)
                    decays(it + 1)
                    for n in range(3, 6):
                        take(it, n)
                    rows_norm(it + 2)
                    keys(it + 1)
                    factors(it + 1, 0)
                    factors(it + 1, 1)
                    take(it, 6)
                    factors(it + 1, 2)
                    take(it, 7)
                    take(it, 8)
                    factors(it + 1, 3)
                    take(it, 9)
                    times_beta(b, it)
                    factors(it + 1, 4)
                    writes(it + 1)
                    steps.restart()

            def invert(g):
                dve.wait_ge(lane_sb, 8 * (g + 1))
                for v in range(1, V):
                    lp = LP[:, v].rearrange("p (h m) -> p h m", h=4)[:, :, 0:v].unsqueeze(2).to_broadcast([128, 4, v, v])
                    x = X[:, 0:v].rearrange("p m (h c) -> p h c m", h=4)[:, :, 0:v, :]
                    steps.link(nc.vector.tensor_tensor(tmp[:, 0:4 * v * v].rearrange("p (h c m) -> p h c m", h=4, c=v), lp, x, ALU.mult))
                    ins = nc.vector.tensor_reduce(X[:, v].rearrange("p (h c) -> p h c", h=4)[:, :, 0:v], tmp[:, 0:4 * v * v].rearrange("p (h c m) -> p h c m", h=4, c=v), axis=AX.X, op=ALU.add)
                    if v < V - 1:
                        steps.link(ins)
                    else:
                        ins.then_inc(inverted, 1)
                steps.restart()

            groups(first, project, invert, lambda g: None, lambda g: None)


def mixture(nc, a, scratch):
    with ExitStack() as ctx:
        m = Memory(nc, ctx)
        acc = m.sb("acc", [128, ST, D])
        ident = m.sb("ident_mix", [128, 128])
        bank = [m.ps(f"mbank{i}") for i in range(4, 8)]
        with ExitStack() as inner:
            dispatch(nc, a, scratch, Memory(nc, inner), acc, ident, bank)
        with ExitStack() as inner:
            answers = m.sb("answers", [128, ST, D])
            experts(nc, a, Memory(nc, inner), acc, answers, ident, bank)
        with ExitStack() as inner:
            combine(nc, a, scratch, Memory(nc, inner), answers, bank)


def dispatch(nc, a, scratch, m, acc, ident, banks):
    by_misc, ring = banks[0], banks[1:4]
    logits = m.ps("logits", [128, NS])
    wo, norm_w = m.sb("wo", [128, 2, D]), m.sb("norm_w", [128, 2])
    phi = m.sb("phi", [128, 2, NS])
    bias = m.sb("bias", [1, NS])
    rest, parts = m.sb("rest", [1, NS]), m.sb("parts", [1, 3, NS], BF16)
    bias3, ones3 = m.sb("bias3", [3, NS], BF16), m.sb("ones3", [3, N], BF16)
    ot = [m.sb(f"ot{i}", [N, D]) for i in range(2)]
    gt = [m.sb(f"gt{i}", [N, D]) for i in range(2)]
    hx = [m.sb(f"mhx{i}", [N, D]) for i in range(2)]
    h2 = [m.sb(f"h2{i}", [N, D]) for i in range(2)]
    fresh = [m.sb(f"fresh{i}", [N, D]) for i in range(2)]
    x = [m.sb(f"mx{i}", [N, D]) for i in range(4)]
    xT = [m.sb(f"mxT{i}", [128, 2, N]) for i in range(2)]
    y, y2, yn, yT = m.sb("y", [N, D]), m.sb("y2", [N, D]), m.sb("yn", [N, D]), m.sb("yT", [128, 2, N])
    ms, rr = m.sb("ms", [N, H]), m.sb("rr", [N, H])
    stats, mv, rstd = m.sb("mstats", [N, 6]), m.sb("mmv", [N, 2]), m.sb("mrstd", [N, 1])
    Dx = [m.sb(f"Dx{i}", [N, NS]) for i in range(4)]
    Cx = [m.sb(f"Cx{i}", [N, NS]) for i in range(4)]
    m1, s1 = m.sb("m1", [N, NEXP]), m.sb("s1", [N, NEXP])
    m2, s2 = m.sb("m2", [N, PS]), m.sb("s2", [N, PS])
    r1, r2 = m.sb("r1", [N, NEXP]), m.sb("r2", [N, PS])
    cT = [m.sb(f"cT{i}", [128, ST, N]) for i in range(2)]
    consts, split, bias_ready, acc_zero = m.sem("mconsts"), m.sem("bias_split"), m.sem("bias_ready"), m.sem("acc_zero")
    loaded = [m.sem("mloaded0"), m.sem("mloaded1")]
    squares, roots, yn_ready, yT_ps, yT_ready, projected = (m.sem(n) for n in ("squares", "roots", "yn_ready", "yT_ps", "yT_ready", "wo_done"))
    h2_ready, moments, rstds, x_ready, x_kept, xT_ps, xT_ready = (
        m.sem(n) for n in ("h2_ready", "mmoments", "mrstds", "mx_ready", "mx_kept", "mxT_ps", "mxT_ready"))
    l_ps, l_copied, e1, max2, e2, exp1, exp2, inv1, inv2, D_ready, C_ready = (
        m.sem(n) for n in ("l_ps", "l_copied", "e1_ready", "max2", "e2_ready", "exp1", "exp2", "inv1", "inv2", "D_ready", "C_ready"))
    cT_ps, cT_sb, acc_ps, acc_added = (m.sem(n) for n in ("cT_ps", "cT_sb", "acc_ps", "acc_added"))
    h_out = [m.sem("h_out0"), m.sem("h_out1")]
    cT_out = [m.sem("cT_out0"), m.sem("cT_out1")]
    dve_steps, act_steps, passed = m.sem("mdve_steps"), m.sem("mact_steps"), m.sem("mpassed")
    PAIRS = B // 2

    def known(h):
        return isinstance(h, int)

    def all_steps(engine, first, step, summing, end):
        first()
        for i in range(2):
            step(0, i, 0)
        end()
        with engine.Fori(0, PAIRS // 2 - 1) as q:
            for p in (1, 0):
                for i in range(2):
                    step(2 * q + 2 - p, i, p)
            end()
        for i in range(2):
            step(PAIRS - 1, i, 1)
        for n in range(8):
            summing(PAIRS - 1, n, 1)
        end()

    def nothing(*_):
        return None

    block = m.ctx.enter_context(nc.Block())

    @block.sync
    def _(sp):
        sp.dma_start(bias[:], a.phi_b.unsqueeze(0)).then_inc(consts, 16)
        sp.dma_start(ident[:], a.ident).then_inc(consts, 16)
        sp.dma_start(wo[:], a.Wo.rearrange("(t p) n -> p t n", p=128)).then_inc(consts, 16)
        sp.dma_start(norm_w[:], a.norm_w).then_inc(consts, 16)
        sp.dma_start(phi[:], a.phi_wT.rearrange("(t p) n -> p t n", p=128)).then_inc(consts, 16)

        def load(f, i):
            sp.dma_start(ot[i][:].rearrange("p (g w) -> p g w", g=2), scratch.o[f, :, 0:N, :].rearrange("g t w -> t g w")).then_inc(loaded[i], 16)
            sp.dma_start(gt[i][:], scratch.gate[f, 0:N, :]).then_inc(loaded[i], 16)
            sp.dma_start(hx[i][0:1 + NPOS], scratch.z[f]).then_inc(loaded[i], 16)
            sp.dma_start(hx[i][1 + NPOS:N], a.txt[f]).then_inc(loaded[i], 16)

        def store_h(f, i):
            hold(sp, h2_ready, f + 1, passed)
            sp.dma_start(scratch.h[f], h2[i][:]).then_inc(h_out[i], 16)

        def first():
            load(0, 0)
            load(1, 1)
            sp.wait_ge(split, 5)
            for r in range(3):
                sp.dma_start(bias3[r:r + 1, :], parts[0:1, r, :]).then_inc(bias_ready, 16)
            store_h(0, 0)

        def store_weights(J, i):
            hold(sp, cT_sb, 8 * J + 4 * i + 4, passed)
            sp.dma_start(scratch.cT[2 * J + i], cT[i][:].rearrange("p s n -> p (s n)")).then_inc(cT_out[i], 16)

        def step(J, i, p):
            h = 2 * J + i
            if not (known(h) and h + 2 >= B):
                load(h + 2, i)
            if not (known(h) and h + 1 >= B):
                store_h(h + 1, 1 - i)
            if not (known(J) and J == 0):
                store_weights(J - 1, i)

        def summing(J, n, p):
            if n % 4 == 3:
                store_weights(J, n // 4)

        all_steps(sp, first, step, summing, nothing)
        for i in range(2):
            sp.wait_ge(h_out[i], 16 * PAIRS)
            sp.wait_ge(cT_out[i], 16 * PAIRS)

    @block.tensor
    def _(pe):
        def wait(sem, value):
            if not (isinstance(value, int) and value <= 0):
                hold(pe, sem, value, passed)

        def gated(f):
            wait(yn_ready, f + 1)
            wait(xT_ready, f)
            wait(h2_ready, f)
            for t in range(2):
                last = nc.tensor.transpose(by_misc[:, 128 * t:128 * t + N], yn[:, 128 * t:128 * t + 128], ident[0:N, 0:N])
            last.then_inc(yT_ps, 1)

        def project(f):
            wait(yT_ready, f + 1)
            for t in range(2):
                last = nc.tensor.matmul(by_misc[0:N, D:], yT[:, t, :], wo[:, t, :], start=t == 0, stop=t == 1)
            last.then_inc(projected, 1)

        def rows(f, i):
            wait(x_ready, f + 1)
            for t in range(2):
                last = nc.tensor.transpose(by_misc[:, 128 * t:128 * t + N], fresh[i][:, 128 * t:128 * t + 128], ident[0:N, 0:N])
            last.then_inc(xT_ps, 1)

        def summing(J, n, p):
            for kind in range(2):
                turn = 2 * n + kind
                if turn < 3:
                    wait(cT_sb, 8 * J)
                    wait(acc_added, 8 * J)
                elif kind == 0:
                    wait(acc_added, 8 * J + (turn - 3) // 2 + 1)
                else:
                    wait(cT_sb, 8 * J + (turn - 3) // 2 + 1)
                out = ring[turn % 3]
                if kind == 0:
                    i, s0 = n // 4, 4 * (n % 4)
                    wait(C_ready, 2 * J + i + 1)
                    for s in range(4):
                        last = nc.tensor.transpose(out[:, 128 * s:128 * s + N], Cx[2 * p + i][:, 128 * (s0 + s):128 * (s0 + s) + 128], ident[0:N, 0:N])
                    last.then_inc(cT_ps, 1)
                else:
                    wait(D_ready, 2 * J + 2)
                    wait(x_kept, 2 * J + 2)
                    for s in range(2):
                        st = 2 * n + s
                        for i in range(2):
                            last = nc.tensor.matmul(out[:, D * s:D * s + D], Dx[2 * p + i][:, 128 * st:128 * st + 128], x[2 * p + i][:], start=i == 0, stop=i == 1)
                    last.then_inc(acc_ps, 1)

        def first():
            gated(0)
            project(0)
            rows(0, 0)

        def step(J, i, p):
            h = 2 * J + i
            wait(xT_ready, h + 1)
            wait(l_copied, h)
            for s in range(4):
                cols = slice(512 * s, 512 * s + 512)
                for t in range(2):
                    nc.tensor.matmul(logits[0:N, cols], xT[i][:, t, :], phi[:, t, cols], start=t == 0, stop=False)
                last = nc.tensor.matmul(logits[0:N, cols], ones3[:], bias3[:, cols], start=False, stop=True)
            last.then_inc(l_ps, 1)
            sums = summing if not (known(J) and J == 0) else nothing
            front = not (known(h) and h + 1 >= B)
            if front:
                gated(h + 1)
            sums(J - 1, 4 * i, 1 - p)
            if front:
                project(h + 1)
            sums(J - 1, 4 * i + 1, 1 - p)
            sums(J - 1, 4 * i + 2, 1 - p)
            if front:
                rows(h + 1, 1 - i)
            sums(J - 1, 4 * i + 3, 1 - p)

        pe.wait_ge(consts, 16 * 5)
        pe.wait_ge(bias_ready, 48)
        all_steps(pe, first, step, summing, nothing)

    @block.scalar
    def _(act):
        steps = Steps(act, act_steps)

        def wait(sem, value):
            if not (isinstance(value, int) and value <= 0):
                act.wait_ge(sem, value)

        def gate_roots(f):
            wait(squares, f + 1)
            wait(yn_ready, f)
            steps.link(nc.scalar.activation(rr[:], ms[:], ACT.Ln, bias=QK_EPS, scale=1.0 / HD))
            nc.scalar.activation(rr[:], rr[:], ACT.Exp, scale=-0.5).then_inc(roots, 1)

        def gated(f):
            wait(yT_ps, f + 1)
            wait(projected, f)
            for t in range(2):
                last = nc.scalar.activation(yT[:, t, :], by_misc[:, 128 * t:128 * t + N], ACT.Copy, scale=norm_w[:, t:t + 1])
            last.then_inc(yT_ready, 1)

        def row_roots(f):
            wait(moments, f + 1)
            wait(x_kept, f)
            inverse_root(nc, steps, rstd[:], mv[:, 1:2], LN_EPS).then_inc(rstds, 1)

        def rows(f, i):
            wait(xT_ps, f + 1)
            wait(l_ps, f - 1)
            nc.scalar.activation(xT[i][:], by_misc[:, 0:256].rearrange("p (t n) -> p t n", t=2)[:, :, 0:N], ACT.Copy).then_inc(xT_ready, 1)

        def summing(J, n, p):
            i, s0 = n // 4, 4 * (n % 4)
            if n % 4 == 0:
                wait(cT_out[i], 16 * J)
            wait(cT_ps, 8 * J + n + 1)
            nc.scalar.activation(cT[i][:, s0:s0 + 4, :], ring[(2 * n) % 3][:].rearrange("p (s n) -> p s n", s=4)[:, :, 0:N], ACT.Copy).then_inc(cT_sb, 1)

        def first():
            gate_roots(0)
            gated(0)
            row_roots(0)
            rows(0, 0)
            gate_roots(1)

        def step(J, i, p):
            h = 2 * J + i
            slot = 2 * p + i
            wait(l_ps, h + 1)
            wait(cT_ps, 8 * (J - 1) if not (known(J) and J == 0) else 0)
            nc.scalar.activation(Cx[slot][:], logits[0:N, :], ACT.Copy).then_inc(l_copied, 1)
            sums = summing if not (known(J) and J == 0) else nothing
            front = not (known(h) and h + 1 >= B)
            if front:
                gated(h + 1)
            sums(J - 1, 4 * i, 1 - p)
            sums(J - 1, 4 * i + 1, 1 - p)
            if front:
                row_roots(h + 1)
            sums(J - 1, 4 * i + 2, 1 - p)
            wait(e1, h + 1)
            nc.scalar.activation(Dx[slot][:], Dx[slot][:], ACT.Exp).then_inc(exp1, 1)
            if front:
                rows(h + 1, 1 - i)
            sums(J - 1, 4 * i + 3, 1 - p)
            if not (known(h) and h + 2 >= B):
                gate_roots(h + 2)
            wait(e2, h + 1)
            nc.scalar.activation(Cx[slot][:], Cx[slot][:], ACT.Exp).then_inc(exp2, 1)

        act.wait_ge(consts, 16 * 5)
        nc.scalar.preload_act_table_set(LN_EXP)
        all_steps(act, first, step, summing, steps.restart)

    @block.gpsimd
    def _(pool):
        def by_expert(t, r):
            return t[:].rearrange("p (n s) -> p n s", n=NEXP), r[:].unsqueeze(2).to_broadcast([N, NEXP, PS])

        def by_slot(t, r):
            return t[:].rearrange("p (n s) -> p n s", n=NEXP), r[:].unsqueeze(1).to_broadcast([N, NEXP, PS])

        def step(J, i, p):
            h = 2 * J + i
            pool.wait_ge(e1, h + 1)
            pool.wait_ge(max2, h + 1)
            c, r = by_slot(Cx[2 * p + i], m2)
            pool.tensor_tensor(c, c, r, ALU.subtract).then_inc(e2, 1)
            pool.wait_ge(inv1, h + 1)
            d, r = by_expert(Dx[2 * p + i], r1)
            pool.tensor_tensor(d, d, r, ALU.mult).then_inc(D_ready, 1)
            pool.wait_ge(inv2, h + 1)
            c, r = by_slot(Cx[2 * p + i], r2)
            pool.tensor_tensor(c, c, r, ALU.mult).then_inc(C_ready, 1)

        all_steps(pool, nothing, step, nothing, nothing)

    @block.vector
    def _(dve):
        steps = Steps(dve, dve_steps)
        nc.vector.memset(acc[:], 0.0).then_inc(acc_zero, 1)
        dve.wait_ge(consts, 16 * 5)
        nc.vector.memset(ones3[:], 1.0).then_inc(split, 1)
        steps.link(nc.vector.tensor_copy(parts[0:1, 0, :], bias[:]))
        steps.link(nc.vector.tensor_tensor(rest[:], bias[:], parts[0:1, 0, :], ALU.subtract))
        steps.link(nc.vector.tensor_copy(parts[0:1, 1, :], rest[:]))
        steps.link(nc.vector.tensor_tensor(rest[:], rest[:], parts[0:1, 1, :], ALU.subtract))
        nc.vector.tensor_copy(parts[0:1, 2, :], rest[:]).then_inc(split, 4)
        steps.restart()
        dve.wait_ge(acc_zero, 1)

        def wait(sem, value):
            if not (isinstance(value, int) and value <= 0):
                dve.wait_ge(sem, value)

        def gate_squares(f, i):
            wait(loaded[i], 64 * (f // 2 + 1) if known(f) else 64 * f[1])
            f = f if known(f) else f[0]
            steps.link(nc.vector.tensor_tensor(y[:], ot[i][:], gt[i][:], ALU.mult))
            steps.link(nc.vector.tensor_tensor(y2[:], y[:], y[:], ALU.mult))
            wait(roots, f)
            nc.vector.tensor_reduce(ms[:], y2[:].rearrange("p (h w) -> p h w", h=H), axis=AX.X, op=ALU.add).then_inc(squares, 1)

        def gate_norm(f):
            wait(roots, f + 1)
            wait(yT_ps, f)
            nc.vector.tensor_tensor(yn[:].rearrange("p (h w) -> p h w", h=H), y[:].rearrange("p (h w) -> p h w", h=H),
                                    rr[:].unsqueeze(2).to_broadcast([N, H, HD]), ALU.mult).then_inc(yn_ready, 1)

        def add_rows(f, i, before):
            wait(projected, f + 1)
            wait(h_out[i], 16 * before)
            nc.vector.tensor_tensor(h2[i][:], by_misc[0:N, D:], hx[i][:], ALU.add).then_inc(h2_ready, 1)
            wait(h2_ready, f + 1)
            steps.link(nc.vector.bn_stats(stats[:], h2[i][:]))
            nc.vector.bn_aggr(mv[:], stats[:]).then_inc(moments, 1)

        def norm_rows(f, i):
            wait(rstds, f + 1)
            wait(xT_ps, f - 1)
            nc.vector.tensor_scalar(fresh[i][:], h2[i][:], mv[:, 0:1], rstd[:], ALU.subtract, ALU.mult).then_inc(x_ready, 1)

        def summing(J, n, p):
            wait(acc_ps, 8 * J + n + 1)
            part = acc[:, 2 * n:2 * n + 2, :].rearrange("p s d -> p (s d)")
            wait(acc_added, 8 * J)
            nc.vector.tensor_tensor(part, ring[(2 * n + 1) % 3][:], part, ALU.add).then_inc(acc_added, 1)

        def first():
            gate_squares(0, 0)
            gate_norm(0)
            add_rows(0, 0, 0)
            norm_rows(0, 0)
            gate_squares(1, 1)
            gate_norm(1)

        def step(J, i, p):
            h = 2 * J + i
            slot = 2 * p + i
            d, c = (t[slot][:].rearrange("p (n s) -> p n s", n=NEXP) for t in (Dx, Cx))
            sums = summing if not (known(J) and J == 0) else nothing
            front = not (known(h) and h + 1 >= B)
            done = 8 * (J - 1) if not (known(J) and J == 0) else 0
            wait(acc_ps, done)
            nc.vector.tensor_scalar(x[slot][:], h2[i][:], mv[:, 0:1], rstd[:], ALU.subtract, ALU.mult).then_inc(x_kept, 1)
            wait(l_copied, h + 1)
            steps.link(nc.vector.tensor_reduce(m1[:], c, axis=AX.X, op=ALU.max))
            sums(J - 1, 4 * i, 1 - p)
            if front:
                add_rows(h + 1, 1 - i, J + i)
            nc.vector.tensor_tensor(d, c, m1[:].unsqueeze(2).to_broadcast([N, NEXP, PS]), ALU.subtract).then_inc(e1, 1)
            sums(J - 1, 4 * i + 1, 1 - p)
            if front:
                norm_rows(h + 1, 1 - i)
            wait(e2, h)
            nc.vector.tensor_reduce(m2[:], c.rearrange("p n s -> p s n"), axis=AX.X, op=ALU.max).then_inc(max2, 1)
            sums(J - 1, 4 * i + 2, 1 - p)
            wait(exp1, h + 1)
            steps.link(nc.vector.tensor_reduce(s1[:], d, axis=AX.X, op=ALU.add))
            wait(D_ready, h)
            nc.vector.reciprocal(r1[:], s1[:]).then_inc(inv1, 1)
            sums(J - 1, 4 * i + 3, 1 - p)
            more = not (known(h) and h + 2 >= B)
            if more:
                gate_squares(h + 2 if known(h) else (h + 2, J + 2), i)
            wait(exp2, h + 1)
            steps.link(nc.vector.tensor_reduce(s2[:], c.rearrange("p n s -> p s n"), axis=AX.X, op=ALU.add))
            wait(C_ready, h)
            nc.vector.reciprocal(r2[:], s2[:]).then_inc(inv2, 1)
            if more:
                gate_norm(h + 2)

        all_steps(dve, first, step, summing, steps.restart)


def experts(nc, a, m, acc, answers, ident, banks):
    eb = m.sb("eb", [128, ST, D])
    stats, mv, rstd = m.sb("estats", [128, ST, 6]), m.sb("emv", [128, ST, 2]), m.sb("erstd", [128, ST])
    th = [m.sb(f"th{i}", [128, D]) for i in range(2)]
    thT = [m.sb(f"thT{i}", [128, 2, 128]) for i in range(2)]
    we = [m.sb(f"we{i}", [128, 4, 2, D]) for i in range(2)]
    b_loaded, w_loaded = m.sem("eb_loaded"), [m.sem("we_loaded0"), m.sem("we_loaded1")]
    moments, rstds, normed, th_ready, thT_ps, thT_ready, y_ps, y_sb = (
        m.sem(n) for n in ("e_moments", "e_rstds", "e_normed", "th_ready", "thT_ps", "thT_ready", "ans_ps", "ans_sb"))
    act_steps, dve_steps, passed = m.sem("e_act_steps"), m.sem("e_dve_steps"), m.sem("e_passed")
    block = m.ctx.enter_context(nc.Block())

    @block.sync
    def _(sp):
        for e in range(4):
            sp.dma_start(eb[32 * e:32 * e + 32], a.expert_b.rearrange("(s e) h -> e s h", e=4)[e].partition_broadcast(32)).then_inc(b_loaded, 16)
        w = a.expert_w.rearrange("(s e) (t p) h -> s p e t h", e=4, p=128)
        with sp.Fori(0, ST // 2) as j:
            for i in range(2):
                hold(sp, y_ps, 2 * j, passed)
                for e in range(4):
                    sp.dma_start(we[i][:, e], w[2 * j + i, :, e]).then_inc(w_loaded[i], 16)

    @block.vector
    def _(dve):
        steps = Steps(dve, dve_steps)
        steps.link(nc.vector.tensor_scalar(acc[:], acc[:], -33000.0, 65000.0, ALU.max, ALU.min))
        for s in range(ST):
            steps.mark(nc.vector.bn_stats(stats[:, s], acc[:, s]))
        steps.wait()
        for s in range(ST):
            nc.vector.bn_aggr(mv[:, s], stats[:, s]).then_inc(moments, 1)
        dve.wait_ge(rstds, 1)
        for s in range(ST):
            nc.vector.tensor_scalar(acc[:, s], acc[:, s], mv[:, s, 0:1], rstd[:, s:s + 1], ALU.subtract, ALU.mult).then_inc(normed, 1)
        dve.wait_ge(b_loaded, 64)
        with dve.Fori(0, ST // 2) as j:
            for i in range(2):
                dve.wait_ge(y_ps, 2 * j + i + 1)
                nc.vector.tensor_tensor(answers[:, 2 * j + i, :], banks[2 + i][:, 0:D], eb[:, 2 * j + i, :], ALU.add).then_inc(y_sb, 1)

    @block.scalar
    def _(act):
        steps = Steps(act, act_steps)
        nc.scalar.preload_act_table_set(LN_EXP)
        act.wait_ge(moments, ST)
        inverse_root(nc, steps, rstd[:], mv[:, :, 1], LN_EPS).then_inc(rstds, 1)
        nc.scalar.preload_act_table_set(SILU)
        act.wait_ge(normed, ST)
        with act.Fori(0, ST // 2) as j:
            for i in range(2):
                n = 2 * j + i
                act.wait_ge(thT_ps, n)
                nc.scalar.activation(th[i][:], acc[:, n, :], ACT.Tanh).then_inc(th_ready, 1)
                act.wait_ge(thT_ps, n + 1)
                act.wait_ge(y_ps, n)
                nc.scalar.activation(thT[i][:], banks[i][:, 0:D].rearrange("p (t n) -> p t n", t=2), ACT.Copy).then_inc(thT_ready, 1)

    @block.tensor
    def _(pe):
        with pe.Fori(0, ST // 2) as j:
            for i in range(2):
                n = 2 * j + i
                hold(pe, th_ready, n + 1, passed)
                hold(pe, thT_ready, n, passed)
                for t in range(2):
                    last = nc.tensor.transpose(banks[i][:, 128 * t:128 * t + 128], th[i][:, 128 * t:128 * t + 128], ident[:])
                last.then_inc(thT_ps, 1)
                hold(pe, thT_ready, n + 1, passed)
                hold(pe, w_loaded[i], 64 * (j + 1), passed)
                hold(pe, y_sb, 2 * j, passed)
                for e in range(4):
                    for t in range(2):
                        last = nc.tensor.matmul(banks[2 + i][32 * e:32 * e + 32, 0:D], thT[i][:, t, 32 * e:32 * e + 32], we[i][:, e, t, :], start=t == 0, stop=t == 1)
                last.then_inc(y_ps, 1)


def combine(nc, a, scratch, m, answers, banks):
    cT = [m.sb(f"ccT{i}", [128, ST, N]) for i in range(2)]
    h = [m.sb(f"ch{i}", [N, D]) for i in range(2)]
    o = [m.sb(f"co{i}", [N, D]) for i in range(2)]
    loaded, stored = [m.sem("c_loaded0"), m.sem("c_loaded1")], [m.sem("c_stored0"), m.sem("c_stored1")]
    summed, added, passed = [m.sem("c_summed0"), m.sem("c_summed1")], [m.sem("c_added0"), m.sem("c_added1")], m.sem("c_passed")
    block = m.ctx.enter_context(nc.Block())

    @block.sync
    def _(sp):
        with sp.Fori(0, B // 2) as j:
            for i in range(2):
                b = 2 * j + i
                hold(sp, summed[i], j, passed)
                sp.dma_start(cT[i][:].rearrange("p s n -> p (s n)"), scratch.cT[b]).then_inc(loaded[i], 16)
                hold(sp, added[i], j, passed)
                sp.dma_start(h[i][:], scratch.h[b]).then_inc(loaded[i], 16)

    @block.tensor
    def _(pe):
        with pe.Fori(0, B // 2) as j:
            for i in range(2):
                hold(pe, loaded[i], 32 * (j + 1), passed)
                hold(pe, added[i], j, passed)
                for s in range(ST):
                    last = nc.tensor.matmul(banks[i][0:N, 0:D], cT[i][:, s, :], answers[:, s, :], start=s == 0, stop=s == ST - 1)
                last.then_inc(summed[i], 1)

    @block.vector
    def _(dve):
        with dve.Fori(0, B // 2) as j:
            for i in range(2):
                dve.wait_ge(summed[i], j + 1)
                dve.wait_ge(loaded[i], 32 * (j + 1))
                dve.wait_ge(stored[i], 16 * j)
                nc.vector.tensor_tensor(o[i][:], banks[i][0:N, 0:D], h[i][:], ALU.add).then_inc(added[i], 1)

    @block.scalar
    def _(act):
        with act.Fori(0, B // 2) as j:
            for i in range(2):
                hold(act, added[i], j + 1, passed)
                act.dma_start(a.out[2 * j + i], o[i][:]).then_inc(stored[i], 16)
        for i in range(2):
            act.wait_ge(stored[i], 16 * (B // 2))


class _Arrays:
    pass


def build(nc, arrays):
    scratch = _Arrays()
    scratch.z = nc.dram_tensor("scratch_z", (B, 1 + NPOS, D), F32, kind="Internal").ap()
    scratch.v = nc.dram_tensor("scratch_v", (B + 1, 2, NT, D // 2), F32, kind="Internal").ap()
    scratch.gate = nc.dram_tensor("scratch_gate", (B + 1, NT, D), F32, kind="Internal").ap()
    scratch.slab = nc.dram_tensor("scratch_slab", (NC, 128, B + 1, SLAB), F32, kind="Internal").ap()
    scratch.o = nc.dram_tensor("scratch_o", (B, 2, NT, D // 2), F32, kind="Internal").ap()
    scratch.h = nc.dram_tensor("scratch_h", (B, N, D), F32, kind="Internal").ap()
    scratch.cT = nc.dram_tensor("scratch_cT", (B, 128, ST * N), F32, kind="Internal").ap()
    for part in (tokenizer, attention, mixture):
        part(nc, arrays, scratch)


def lay_out(inputs):
    import numpy as np
    x = {n: np.ascontiguousarray(v) for n, v in inputs.items()}
    p = x["x"].reshape(B, 3, GRID, 16, GRID, 16).transpose(2, 4, 0, 3, 5, 1).reshape(B * NPOS // 128, 128, PD)
    level = np.zeros((LV, V, 2 * T), np.int32)
    for l in range(LV):
        up = [(t, kind) for t in range(T) for kind in range(3)
              if ((kind > 0) if l == 0 else (2 * t) >> l & 1)]
        for at, (t, kind) in enumerate(up):
            q = 2 * t + min(kind, 1)
            for key in range(V):
                level[l, key, at] = key < q and key >> l != q >> l and key >> (l + 1) == q >> (l + 1)
                if kind == 2 and l == 0 and key == q:
                    level[l, key, at] = 1
    return {
        "patches": p,
        "txt": x["txt"],
        "ln1_g": x["L0_tok_ln1_g"].reshape(6, 128).T, "ln1_b": x["L0_tok_ln1_b"].reshape(6, 128).T,
        "W_proj": x["L0_tok_W_proj"], "b_proj": x["L0_tok_b_proj"],
        "ln2_g": x["L0_tok_ln2_g"], "ln2_b": x["L0_tok_ln2_b"],
        "cls_token": x["L0_tok_cls_token"].reshape(D), "pos_emb": x["L0_tok_pos_emb"][0],
        "Wq": x["L0_attn_Wq"], "Wk": x["L0_attn_Wk"], "Wv": x["L0_attn_Wv"],
        "Wf1": x["L0_attn_Wf1"], "Wf2": x["L0_attn_Wf2"], "Wbeta": x["L0_attn_Wbeta"],
        "Wog1": x["L0_attn_Wog1"], "Wog2": x["L0_attn_Wog2"],
        "norm_w": x["L0_attn_norm_w"].reshape(2, 128).T, "Wo": x["L0_attn_Wo"],
        "phi_wT": x["L0_ffn_phi_w"].T, "phi_b": x["L0_ffn_phi_b"],
        "expert_w": x["L0_ffn_expert_w"], "expert_b": x["L0_ffn_expert_b"],
        "ident": np.eye(128, dtype=np.float32),
        "head_ones": np.kron(np.eye(4, dtype=np.float32), np.ones((HD, HD), np.float32)),
        "levels": np.tile(level.transpose(1, 0, 2), (4, 1, 1)).reshape(128, LV * 2 * T),
        "in_chunk": np.tile((np.arange(NC * 2 * V) % V > 0).astype(np.float32), (128, 1)),
    }


def kernel(**inputs):
    import numpy as np
    import concourse.bacc as bacc
    from concourse.bass_utils import run_bass_kernel_spmd

    nc = bacc.Bacc("TRN2", target_bir_lowering=False, num_devices=1)
    data = {name: np.ascontiguousarray(v) for name, v in lay_out(inputs).items()}
    arrays = _Arrays()
    for name, v in data.items():
        arrays.__dict__[name] = nc.dram_tensor(f"in_{name}", v.shape, mybir.dt.from_np(v.dtype), kind="ExternalInput").ap()
    arrays.out = nc.dram_tensor("out", (B, N, D), F32, kind="ExternalOutput").ap()
    build(nc, arrays)
    result = run_bass_kernel_spmd(nc, [{f"in_{name}": v for name, v in data.items()}], core_ids=[0])
    return result.results[0]["out"]
```

```python
import concourse.bass as bass
from concourse import mybir
from contextlib import ExitStack

F32 = mybir.dt.float32
BF16 = mybir.dt.bfloat16
I32 = mybir.dt.int32
ALU = mybir.AluOpType
ACT = mybir.ActivationFunctionType
AX = mybir.AxisListType

B, NTXT, D = 32, 77, 256
GRID, NPOS = 6, 36
PD = 768
N = 1 + NPOS + NTXT
H, HD = 8, 32
T = 16
NC = 8
NT = NC * T
V = 2 * T
GB = 8
NG = B // GB
LV = 5
W = V + T
NEXP, PS = 64, 32
NS = NEXP * PS
ST = NS // 128
WS = 4
LN_EPS, QK_EPS = 1e-5, 1e-6
UP = [2 * T] + [W // 2] * (LV - 1)
KIN, KOUT, Q_E, A_T = 0, 2 * V, 4 * V, 4 * V + 2 * T
SLAB = 4 * V + 4 * T
LN_EXP, SILU, SIGMOID = "natural_log_exp_and_others", "silu_and_others", "sigmoid_and_others"


class Steps:

    def __init__(self, engine, sem):
        self.engine, self.sem, self.n = engine, sem, 0

    def mark(self, ins):
        self.n += 1
        ins.then_inc(self.sem, 1)
        return self.n

    def wait(self, n=None):
        self.engine.wait_ge(self.sem, self.n if n is None else n)

    def link(self, ins):
        self.mark(ins)
        self.wait()

    def restart(self):
        self.wait()
        self.engine.sem_clear(self.sem)
        self.n = 0


class Memory:
    def __init__(self, nc, ctx):
        self.nc, self.ctx = nc, ctx

    def sb(self, name, shape, dt=F32):
        return self.ctx.enter_context(self.nc.sbuf_tensor(name, shape, dt))

    def ps(self, name, shape=(128, 512), dt=F32):
        return self.ctx.enter_context(self.nc.psum_tensor(name, list(shape), dt))

    def sem(self, name):
        return self.ctx.enter_context(self.nc.semaphore(name))


def hold(engine, sem, value, passed):
    engine.wait_ge(sem, value)
    engine.sem_inc(passed, 1)


def inverse_root(nc, steps, out, x, eps):
    steps.link(nc.scalar.activation(out, x, ACT.Ln, bias=eps))
    return nc.scalar.activation(out, out, ACT.Exp, scale=-0.5)


def tokenizer(nc, a, scratch):
    TILES = B * NPOS // 128
    KT = PD // 128
    with ExitStack() as ctx:
        m = Memory(nc, ctx)

        def two(kind, name, *shape):
            return [kind(f"{name}{p}", *shape) for p in range(2)]

        wp = m.sb("wp", [128, KT, D])
        g1, b1 = m.sb("g1", [128, KT]), m.sb("b1", [128, KT])
        bproj, g2, b2 = m.sb("bproj", [128, D]), m.sb("g2", [128, D]), m.sb("b2", [128, D])
        pos = m.sb("pos", [128, TILES, D])
        cls, pos0 = m.sb("cls", [32, D]), m.sb("pos0", [32, D])
        ident = m.sb("ident_tok", [128, 128])
        patch, xn, xnT = two(m.sb, "patch", [128, PD]), two(m.sb, "tok_xn", [128, PD]), two(m.sb, "tok_xnT", [128, KT, 128])
        stats, mv, rstd = two(m.sb, "tok_stats", [128, 12]), two(m.sb, "tok_mv", [128, 2]), two(m.sb, "tok_rstd", [128, 1])
        stats2, mv2, rstd2 = m.sb("tok_stats2", [128, 6]), m.sb("tok_mv2", [128, 2]), m.sb("tok_rstd2", [128, 1])
        z, zo = two(m.sb, "tok_z", [128, D]), two(m.sb, "tok_zo", [128, D])
        pT = [two(m.ps, f"pT{p}") for p in range(2)]
        pZ = two(m.ps, "pZ")
        weights, offsets, dve_steps, act_steps, passed = (m.sem(n) for n in ("tok_weights", "tok_offsets", "tok_dve_steps", "tok_act_steps", "tok_passed"))
        loaded, moments, rstds, normed, transposed, evacuated, projected, z_ready, stored = (
            two(m.sem, n) for n in ("tok_loaded", "tok_moments", "tok_rstds", "tok_normed", "tok_transposed", "tok_evacuated", "tok_projected", "z_ready", "tok_stored"))
        moments2, rstds2, cls_ready, cls_stored = (m.sem(n) for n in ("tok_moments2", "tok_rstds2", "cls_ready", "cls_stored"))
        block = ctx.enter_context(nc.Block())

        def tiles(engine, step):
            with engine.Fori(0, (TILES - 3) // 2) as q:
                for p in range(2):
                    step(2 * q + p, p, q, 3)
            for j in range(TILES - 3, TILES):
                step(j, j % 2, j // 2, TILES - 1 - j)

        @block.sync
        def _(sp):
            def load(j, p, k):
                hold(sp, normed[p], k, passed)
                sp.dma_start(patch[p][:], a.patches[j]).then_inc(loaded[p], 16)

            load(0, 0, 0)
            sp.dma_start(ident[:], a.ident).then_inc(weights, 16)
            sp.dma_start(g1[:], a.ln1_g).then_inc(weights, 16)
            sp.dma_start(b1[:], a.ln1_b).then_inc(weights, 16)
            sp.dma_start(wp[:], a.W_proj.rearrange("(k p) e -> p k e", p=128)).then_inc(weights, 16)
            load(1, 1, 0)
            sp.dma_start(bproj[:], a.b_proj.partition_broadcast(128)).then_inc(offsets, 16)
            sp.dma_start(g2[:], a.ln2_g.partition_broadcast(128)).then_inc(offsets, 16)
            sp.dma_start(b2[:], a.ln2_b.partition_broadcast(128)).then_inc(offsets, 16)
            by_tile = a.pos_emb[1:1 + NPOS].rearrange("(j q) e -> q j e", q=4)
            for q in range(4):
                sp.dma_start(pos[32 * q:32 * q + 32], by_tile[q].partition_broadcast(32)).then_inc(offsets, 16)
            load(2, 0, 1)
            sp.dma_start(cls[:], a.cls_token.partition_broadcast(32)).then_inc(offsets, 16)
            sp.dma_start(pos0[:], a.pos_emb[0].partition_broadcast(32)).then_inc(offsets, 16)

            def step(j, p, k, more):
                if more > 2:
                    load(j + 3, 1 - p, k + p + 1)
                hold(sp, z_ready[p], k + 1, passed)
                for q in range(4):
                    sp.dma_start(scratch.z[:, 1 + 4 * j + q, :], zo[p][32 * q:32 * q + 32]).then_inc(stored[p], 16)

            tiles(sp, step)
            sp.wait_ge(cls_ready, 1)
            sp.dma_start(scratch.z[:, 0, :], cls[:]).then_inc(cls_stored, 16)
            sp.wait_ge(cls_stored, 16)
            for p in range(2):
                sp.wait_ge(stored[p], 64 * ((TILES + 1 - p) // 2))

        @block.vector
        def _(dve):
            steps = Steps(dve, dve_steps)

            def patches(p, k):
                dve.wait_ge(loaded[p], 16 * (k + 1))
                for i in range(2):
                    steps.mark(nc.vector.bn_stats(stats[p][:, 6 * i:6 * i + 6], patch[p][:, 384 * i:384 * i + 384]))
                steps.wait()
                nc.vector.bn_aggr(mv[p][:], stats[p][:]).then_inc(moments[p], 1)
                dve.wait_ge(rstds[p], k + 1)
                dve.wait_ge(transposed[p], k)
                nc.vector.tensor_scalar(xn[p][:], patch[p][:], mv[p][:, 0:1], rstd[p][:], ALU.subtract, ALU.mult).then_inc(normed[p], 1)

            patches(0, 0)
            patches(1, 0)
            dve.wait_ge(offsets, 16 * 9)
            nc.vector.tensor_tensor(cls[:], cls[:], pos0[:], ALU.add).then_inc(cls_ready, 1)
            steps.link(nc.vector.tensor_tensor(pos[:], pos[:], b2[:].unsqueeze(1).to_broadcast([128, TILES, D]), ALU.add))

            steps.restart()

            def step(j, p, k, more):
                if more > 1:
                    patches(p, k + 1)
                dve.wait_ge(projected[p], k + 1)
                steps.link(nc.vector.tensor_tensor(z[p][:], pZ[p][:, 0:D], bproj[:], ALU.add))
                steps.link(nc.vector.bn_stats(stats2[:], z[p][:]))
                nc.vector.bn_aggr(mv2[:], stats2[:]).then_inc(moments2, 1)
                dve.wait_ge(rstds2, j + 1)
                steps.link(nc.vector.tensor_scalar(z[p][:], z[p][:], mv2[:, 0:1], rstd2[:], ALU.subtract, ALU.mult))
                steps.link(nc.vector.tensor_tensor(z[p][:], z[p][:], g2[:], ALU.mult))
                dve.wait_ge(stored[p], 64 * k)
                nc.vector.tensor_tensor(zo[p][:], z[p][:], pos[:, j, :], ALU.add).then_inc(z_ready[p], 1)
                steps.restart()

            tiles(dve, step)

        @block.tensor
        def _(pe):
            def transposes(p, k):
                hold(pe, normed[p], k + 1, passed)
                hold(pe, evacuated[p], k, passed)
                for t in range(KT):
                    last = nc.tensor.transpose(pT[p][t // 4][:, 128 * (t % 4):128 * (t % 4) + 128], xn[p][:, 128 * t:128 * t + 128], ident[:])
                last.then_inc(transposed[p], 1)

            def step(j, p, k, more):
                if more:
                    transposes(1 - p, k + p)
                hold(pe, evacuated[p], k + 1, passed)
                hold(pe, z_ready[p], k, passed)
                for t in range(KT):
                    last = nc.tensor.matmul(pZ[p][:, 0:D], xnT[p][:, t, :], wp[:, t, :], start=t == 0, stop=t == KT - 1)
                last.then_inc(projected[p], 1)

            pe.wait_ge(weights, 16 * 4)
            transposes(0, 0)
            tiles(pe, step)

        @block.scalar
        def _(act):
            steps = Steps(act, act_steps)

            def root(p, k):
                act.wait_ge(moments[p], k + 1)
                inverse_root(nc, steps, rstd[p][:], mv[p][:, 1:2], LN_EPS).then_inc(rstds[p], 1)

            def step(j, p, k, more):
                act.wait_ge(transposed[p], k + 1)
                act.wait_ge(projected[p], k)
                for t in range(KT):
                    last = nc.scalar.activation(xnT[p][:, t, :], pT[p][t // 4][:, 128 * (t % 4):128 * (t % 4) + 128],
                                                ACT.Identity, bias=b1[:, t:t + 1], scale=g1[:, t:t + 1])
                last.then_inc(evacuated[p], 1)
                if more > 1:
                    root(p, k + 1)
                act.wait_ge(moments2, j + 1)
                inverse_root(nc, steps, rstd2[:], mv2[:, 1:2], LN_EPS).then_inc(rstds2, 1)
                steps.restart()

            nc.scalar.preload_act_table_set(LN_EXP)
            root(0, 0)
            root(1, 0)
            steps.restart()
            act.wait_ge(weights, 16 * 4)
            tiles(act, step)


def attention(nc, a, scratch):
    with ExitStack() as ctx:
        m = Memory(nc, ctx)
        wq, wk, wv = m.sb("wq", [128, 2, D]), m.sb("wk", [128, 2, D]), m.sb("wv", [128, 2, D])
        wfg = m.sb("wfg", [128, 2, 2 * HD])
        wf2, wog2 = m.sb("wf2", [HD, D]), m.sb("wog2", [HD, D])
        wb8, wb = m.sb("wb8", [128, 2, H]), m.sb("wb", [128, 2, D])
        ident, head_ones = m.sb("ident_att", [128, 128]), m.sb("head_ones", [128, 128])
        levels = m.sb("levels", [128, LV, 2 * T], I32)
        in_chunk = m.sb("in_chunk", [128, 2 * NC * V])
        hx = m.sb("hx", [128, D])
        stats, mv, rstd = m.sb("stats", [128, 6]), m.sb("mv", [128, 2]), m.sb("rstd", [128, 1])
        xn, xT = m.sb("xn", [128, D]), m.sb("xT", [128, 2, NT])
        fg = m.sb("fg", [HD, 2, NT])
        q, kraw, k2, k = m.sb("q", [128, D]), m.sb("kraw", [128, D]), m.sb("k2", [128, D]), m.sb("k", [128, D])
        kr, vt, gate = m.sb("kr", [128, D]), m.sb("vt", [128, D]), m.sb("gate", [128, D])
        tanh_beta, tanh_gate = m.sb("tanh_beta", [128, D]), m.sb("tanh_gate", [128, D])
        nbeta, nbk = m.sb("nbeta", [128, D]), m.sb("nbk", [128, D])
        fabs, flog = m.sb("fabs", [128, D]), m.sb("flog", [128, D])
        decay = m.sb("decay", [128, 2 * NC * V])
        L = m.sb("L", [128, 2 * NC * V])
        fac, facin = m.sb("fac", [128, LV + 1, 2 * NC * V]), m.sb("facin", [128, 2 * NC * V])
        diff = fac
        lower = m.sb("lower", [128, LV, 2 * NC, V])
        above = [m.sb(f"above{l}", [128, 2 * NC * UP[l]]) for l in range(LV)]
        kout, koutT = m.sb("kout", [128, 2 * NC * V]), m.sb("koutT", [128, 2 * NC * V])
        PA = m.sb("PA", [128, 2, NC, W])
        kiq, at = m.sb("kiq", [128, NC, A_T]), m.sb("at", [128, NC, SLAB - A_T])
        Pb = m.sb("Pb", [128, V, 128])
        LP = Pb
        X = m.sb("X", [128, V, 128])
        XT = m.sb("XT", [128, NC, 2 * GB * V])
        tmp = m.sb("tmp", [128, 4 * (V - 1) ** 2])
        eg = m.sb("eg", [128, NC, 2 * (B + 1)])
        stage = [m.sb(f"stage{i}", [128, GB, SLAB]) for i in range(2)]
        xst = [m.sb(f"xst{i}", [128, 2 * GB * V]) for i in range(2)]
        vst = [m.sb(f"vst{i}", [128, 512]) for i in range(2)]
        S = [m.sb(f"S{i}", [128, 512]) for i in range(2)]
        tS, R, U, O = m.sb("tS", [128, 512]), m.sb("R", [128, 512]), m.sb("U", [128, 512]), m.sb("O", [128, 512])
        bank = [m.ps(f"bank{i}") for i in range(8)]
        b_x, b_qk, b_vb, b_fg = bank[4:8]
        ring = bank[0:4]

        consts, wb_ready, zeroed = m.sem("consts"), m.sem("wb_ready"), m.sem("zeroed")
        loaded, moments, rstds, normed = m.sem("loaded"), m.sem("moments"), m.sem("rstds"), m.sem("normed")
        pe_x, x_ready, pe_fg, fg_ready = m.sem("pe_x"), m.sem("x_ready"), m.sem("pe_fg"), m.sem("fg_ready")
        pe_proj, pe_qk, pe_f, act_proj, k2_ready, pe_ss = m.sem("pe_proj"), m.sem("pe_qk"), m.sem("pe_f"), m.sem("act_proj"), m.sem("k2_ready"), m.sem("pe_ss")
        k_ready, kr_ready, flog_ready = m.sem("k_ready"), m.sem("kr_ready"), m.sem("flog_ready")
        diff_ready, fac_ready, kq_ready = m.sem("diff_ready"), m.sem("fac_ready"), m.sem("kq_ready")
        scores, taken = m.sem("scores"), m.sem("taken")
        v_out, gate_out, kiq_out, at_out = m.sem("v_out"), m.sem("gate_out"), m.sem("kiq_out"), m.sem("at_out")
        gate_ready, nb_ready, pool_done = m.sem("gate_ready"), m.sem("nb_ready"), m.sem("pool_done")
        pa_ready, at_copied, kout_ready, kout_copied = m.sem("pa_ready"), m.sem("at_copied"), m.sem("kout_ready"), m.sem("kout_copied")
        lane_ps, lane_sb, inverted = m.sem("lane_ps"), m.sem("lane_sb"), m.sem("inverted")
        xt_ps, xt_sb = m.sem("xt_ps"), m.sem("xt_sb")
        staged, v_staged = [m.sem("staged0"), m.sem("staged1")], [m.sem("v_staged0"), m.sem("v_staged1")]
        R_ps, R_sb, U_ps, U_sb = m.sem("R_ps"), m.sem("R_sb"), m.sem("U_ps"), m.sem("U_sb")
        S_ps, S_sb, O_ps, O_sb, o_out = m.sem("S_ps"), m.sem("S_sb"), m.sem("O_ps"), m.sem("O_sb"), m.sem("o_out")
        tS_ready, R_copied, S_copied = m.sem("tS_ready"), m.sem("R_copied"), m.sem("S_copied")
        act_steps, dve_steps, pool_steps, passed = m.sem("act_steps"), m.sem("dve_steps"), m.sem("pool_steps"), m.sem("passed")
        block = ctx.enter_context(nc.Block())

        def chunks(x):
            return x.rearrange("p (g c w) -> p g c w", g=2, c=NC)

        def tokens(x):
            return x.rearrange("p (n t) -> p n t", t=T)

        def upper(x, l):
            if l == 0:
                return x.rearrange("p c (t k) -> p c t k", k=3)[:, :, :, 1:]
            return x.rearrange("p c (s u k) -> p c s u k", u=2, k=3 << (l - 1))[:, :, :, 1]

        def fronts(g):
            return GB * (g + 1) + 1

        def groups(first, project, invert, finish, sweep):
            first()
            project(0)
            invert(0)
            finish(0)
            with block_engine[0].Fori(0, NG - 1) as g:
                project(g + 1)
                invert(g + 1)
                sweep(g)
                finish(g + 1)
            sweep(NG - 1)

        block_engine = [None]

        @block.sync
        def _(sp):
            block_engine[0] = sp
            for dst, src in ((wq, a.Wq), (wk, a.Wk), (wv, a.Wv), (wb8, a.Wbeta)):
                sp.dma_start(dst[:], src.rearrange("(t p) n -> p t n", p=128)).then_inc(consts, 16)
            sp.dma_start(wfg[:, :, 0:HD], a.Wf1.rearrange("(t p) n -> p t n", p=128)).then_inc(consts, 16)
            sp.dma_start(wfg[:, :, HD:], a.Wog1.rearrange("(t p) n -> p t n", p=128)).then_inc(consts, 16)
            sp.dma_start(wf2[:], a.Wf2).then_inc(consts, 16)
            sp.dma_start(wog2[:], a.Wog2).then_inc(consts, 16)
            sp.dma_start(ident[:], a.ident).then_inc(consts, 16)
            sp.dma_start(head_ones[:], a.head_ones).then_inc(consts, 16)
            sp.dma_start(levels[:], a.levels.rearrange("p (l w) -> p l w", l=LV)).then_inc(consts, 16)
            sp.dma_start(in_chunk[:], a.in_chunk).then_inc(consts, 16)

            def load(y, at_batch):
                if not (isinstance(y, int) and y == 0):
                    hold(sp, normed, y, passed)
                sp.dma_start(hx[0:1 + NPOS], scratch.z[at_batch]).then_inc(loaded, 16)
                sp.dma_start(hx[1 + NPOS:N], a.txt[at_batch]).then_inc(loaded, 16)

            def store_front(x, load_next=lambda: None):
                hold(sp, gate_ready, x + 1, passed)
                hold(sp, act_proj, 3 * x + 3, passed)
                sp.dma_start(scratch.v[x].rearrange("g t w -> t g w"), vt[:].rearrange("p (g w) -> p g w", g=2)).then_inc(v_out, 16)
                sp.dma_start(scratch.gate[x], gate[:]).then_inc(gate_out, 16)
                load_next()
                hold(sp, pool_done, 5 * (x + 1), passed)
                hold(sp, kout_copied, x + 1, passed)
                sp.dma_start(scratch.slab[:, :, x, 0:A_T].rearrange("c p w -> p c w"), kiq[:]).then_inc(kiq_out, 16)

            def first():
                load(0, 0)
                load(1, 1)
                load(2, 2)
                store_front(0)

            def project(g):
                with sp.Fori(0, GB // 2) as b2:
                    for b in (b2 * 2, b2 * 2 + 1):
                        it = g * GB + b
                        store_front(it + 1, lambda: load(it + 3, (it + 3) % B))
                        hold(sp, at_copied, it + 1, passed)
                        sp.dma_start(scratch.slab[:, :, it, A_T:].rearrange("c p w -> p c w"), at[:]).then_inc(at_out, 16)

            values = scratch.v.rearrange("b g (c t) (h w) -> h c t (b g) w", c=NC, h=4)
            outs = scratch.o.rearrange("b g (c t) (h w) -> h c t (b g) w", c=NC, h=4)

            def sweep(g):
                hold(sp, v_out, 16 * (fronts(g + 1) if not isinstance(g, int) else fronts(g)), passed)
                hold(sp, kiq_out, 16 * (fronts(g + 1) if not isinstance(g, int) else fronts(g)), passed)
                hold(sp, at_out, 16 * GB * ((g + 2) if not isinstance(g, int) else NG), passed)
                hold(sp, xt_sb, 8 * (g + 1), passed)
                def load_chunk(c, i, before):
                    if before is not None:
                        hold(sp, O_ps, 2 * before + 4, passed)
                    sp.dma_start(stage[i][:], scratch.slab[c, :, bass.ds(g * GB, GB), :]).then_inc(staged[i], 16)
                    sp.dma_start(xst[i][:], XT[:, c, :]).then_inc(staged[i], 16)
                    for h in range(4):
                        sp.dma_start(vst[i][32 * h + 1:32 * h + 32:2].rearrange("p (y w) -> p y w", y=2 * GB),
                                     values[h, c, :, bass.ds(g * (2 * GB), 2 * GB), :]).then_inc(v_staged[i], 16)

                def store_chunk(c):
                    hold(sp, O_sb, 2 * (g * NC + c) + 2, passed)
                    for h in range(4):
                        sp.dma_start(outs[h, c, :, bass.ds(g * (2 * GB), 2 * GB), :],
                                     O[32 * h:32 * h + T].rearrange("p (y w) -> p y w", y=2 * GB)).then_inc(o_out, 16)

                sp.wait_ge(zeroed, 4)
                hold(sp, O_ps, 2 * NC * g + 2, passed)
                load_chunk(0, 0, None)
                load_chunk(1, 1, None)
                with sp.Fori(0, NC // 2 - 1) as c2:
                    for i in range(2):
                        c = c2 * 2 + i
                        store_chunk(c)
                        load_chunk(c + 2, i, g * NC + c)
                store_chunk(NC - 2)
                store_chunk(NC - 1)

            groups(first, project, lambda g: None, lambda g: None, sweep)
            sp.wait_ge(o_out, 64 * NG * NC)
            sp.wait_ge(loaded, 32 * (B + 3))
            sp.wait_ge(gate_out, 16 * (B + 1))
            sp.wait_ge(v_out, 16 * (B + 1))
            sp.wait_ge(kiq_out, 16 * (B + 1))
            sp.wait_ge(at_out, 16 * B)

        @block.tensor
        def _(pe):
            block_engine[0] = pe

            def wait(sem, value):
                if not (isinstance(value, int) and value <= 0):
                    hold(pe, sem, value, passed)

            pe.wait_ge(consts, 16 * 12)
            pe.wait_ge(wb_ready, 1)
            pe.wait_ge(zeroed, 4)
            pe.sem_inc(O_ps, 2)

            def transposes(y):
                wait(normed, y + 1)
                for t in range(2):
                    last = nc.tensor.transpose(b_x[:, 128 * t:128 * t + N], xn[0:N, 128 * t:128 * t + 128], ident[0:N, 0:N])
                last.then_inc(pe_x, 1)

            def project_qk(x):
                wait(x_ready, x + 1)
                for j in range(2):
                    for t in range(2):
                        last = nc.tensor.matmul(b_x[0:HD, 256 + 128 * j:384 + 128 * j], wfg[:, t, HD * j:HD * j + HD], xT[:, t, :], start=t == 0, stop=t == 1)
                last.then_inc(pe_fg, 1)
                for w, at_col in ((wk, D), (wq, 0)):
                    for hg in range(2):
                        for t in range(2):
                            last = nc.tensor.matmul(b_qk[:, at_col + 128 * hg:at_col + 128 * hg + 128], w[:, t, 128 * hg:128 * hg + 128], xT[:, t, :], start=t == 0, stop=t == 1)
                last.then_inc(pe_qk, 1)
                factors_out(x)

            def factors_out(x):
                wait(fg_ready, x + 1)
                for hg in range(2):
                    nc.tensor.matmul(b_fg[:, 128 * hg:128 * hg + 128], wf2[:, 128 * hg:128 * hg + 128], fg[:, 0, :], start=True, stop=True)
                nc.tensor.matmul(b_fg[:, D:], fg[:, 1, :], wog2[:], start=True, stop=True).then_inc(pe_f, 1)

            def project_rest(x):
                for t in range(2):
                    nc.tensor.matmul(b_vb[:, 0:D], xT[:, t, :], wv[:, t, :], start=t == 0, stop=t == 1)
                for hg in range(2):
                    for t in range(2):
                        last = nc.tensor.matmul(b_vb[:, D + 128 * hg:D + 128 * hg + 128], wb[:, t, 128 * hg:128 * hg + 128], xT[:, t, :], start=t == 0, stop=t == 1)
                last.then_inc(pe_proj, 1)

            def squares(x):
                wait(k2_ready, x + 1)
                nc.tensor.matmul(b_x[:, 0:D], head_ones[:], k2[:], start=True, stop=True).then_inc(pe_ss, 1)

            def score(it, n):
                l, hg = n // 2, n % 2
                if hg == 0:
                    wait(kq_ready, 3 * (LV * it + l + 1))
                if n == 0 or n > 3:
                    wait(taken, 2 * LV * it + max(0, n - 3))
                for c in range(NC):
                    for h in range(4):
                        r = slice(32 * h, 32 * h + 32)
                        last = nc.tensor.matmul(ring[n % 4][r, 32 * c:32 * c + UP[l]], lower[r, l, hg * NC + c, :], above[l][r, UP[l] * (hg * NC + c):UP[l] * (hg * NC + c) + UP[l]], start=True, stop=True)
                last.then_inc(scores, 1)

            def first():
                transposes(0)
                project_qk(0)
                project_rest(0)
                squares(0)
                transposes(1)

            def project(g):
                wait(O_sb, 2 * NC * (g - 1 if not isinstance(g, int) else 0))
                wait(S_sb, 18 * (g - 1 if not isinstance(g, int) else 0))
                wait(xt_sb, 8 * g)
                with pe.Fori(0, GB // 2) as b2:
                    for b in (b2 * 2, b2 * 2 + 1):
                        it = g * GB + b
                        project_qk(it + 1)
                        project_rest(it + 1)
                        score(it, 0)
                        score(it, 1)
                        squares(it + 1)
                        for n in range(2, 6):
                            score(it, n)
                        transposes(it + 2)
                        for n in range(6, 2 * LV):
                            score(it, n)
                wait(pa_ready, 2 * GB * (g + 1))
                wait(taken, 2 * LV * GB * (g + 1))
                for n in range(V // 4):
                    if n >= 4:
                        wait(lane_sb, 8 * g + n - 3)
                    for i in range(4):
                        last = nc.tensor.transpose(ring[n % 4][:, 128 * i:128 * i + 128], Pb[:, 4 * n + i, :], ident[:])
                    last.then_inc(lane_ps, 1)

            def finish(g):
                wait(inverted, g + 1)
                wait(lane_sb, 8 * (g + 1))
                wait(R_sb, 2 * NC * g)
                wait(U_sb, 2 * NC * g)
                for n in range(V // 4):
                    if n >= 4:
                        wait(xt_sb, 8 * g + n - 3)
                    for i in range(4):
                        last = nc.tensor.transpose(ring[n % 4][:, 128 * i:128 * i + 128], X[:, 4 * n + i, :], ident[:])
                    last.then_inc(xt_ps, 1)

            def sweep(g):
                wait(xt_sb, 8 * (g + 1))
                wait(lane_sb, 8 * (g + 2 if not isinstance(g, int) else NG))
                x1 = fronts(g + 1) if not isinstance(g, int) else fronts(g)
                wait(act_proj, 3 * x1)
                wait(flog_ready, x1)
                wait(kr_ready, x1)
                wait(x_ready, x1 + 1)
                with pe.Fori(0, NC // 2) as c2:
                    for i in range(2):
                        n = g * NC + c2 * 2 + i
                        st = stage[i]

                        def chain(p, h, at_col, w):
                            return st[32 * h:32 * h + 32, p // 2, at_col + w * (p % 2):at_col + w * (p % 2) + w]

                        wait(staged[i], 32 * (g * (NC // 2) + c2 + 1))
                        for half in range(2):
                            wait(S_sb, 18 * g + 2 * (c2 * 2 + i) + half + 1)
                            for p in range(8 * half, 8 * half + 8):
                                for h in range(4):
                                    r = slice(32 * h, 32 * h + 32)
                                    last = nc.tensor.matmul(bank[half][r, 32 * p:32 * p + 32], chain(p, h, KIN, V), S[i][r, 32 * p:32 * p + 32], start=True, stop=True)
                            last.then_inc(R_ps, 1)
                        for half in range(2):
                            wait(R_sb, 2 * n + half + 1)
                            for p in range(8 * half, 8 * half + 8):
                                for h in range(4):
                                    r = slice(32 * h, 32 * h + 32)
                                    last = nc.tensor.matmul(bank[2 + half][r, 32 * p:32 * p + 32], xst[i][r, 32 * p:32 * p + 32], R[r, 32 * p:32 * p + 32], start=True, stop=True)
                            last.then_inc(U_ps, 1)
                        for half in range(2):
                            wait(U_sb, 2 * n + half + 1)
                            for p in range(8 * half, 8 * half + 8):
                                for h in range(4):
                                    r = slice(32 * h, 32 * h + 32)
                                    last = nc.tensor.matmul(bank[4 + half][r, 32 * p:32 * p + 32], chain(p, h, KOUT, V), U[r, 32 * p:32 * p + 32], start=True, stop=True)
                            last.then_inc(S_ps, 1)
                        wait(O_sb, 2 * n)
                        for half in range(2):
                            for p in range(8 * half, 8 * half + 8):
                                for h in range(4):
                                    r = slice(32 * h, 32 * h + 32)
                                    o = bank[6 + half][32 * h:32 * h + T, 32 * p:32 * p + 32]
                                    nc.tensor.matmul(o, chain(p, h, Q_E, T), S[i][r, 32 * p:32 * p + 32], start=True, stop=False)
                                    last = nc.tensor.matmul(o, chain(p, h, A_T, T), U[r, 32 * p:32 * p + 32], start=False, stop=True)
                            last.then_inc(O_ps, 1)

            groups(first, project, lambda g: None, finish, sweep)

        @block.scalar
        def _(act):
            block_engine[0] = act
            steps = Steps(act, act_steps)

            def wait(sem, value):
                if not (isinstance(value, int) and value <= 0):
                    act.wait_ge(sem, value)

            def rows_root(y):
                wait(moments, y + 1)
                inverse_root(nc, steps, rstd[0:N], mv[0:N, 1:2], LN_EPS).then_inc(rstds, 1)

            def rows_copy(y):
                wait(pe_x, y + 1)
                wait(pe_proj, y)
                nc.scalar.activation(xT[:, :, 0:N], b_x[:, 0:256].rearrange("p (t n) -> p t n", t=2)[:, :, 0:N], ACT.Copy).then_inc(x_ready, 1)

            def front(x, y):
                wait(pe_fg, x + 1)
                wait(pe_f, x)
                nc.scalar.activation(fg[:], b_x[0:HD, 256:512].rearrange("p (t n) -> p t n", t=2), ACT.Copy).then_inc(fg_ready, 1)
                wait(pe_f, x + 1)
                wait(flog_ready, x)
                steps.link(nc.scalar.activation(fabs[:], b_fg[:, 0:D], ACT.Abs))
                steps.link(nc.scalar.activation(fabs[:], fabs[:], ACT.Exp, scale=-1.0))
                nc.scalar.activation(flog[:], fabs[:], ACT.Ln, bias=1.0).then_inc(act_proj, 1)
                nc.scalar.preload_act_table_set(SILU)
                wait(pe_qk, x + 1)
                wait(k_ready, x)
                wait(pe_ss, x)
                wait(kq_ready, 3 * LV * x)
                steps.link(nc.scalar.activation(kraw[:], b_qk[:, D:], ACT.Silu))
                nc.scalar.activation(k2[:], kraw[:], ACT.Square).then_inc(k2_ready, 1)
                wait(pool_done, 5 * x)
                steps.mark(nc.scalar.activation(q[:], b_qk[:, 0:D], ACT.Silu))
                wait(gate_ready, x)
                wait(flog_ready, x + 1)
                nc.scalar.activation(tanh_gate[:], b_fg[:, D:], ACT.Tanh, scale=0.5).then_inc(act_proj, 1)
                wait(pe_proj, x + 1)
                wait(v_out, 16 * x)
                steps.mark(nc.scalar.activation(vt[:], b_vb[:, 0:D], ACT.Silu))
                wait(nb_ready, x)
                steps.link(nc.scalar.activation(tanh_beta[:], b_vb[:, D:], ACT.Tanh, scale=0.5))
                act.sem_inc(act_proj, 1)
                nc.scalar.preload_act_table_set(LN_EXP)
                wait(pe_ss, x + 1)
                steps.link(nc.scalar.activation(kr[:], b_x[:, 0:D], ACT.Ln, bias=QK_EPS))
                nc.scalar.activation(kr[:], kr[:], ACT.Exp, scale=-0.5).then_inc(kr_ready, 1)
                rows_root(y)
                wait(diff_ready, x + 1)
                steps.mark(nc.scalar.activation(facin[:], L[:], ACT.Exp))
                nc.scalar.activation(fac[:], diff[:], ACT.Exp).then_inc(fac_ready, 1)

            def kout_section(x):
                wait(kout_ready, x + 1)
                wait(kiq_out, 16 * x)
                kt = chunks(koutT[:])
                nc.scalar.activation(kiq[:, :, KOUT:KOUT + 2 * V].rearrange("p c (g w) -> p g c w", g=2), kt, ACT.Copy).then_inc(kout_copied, 1)

            def first():
                nc.scalar.preload_act_table_set(LN_EXP)
                wait(zeroed, 4)
                rows_root(0)
                rows_copy(0)
                front(0, 1)
                rows_copy(1)
                kout_section(0)
                steps.restart()

            def project(g):
                with act.Fori(0, GB // 2) as b2:
                    for b in (b2 * 2, b2 * 2 + 1):
                        it = g * GB + b
                        front(it + 1, it + 2)
                        rows_copy(it + 2)
                        wait(at_out, 16 * it)
                        wait(pa_ready, 2 * it + 2)
                        nc.scalar.activation(at[:].rearrange("p c (g t) -> p g c t", g=2), PA[:].rearrange("p g c (t k) -> p g c t k", k=3)[:, :, :, :, 2], ACT.Copy).then_inc(at_copied, 1)
                        kout_section(it + 1)
                        steps.restart()
                for n in range(V // 4):
                    act.wait_ge(lane_ps, 8 * g + n + 1)
                    nc.scalar.activation(LP[:, 4 * n:4 * n + 4, :], ring[n % 4][:].rearrange("p (v x) -> p v x", v=4), ACT.Copy).then_inc(lane_sb, 1)

            def finish(g):
                for i in range(2):
                    wait(staged[i], 32 * (NC // 2) * g)
                for n in range(V // 4):
                    act.wait_ge(xt_ps, 8 * g + n + 1)
                    for i in range(4):
                        last = nc.scalar.activation(XT[:, :, 4 * n + i::V], ring[n % 4][:, 128 * i:128 * i + 128].rearrange("p (c x) -> p c x", c=NC), ACT.Copy)
                    last.then_inc(xt_sb, 1)

            def sweep(g):
                act.wait_ge(S_sb, 18 * g + 2)
                with act.Fori(0, NC // 2) as c2:
                    for i in range(2):
                        c = c2 * 2 + i
                        n = g * NC + c
                        parts = (slice(0, 256), slice(256, 512))
                        for half, cols in enumerate(parts):
                            act.wait_ge(R_ps, 2 * n + half + 1)
                            if half == 0:
                                act.wait_ge(U_ps, 2 * n)
                            nc.scalar.activation(R[:, cols], bank[half][:, cols], ACT.Copy).then_inc(R_copied, 1)
                        for half, cols in enumerate(parts):
                            act.wait_ge(U_ps, 2 * n + half + 1)
                            if half == 0:
                                act.wait_ge(O_ps, 2 * n + 2)
                            nc.scalar.activation(U[:, cols], bank[2 + half][:, cols], ACT.Copy).then_inc(U_sb, 1)
                        for half, cols in enumerate(parts):
                            act.wait_ge(S_ps, 2 * n + half + 1)
                            if half == 0:
                                act.wait_ge(tS_ready, n)
                            nc.scalar.activation(S[1 - i][:, cols], bank[4 + half][:, cols], ACT.Copy).then_inc(S_copied, 1)
                        for half, cols in enumerate(parts):
                            act.wait_ge(O_ps, 2 * n + half + 3)
                            if half == 0:
                                act.wait_ge(o_out, 64 * n)
                            nc.scalar.activation(O[:, cols], bank[6 + half][:, cols], ACT.Copy).then_inc(O_sb, 1)

            groups(first, project, lambda g: None, finish, sweep)

        @block.gpsimd
        def _(pool):
            block_engine[0] = pool

            def wait(sem, value):
                if not (isinstance(value, int) and value <= 0):
                    pool.wait_ge(sem, value)

            def front(x):
                wait(fac_ready, x + 1)
                wait(nb_ready, x + 1)
                wait(kiq_out, 16 * x)
                fin = chunks(facin[:])
                for hg in range(2):
                    kk = nbk[:, 128 * hg:128 * hg + 128].rearrange("p (c t) -> p c t", c=NC).unsqueeze(3).to_broadcast([128, NC, T, 2])
                    pool.tensor_tensor(kiq[:, :, KIN + V * hg:KIN + V * hg + V].rearrange("p c (t a) -> p c t a", a=2),
                                       fin[:, hg].rearrange("p c (t a) -> p c t a", a=2), kk, ALU.mult).then_inc(pool_done, 1)
                    pool.tensor_tensor(kiq[:, :, Q_E + T * hg:Q_E + T * hg + T], fin[:, hg, :, 1:V:2],
                                       q[:, 128 * hg:128 * hg + 128].rearrange("p (c t) -> p c t", c=NC), ALU.mult).then_inc(pool_done, 1)
                pool.tensor_copy(eg[:, :, bass.ds(2 * x, 2)], fin[:, :, :, V - 1].rearrange("p g c -> p c g")).then_inc(pool_done, 1)

            def project(g):
                with pool.Fori(0, GB // 2) as b2:
                    for b in (b2 * 2, b2 * 2 + 1):
                        front(g * GB + b + 1)

            def sweep(g):
                hold(pool, pool_done, 5 * (fronts(g + 1) if not isinstance(g, int) else fronts(g)), passed)
                hold(pool, S_sb, 18 * g, passed)
                nc.gpsimd.memset(S[0][:, 0:256], 0.0).then_inc(S_sb, 1)
                nc.gpsimd.memset(S[0][:, 256:512], 0.0).then_inc(S_sb, 1)
                with pool.Fori(0, NC // 2) as c2:
                    for i in range(2):
                        c = c2 * 2 + i
                        n = g * NC + c
                        pool.wait_ge(S_sb, 18 * g + 2 * c + 2)
                        pool.tensor_tensor(tS[:].rearrange("p (x w) -> p x w", w=HD), S[i][:].rearrange("p (x w) -> p x w", w=HD),
                                           eg[:, c, bass.ds(g * (2 * GB), 2 * GB)].unsqueeze(2).to_broadcast([128, 2 * GB, HD]), ALU.mult).then_inc(tS_ready, 1)
                        pool.wait_ge(v_staged[i], 64 * (g * (NC // 2) + c2 + 1))
                        for half in range(2):
                            cols = slice(256 * half, 256 * half + 256)
                            pool.wait_ge(R_copied, 2 * n + half + 1)
                            pool.tensor_tensor(R[:, cols], R[:, cols], vst[i][:, cols], ALU.add).then_inc(R_sb, 1)
                        pool.wait_ge(tS_ready, n + 1)
                        for half in range(2):
                            cols = slice(256 * half, 256 * half + 256)
                            pool.wait_ge(S_copied, 2 * n + half + 1)
                            pool.tensor_tensor(S[1 - i][:, cols], S[1 - i][:, cols], tS[:, cols], ALU.add).then_inc(S_sb, 1)

            groups(lambda: front(0), project, lambda g: None, lambda g: None, sweep)

        @block.vector
        def _(dve):
            block_engine[0] = dve
            steps = Steps(dve, dve_steps)

            def wait(sem, value):
                if not (isinstance(value, int) and value <= 0):
                    dve.wait_ge(sem, value)

            dve.wait_ge(consts, 16 * 12)
            nc.vector.tensor_copy(wb[:].rearrange("p t (h w) -> p t h w", h=H), wb8[:].unsqueeze(3).to_broadcast([128, 2, H, HD])).then_inc(wb_ready, 1)
            for x in (xT, vst[0], vst[1], lower):
                nc.vector.memset(x[:], 0.0).then_inc(zeroed, 1)
            steps.mark(nc.vector.memset(decay[:], 0.0))
            steps.mark(nc.vector.memset(PA[:], 0.0))
            steps.link(nc.vector.memset(X[:], 0.0))
            for v in range(V):
                steps.mark(nc.vector.memset(X[:, v, v:128:V], 1.0))
            steps.restart()

            def rows_stats(y):
                wait(rstds, y)
                wait(loaded, 32 * (y + 1))
                steps.link(nc.vector.bn_stats(stats[0:N], hx[0:N]))
                nc.vector.bn_aggr(mv[0:N], stats[0:N]).then_inc(moments, 1)

            def rows_norm(y):
                wait(rstds, y + 1)
                wait(pe_x, y)
                nc.vector.tensor_scalar(xn[0:N], hx[0:N], mv[0:N, 0:1], rstd[0:N], ALU.subtract, ALU.mult).then_inc(normed, 1)

            def decays(x):
                wait(act_proj, 3 * x + 1)
                wait(fac_ready, x)
                nc.vector.scalar_tensor_tensor(out=decay[:, 1::2], in0=b_fg[:, 0:D], scalar=0.0, in1=flog[:], op0=ALU.min, op1=ALU.subtract).then_inc(flog_ready, 1)
                wait(flog_ready, x + 1)
                steps.link(nc.vector.tensor_tensor_scan(L[:], in_chunk[:], decay[:], 0.0, ALU.mult, ALU.add))
                for l in range(LV):
                    w = 1 << l
                    s = L[:].rearrange("p (n s w) -> p n s w", s=2, w=w)
                    d = diff[:, l].rearrange("p (n s w) -> p n s w", s=2, w=w)
                    top = s[:, :, 1, 0:1].to_broadcast([128, 2 * NC * V // (2 * w), w])
                    steps.mark(nc.vector.tensor_tensor(d[:, :, 1], s[:, :, 1], top, ALU.subtract))
                    steps.mark(nc.vector.tensor_tensor(d[:, :, 0], top, s[:, :, 0], ALU.subtract))
                s = L[:].rearrange("p (n w) -> p n w", w=V)
                steps.mark(nc.vector.tensor_tensor(diff[:, LV].rearrange("p (n w) -> p n w", w=V), s[:, :, V - 1:V].to_broadcast([128, 2 * NC, V]), s, ALU.subtract))
                steps.wait()
                dve.sem_inc(diff_ready, 1)

            def gates(x):
                wait(act_proj, 3 * x + 2)
                wait(gate_out, 16 * x)
                nc.vector.tensor_scalar(gate[:], tanh_gate[:], 0.5, 0.5, ALU.mult, ALU.add).then_inc(gate_ready, 1)

            def keys(x):
                gates(x)
                wait(kr_ready, x + 1)
                nc.vector.tensor_tensor(k[:], kraw[:], kr[:], ALU.mult).then_inc(k_ready, 1)
                wait(k_ready, x + 1)
                wait(fac_ready, x + 1)

            def pairs_of_keys():
                return tokens(k[:]).unsqueeze(3).to_broadcast([128, 2 * NC, T, 2])

            def factors(x, l):
                wait(scores, 2 * LV * (x - 1) + 2 * l + 2 if not isinstance(x, int) else 0)
                if l == 0:
                    f, up = tokens(fac[:, 0, 1::2]), above[0][:].rearrange("p (n t k) -> p n t k", t=T, k=2)
                    nc.vector.tensor_tensor(lower[:, 0].rearrange("p n (t a) -> p n t a", a=2), fac[:, 0].rearrange("p (n t a) -> p n t a", t=T, a=2),
                                            pairs_of_keys(), ALU.mult).then_inc(kq_ready, 1)
                    nc.vector.tensor_tensor(up[:, :, :, 0], f, tokens(k[:]), ALU.mult).then_inc(kq_ready, 1)
                    nc.vector.tensor_tensor(up[:, :, :, 1], f, tokens(q[:]), ALU.mult).then_inc(kq_ready, 1)
                    return
                w = 1 << (l - 1)
                kb = k[:].rearrange("p (s u w) -> p s u w", u=2, w=w)
                qb = q[:].rearrange("p (s u w) -> p s u w", u=2, w=w)
                f = fac[:, l].rearrange("p (s u w a) -> p s u w a", u=2, w=w, a=2)
                low = lower[:, l].rearrange("p n v -> p (n v)").rearrange("p (s u w a) -> p s u w a", u=2, w=w, a=2)
                up = above[l][:].rearrange("p (s w k) -> p s w k", w=w, k=3)
                both = [128, D // (2 * w), w, 2]
                nc.vector.tensor_tensor(low[:, :, 0], f[:, :, 0], kb[:, :, 0].unsqueeze(3).to_broadcast(both), ALU.mult).then_inc(kq_ready, 1)
                nc.vector.tensor_tensor(up[:, :, :, 0:2], f[:, :, 1], kb[:, :, 1].unsqueeze(3).to_broadcast(both), ALU.mult).then_inc(kq_ready, 1)
                nc.vector.tensor_tensor(up[:, :, :, 2], f[:, :, 1, :, 1], qb[:, :, 1], ALU.mult).then_inc(kq_ready, 1)

            def writes(x):
                steps.link(nc.vector.tensor_tensor(kout[:].rearrange("p (n t a) -> p n t a", t=T, a=2), fac[:, LV].rearrange("p (n t a) -> p n t a", t=T, a=2), pairs_of_keys(), ALU.mult))
                wait(kout_copied, x)
                nc.vector.transpose(koutT[:], kout[:]).then_inc(kout_ready, 1)
                wait(act_proj, 3 * x + 3)
                steps.link(nc.vector.tensor_scalar(nbeta[:], tanh_beta[:], -1.0, -1.0, ALU.mult, ALU.add))
                wait(pool_done, 5 * x)
                nc.vector.tensor_tensor(nbk[:], k[:], nbeta[:], ALU.mult).then_inc(nb_ready, 1)

            def take(it, n):
                l, hg = n // 2, n % 2
                hold(dve, scores, 2 * LV * it + n + 1, passed)
                dst = upper(PA[:, hg], l)
                k1, k0 = dst.shape[-2:]
                mask = levels[:, l, 0:UP[l]].rearrange("p (s k) -> p s k", s=k1).unsqueeze(1).to_broadcast([128, NC, k1, k0])
                src = ring[n % 4][:, 0:NC * 32].rearrange("p (c w) -> p c w", w=32)[:, :, 0:UP[l]].rearrange("p c (s k) -> p c s k", s=k1)
                nc.vector.copy_predicated(dst, mask, src).then_inc(taken, 1)
                hold(dve, taken, 2 * LV * it + n + 1, passed)

            def times_beta(b, it):
                pbv = Pb[:].rearrange("p (t a) (c y) -> p c t a y", a=2, c=NC)
                for hg in range(2):
                    nb = nbeta[:, 128 * hg:128 * hg + 128].rearrange("p (c t) -> p c t", c=NC).unsqueeze(3).to_broadcast([128, NC, T, 2])
                    nc.vector.tensor_tensor(pbv[:, :, :, :, 2 * b + hg], PA[:, hg].rearrange("p c (t k) -> p c t k", k=3)[:, :, :, 0:2], nb, ALU.mult).then_inc(pa_ready, 1)

            def first():
                rows_stats(0)
                rows_norm(0)
                rows_stats(1)
                decays(0)
                rows_norm(1)
                keys(0)
                for l in range(LV):
                    factors(0, l)
                writes(0)
                steps.restart()

            def project(g):
                with dve.Fori(0, GB // 2) as b2:
                    for b in (b2 * 2, b2 * 2 + 1):
                        it = g * GB + b
                        dve.wait_ge(nb_ready, it + 1)
                        dve.wait_ge(at_copied, it)
                        rows_stats(it + 2)
                        decays(it + 1)
                        for n in range(3):
                            take(it, n)
                        rows_norm(it + 2)
                        for n in range(3, 6):
                            take(it, n)
                        keys(it + 1)
                        factors(it + 1, 0)
                        factors(it + 1, 1)
                        take(it, 6)
                        factors(it + 1, 2)
                        take(it, 7)
                        take(it, 8)
                        factors(it + 1, 3)
                        take(it, 9)
                        times_beta(b, it)
                        factors(it + 1, 4)
                        writes(it + 1)
                        steps.restart()

            def invert(g):
                dve.wait_ge(lane_sb, 8 * (g + 1))
                for v in range(1, V):
                    lp = LP[:, v].rearrange("p (h m) -> p h m", h=4)[:, :, 0:v].unsqueeze(2).to_broadcast([128, 4, v, v])
                    x = X[:, 0:v].rearrange("p m (h c) -> p h c m", h=4)[:, :, 0:v, :]
                    steps.link(nc.vector.tensor_tensor(tmp[:, 0:4 * v * v].rearrange("p (h c m) -> p h c m", h=4, c=v), lp, x, ALU.mult))
                    ins = nc.vector.tensor_reduce(X[:, v].rearrange("p (h c) -> p h c", h=4)[:, :, 0:v], tmp[:, 0:4 * v * v].rearrange("p (h c m) -> p h c m", h=4, c=v), axis=AX.X, op=ALU.add)
                    if v < V - 1:
                        steps.link(ins)
                    else:
                        ins.then_inc(inverted, 1)
                steps.restart()

            groups(first, project, invert, lambda g: None, lambda g: None)


def mixture(nc, a, scratch):
    with ExitStack() as ctx:
        m = Memory(nc, ctx)
        acc = m.sb("acc", [128, ST, D])
        ident = m.sb("ident_mix", [128, 128])
        we = [m.sb(f"we{i}", [128, 4, 2, D]) for i in range(WS)]
        w_loaded = [m.sem(f"we_loaded{i}") for i in range(WS)]
        bank = [m.ps(f"mbank{i}") for i in range(4, 8)]
        with ExitStack() as inner:
            dispatch(nc, a, scratch, Memory(nc, inner), acc, ident, bank, we, w_loaded)
        with ExitStack() as inner:
            answers = m.sb("answers", [128, ST, D])
            experts(nc, a, Memory(nc, inner), acc, answers, ident, bank, we, w_loaded)
        with ExitStack() as inner:
            combine(nc, a, scratch, Memory(nc, inner), answers, bank)


def load_expert_weights(sp, a, we, w_loaded, tile, slot):
    w = a.expert_w.rearrange("(s e) (t p) h -> s p e t h", e=4, p=128)
    for e in range(4):
        sp.dma_start(we[slot][:, e], w[tile, :, e]).then_inc(w_loaded[slot], 16)


def dispatch(nc, a, scratch, m, acc, ident, banks, we, w_loaded):
    by_misc, ring = banks[0], banks[1:4]
    logits = m.ps("logits", [128, NS])
    wo, norm_w = m.sb("wo", [128, 2, D]), m.sb("norm_w", [128, 2])
    phi = m.sb("phi", [128, 2, NS])
    parts = m.sb("parts", [1, 3, NS], BF16)
    bias3, ones3 = m.sb("bias3", [3, NS], BF16), m.sb("ones3", [3, N], BF16)
    ot = [m.sb(f"ot{i}", [N, D]) for i in range(2)]
    gt = [m.sb(f"gt{i}", [N, D]) for i in range(2)]
    hx = [m.sb(f"mhx{i}", [N, D]) for i in range(2)]
    h2 = [m.sb(f"h2{i}", [N, D]) for i in range(2)]
    fresh = [m.sb(f"fresh{i}", [N, D]) for i in range(2)]
    x = [m.sb(f"mx{i}", [N, D]) for i in range(4)]
    xT = [m.sb(f"mxT{i}", [128, 2, N]) for i in range(2)]
    y, y2, yn, yT = m.sb("y", [N, D]), m.sb("y2", [N, D]), m.sb("yn", [N, D]), m.sb("yT", [128, 2, N])
    ms, rr = m.sb("ms", [N, H]), m.sb("rr", [N, H])
    stats, mv, rstd = m.sb("mstats", [N, 6]), m.sb("mmv", [N, 2]), m.sb("mrstd", [N, 1])
    Dx = [m.sb(f"Dx{i}", [N, NS]) for i in range(4)]
    Cx = [m.sb(f"Cx{i}", [N, NS]) for i in range(4)]
    bias, rest = Cx[0][0:1], Cx[1][0:1]
    m1, s1 = m.sb("m1", [N, NEXP]), m.sb("s1", [N, NEXP])
    m2, s2 = m.sb("m2", [N, PS]), m.sb("s2", [N, PS])
    r1, r2 = m.sb("r1", [N, NEXP]), m.sb("r2", [N, PS])
    cT = [m.sb(f"cT{i}", [128, ST, N]) for i in range(2)]
    consts, split, bias_ready, acc_zero = m.sem("mconsts"), m.sem("bias_split"), m.sem("bias_ready"), m.sem("acc_zero")
    loaded = [m.sem("mloaded0"), m.sem("mloaded1")]
    squares, roots, yn_ready, yT_ps, yT_ready, projected = (m.sem(n) for n in ("squares", "roots", "yn_ready", "yT_ps", "yT_ready", "wo_done"))
    h2_ready, moments, rstds, x_ready, x_kept, xT_ps, xT_ready = (
        m.sem(n) for n in ("h2_ready", "mmoments", "mrstds", "mx_ready", "mx_kept", "mxT_ps", "mxT_ready"))
    l_ps, l_copied, e1, max2, e2, exp1, exp2, inv1, inv2, D_ready, C_ready = (
        m.sem(n) for n in ("l_ps", "l_copied", "e1_ready", "max2", "e2_ready", "exp1", "exp2", "inv1", "inv2", "D_ready", "C_ready"))
    cT_ps, cT_sb, acc_ps, acc_added = (m.sem(n) for n in ("cT_ps", "cT_sb", "acc_ps", "acc_added"))
    h_out = [m.sem("h_out0"), m.sem("h_out1")]
    cT_out = [m.sem("cT_out0"), m.sem("cT_out1")]
    dve_steps, act_steps, passed = m.sem("mdve_steps"), m.sem("mact_steps"), m.sem("mpassed")
    PAIRS = B // 2

    def known(h):
        return isinstance(h, int)

    def all_steps(engine, first, step, summing, end):
        first()
        for i in range(2):
            step(0, i, 0)
        end()
        with engine.Fori(0, PAIRS // 2 - 1) as q:
            for p in (1, 0):
                for i in range(2):
                    step(2 * q + 2 - p, i, p)
            end()
        for i in range(2):
            step(PAIRS - 1, i, 1)
        for n in range(8):
            summing(PAIRS - 1, n, 1)
        end()

    def nothing(*_):
        return None

    block = m.ctx.enter_context(nc.Block())

    @block.sync
    def _(sp):
        sp.dma_start(bias, a.phi_b.unsqueeze(0)).then_inc(consts, 16)
        sp.dma_start(ident[:], a.ident).then_inc(consts, 16)
        sp.dma_start(wo[:], a.Wo.rearrange("(t p) n -> p t n", p=128)).then_inc(consts, 16)
        sp.dma_start(norm_w[:], a.norm_w).then_inc(consts, 16)
        sp.dma_start(phi[:], a.phi_wT.rearrange("(t p) n -> p t n", p=128)).then_inc(consts, 16)

        def load(f, i):
            sp.dma_start(ot[i][:].rearrange("p (g w) -> p g w", g=2), scratch.o[f, :, 0:N, :].rearrange("g t w -> t g w")).then_inc(loaded[i], 16)
            sp.dma_start(gt[i][:], scratch.gate[f, 0:N, :]).then_inc(loaded[i], 16)
            sp.dma_start(hx[i][0:1 + NPOS], scratch.z[f]).then_inc(loaded[i], 16)
            sp.dma_start(hx[i][1 + NPOS:N], a.txt[f]).then_inc(loaded[i], 16)

        def store_h(f, i):
            hold(sp, h2_ready, f + 1, passed)
            sp.dma_start(scratch.h[f], h2[i][:]).then_inc(h_out[i], 16)

        def first():
            load(0, 0)
            load(1, 1)
            sp.wait_ge(split, 5)
            for r in range(3):
                sp.dma_start(bias3[r:r + 1, :], parts[0:1, r, :]).then_inc(bias_ready, 16)
            store_h(0, 0)
            for tile in range(WS):
                load_expert_weights(sp, a, we, w_loaded, tile, tile)

        def store_weights(J, i):
            hold(sp, cT_sb, 8 * J + 4 * i + 4, passed)
            sp.dma_start(scratch.cT[2 * J + i], cT[i][:].rearrange("p s n -> p (s n)")).then_inc(cT_out[i], 16)

        def step(J, i, p):
            h = 2 * J + i
            if not (known(h) and h + 2 >= B):
                load(h + 2, i)
            if not (known(h) and h + 1 >= B):
                store_h(h + 1, 1 - i)
            if not (known(J) and J == 0):
                store_weights(J - 1, i)

        def summing(J, n, p):
            if n % 4 == 3:
                store_weights(J, n // 4)

        all_steps(sp, first, step, summing, nothing)
        for i in range(2):
            sp.wait_ge(h_out[i], 16 * PAIRS)
            sp.wait_ge(cT_out[i], 16 * PAIRS)

    @block.tensor
    def _(pe):
        def wait(sem, value):
            if not (isinstance(value, int) and value <= 0):
                hold(pe, sem, value, passed)

        def gated(f):
            wait(yn_ready, f + 1)
            wait(xT_ready, f)
            wait(h2_ready, f)
            for t in range(2):
                last = nc.tensor.transpose(by_misc[:, 128 * t:128 * t + N], yn[:, 128 * t:128 * t + 128], ident[0:N, 0:N])
            last.then_inc(yT_ps, 1)

        def project(f):
            wait(yT_ready, f + 1)
            for t in range(2):
                last = nc.tensor.matmul(by_misc[0:N, D:], yT[:, t, :], wo[:, t, :], start=t == 0, stop=t == 1)
            last.then_inc(projected, 1)

        def rows(f, i):
            wait(x_ready, f + 1)
            for t in range(2):
                last = nc.tensor.transpose(by_misc[:, 128 * t:128 * t + N], fresh[i][:, 128 * t:128 * t + 128], ident[0:N, 0:N])
            last.then_inc(xT_ps, 1)

        def summing(J, n, p):
            for kind in range(2):
                turn = 2 * n + kind
                if turn < 3:
                    wait(cT_sb, 8 * J)
                    wait(acc_added, 8 * J)
                elif kind == 0:
                    wait(acc_added, 8 * J + (turn - 3) // 2 + 1)
                else:
                    wait(cT_sb, 8 * J + (turn - 3) // 2 + 1)
                out = ring[turn % 3]
                if kind == 0:
                    i, s0 = n // 4, 4 * (n % 4)
                    wait(C_ready, 2 * J + i + 1)
                    for s in range(4):
                        last = nc.tensor.transpose(out[:, 128 * s:128 * s + N], Cx[2 * p + i][:, 128 * (s0 + s):128 * (s0 + s) + 128], ident[0:N, 0:N])
                    last.then_inc(cT_ps, 1)
                else:
                    wait(D_ready, 2 * J + 2)
                    wait(x_kept, 2 * J + 2)
                    for s in range(2):
                        st = 2 * n + s
                        for i in range(2):
                            last = nc.tensor.matmul(out[:, D * s:D * s + D], Dx[2 * p + i][:, 128 * st:128 * st + 128], x[2 * p + i][:], start=i == 0, stop=i == 1)
                    last.then_inc(acc_ps, 1)

        def first():
            gated(0)
            project(0)
            rows(0, 0)

        def step(J, i, p):
            h = 2 * J + i
            wait(xT_ready, h + 1)
            wait(l_copied, h)
            for s in range(4):
                cols = slice(512 * s, 512 * s + 512)
                for t in range(2):
                    nc.tensor.matmul(logits[0:N, cols], xT[i][:, t, :], phi[:, t, cols], start=t == 0, stop=False)
                last = nc.tensor.matmul(logits[0:N, cols], ones3[:], bias3[:, cols], start=False, stop=True)
            last.then_inc(l_ps, 1)
            sums = summing if not (known(J) and J == 0) else nothing
            front = not (known(h) and h + 1 >= B)
            if front:
                gated(h + 1)
            sums(J - 1, 4 * i, 1 - p)
            if front:
                project(h + 1)
            sums(J - 1, 4 * i + 1, 1 - p)
            sums(J - 1, 4 * i + 2, 1 - p)
            if front:
                rows(h + 1, 1 - i)
            sums(J - 1, 4 * i + 3, 1 - p)

        pe.wait_ge(consts, 16 * 5)
        pe.wait_ge(bias_ready, 48)
        all_steps(pe, first, step, summing, nothing)

    @block.scalar
    def _(act):
        steps = Steps(act, act_steps)

        def wait(sem, value):
            if not (isinstance(value, int) and value <= 0):
                act.wait_ge(sem, value)

        def gate_roots(f):
            wait(squares, f + 1)
            wait(yn_ready, f)
            steps.link(nc.scalar.activation(rr[:], ms[:], ACT.Ln, bias=QK_EPS, scale=1.0 / HD))
            nc.scalar.activation(rr[:], rr[:], ACT.Exp, scale=-0.5).then_inc(roots, 1)

        def gated(f):
            wait(yT_ps, f + 1)
            wait(projected, f)
            for t in range(2):
                last = nc.scalar.activation(yT[:, t, :], by_misc[:, 128 * t:128 * t + N], ACT.Copy, scale=norm_w[:, t:t + 1])
            last.then_inc(yT_ready, 1)

        def row_roots(f):
            wait(moments, f + 1)
            wait(x_kept, f)
            inverse_root(nc, steps, rstd[:], mv[:, 1:2], LN_EPS).then_inc(rstds, 1)

        def rows(f, i):
            wait(xT_ps, f + 1)
            wait(l_ps, f - 1)
            nc.scalar.activation(xT[i][:], by_misc[:, 0:256].rearrange("p (t n) -> p t n", t=2)[:, :, 0:N], ACT.Copy).then_inc(xT_ready, 1)

        def summing(J, n, p):
            i, s0 = n // 4, 4 * (n % 4)
            if n % 4 == 0:
                wait(cT_out[i], 16 * J)
            wait(cT_ps, 8 * J + n + 1)
            nc.scalar.activation(cT[i][:, s0:s0 + 4, :], ring[(2 * n) % 3][:].rearrange("p (s n) -> p s n", s=4)[:, :, 0:N], ACT.Copy).then_inc(cT_sb, 1)

        def first():
            gate_roots(0)
            gated(0)
            row_roots(0)
            rows(0, 0)
            gate_roots(1)

        def step(J, i, p):
            h = 2 * J + i
            slot = 2 * p + i
            wait(l_ps, h + 1)
            wait(cT_ps, 8 * (J - 1) if not (known(J) and J == 0) else 0)
            nc.scalar.activation(Cx[slot][:], logits[0:N, :], ACT.Copy).then_inc(l_copied, 1)
            sums = summing if not (known(J) and J == 0) else nothing
            front = not (known(h) and h + 1 >= B)
            if front:
                gated(h + 1)
            sums(J - 1, 4 * i, 1 - p)
            sums(J - 1, 4 * i + 1, 1 - p)
            if front:
                row_roots(h + 1)
            sums(J - 1, 4 * i + 2, 1 - p)
            wait(e1, h + 1)
            nc.scalar.activation(Dx[slot][:], Dx[slot][:], ACT.Exp).then_inc(exp1, 1)
            if front:
                rows(h + 1, 1 - i)
            sums(J - 1, 4 * i + 3, 1 - p)
            if not (known(h) and h + 2 >= B):
                gate_roots(h + 2)
            wait(e2, h + 1)
            nc.scalar.activation(Cx[slot][:], Cx[slot][:], ACT.Exp).then_inc(exp2, 1)

        act.wait_ge(consts, 16 * 5)
        nc.scalar.preload_act_table_set(LN_EXP)
        all_steps(act, first, step, summing, steps.restart)

    @block.gpsimd
    def _(pool):
        def by_expert(t, r):
            return t[:].rearrange("p (n s) -> p n s", n=NEXP), r[:].unsqueeze(2).to_broadcast([N, NEXP, PS])

        def by_slot(t, r):
            return t[:].rearrange("p (n s) -> p n s", n=NEXP), r[:].unsqueeze(1).to_broadcast([N, NEXP, PS])

        def step(J, i, p):
            h = 2 * J + i
            pool.wait_ge(e1, h + 1)
            pool.wait_ge(max2, h + 1)
            c, r = by_slot(Cx[2 * p + i], m2)
            pool.tensor_tensor(c, c, r, ALU.subtract).then_inc(e2, 1)
            pool.wait_ge(inv1, h + 1)
            d, r = by_expert(Dx[2 * p + i], r1)
            pool.tensor_tensor(d, d, r, ALU.mult).then_inc(D_ready, 1)
            pool.wait_ge(inv2, h + 1)
            c, r = by_slot(Cx[2 * p + i], r2)
            pool.tensor_tensor(c, c, r, ALU.mult).then_inc(C_ready, 1)

        all_steps(pool, nothing, step, nothing, nothing)

    @block.vector
    def _(dve):
        steps = Steps(dve, dve_steps)
        nc.vector.memset(acc[:], 0.0).then_inc(acc_zero, 1)
        dve.wait_ge(consts, 16 * 5)
        nc.vector.memset(ones3[:], 1.0).then_inc(split, 1)
        steps.link(nc.vector.tensor_copy(parts[0:1, 0, :], bias))
        steps.link(nc.vector.tensor_tensor(rest, bias, parts[0:1, 0, :], ALU.subtract))
        steps.link(nc.vector.tensor_copy(parts[0:1, 1, :], rest))
        steps.link(nc.vector.tensor_tensor(rest, rest, parts[0:1, 1, :], ALU.subtract))
        nc.vector.tensor_copy(parts[0:1, 2, :], rest).then_inc(split, 4)
        steps.restart()
        dve.wait_ge(acc_zero, 1)

        def wait(sem, value):
            if not (isinstance(value, int) and value <= 0):
                dve.wait_ge(sem, value)

        def gate_squares(f, i):
            wait(loaded[i], 64 * (f // 2 + 1) if known(f) else 64 * f[1])
            f = f if known(f) else f[0]
            steps.link(nc.vector.tensor_tensor(y[:], ot[i][:], gt[i][:], ALU.mult))
            steps.link(nc.vector.tensor_tensor(y2[:], y[:], y[:], ALU.mult))
            wait(roots, f)
            nc.vector.tensor_reduce(ms[:], y2[:].rearrange("p (h w) -> p h w", h=H), axis=AX.X, op=ALU.add).then_inc(squares, 1)

        def gate_norm(f):
            wait(roots, f + 1)
            wait(yT_ps, f)
            nc.vector.tensor_tensor(yn[:].rearrange("p (h w) -> p h w", h=H), y[:].rearrange("p (h w) -> p h w", h=H),
                                    rr[:].unsqueeze(2).to_broadcast([N, H, HD]), ALU.mult).then_inc(yn_ready, 1)

        def add_rows(f, i, before):
            wait(projected, f + 1)
            wait(h_out[i], 16 * before)
            nc.vector.tensor_tensor(h2[i][:], by_misc[0:N, D:], hx[i][:], ALU.add).then_inc(h2_ready, 1)
            wait(h2_ready, f + 1)
            steps.link(nc.vector.bn_stats(stats[:], h2[i][:]))
            nc.vector.bn_aggr(mv[:], stats[:]).then_inc(moments, 1)

        def norm_rows(f, i):
            wait(rstds, f + 1)
            wait(xT_ps, f - 1)
            nc.vector.tensor_scalar(fresh[i][:], h2[i][:], mv[:, 0:1], rstd[:], ALU.subtract, ALU.mult).then_inc(x_ready, 1)

        def summing(J, n, p):
            wait(acc_ps, 8 * J + n + 1)
            part = acc[:, 2 * n:2 * n + 2, :].rearrange("p s d -> p (s d)")
            wait(acc_added, 8 * J)
            nc.vector.tensor_tensor(part, ring[(2 * n + 1) % 3][:], part, ALU.add).then_inc(acc_added, 1)

        def first():
            gate_squares(0, 0)
            gate_norm(0)
            add_rows(0, 0, 0)
            norm_rows(0, 0)
            gate_squares(1, 1)
            gate_norm(1)

        def step(J, i, p):
            h = 2 * J + i
            slot = 2 * p + i
            d, c = (t[slot][:].rearrange("p (n s) -> p n s", n=NEXP) for t in (Dx, Cx))
            sums = summing if not (known(J) and J == 0) else nothing
            front = not (known(h) and h + 1 >= B)
            done = 8 * (J - 1) if not (known(J) and J == 0) else 0
            wait(acc_ps, done)
            nc.vector.tensor_scalar(x[slot][:], h2[i][:], mv[:, 0:1], rstd[:], ALU.subtract, ALU.mult).then_inc(x_kept, 1)
            wait(l_copied, h + 1)
            steps.link(nc.vector.tensor_reduce(m1[:], c, axis=AX.X, op=ALU.max))
            sums(J - 1, 4 * i, 1 - p)
            if front:
                add_rows(h + 1, 1 - i, J + i)
            nc.vector.tensor_tensor(d, c, m1[:].unsqueeze(2).to_broadcast([N, NEXP, PS]), ALU.subtract).then_inc(e1, 1)
            sums(J - 1, 4 * i + 1, 1 - p)
            if front:
                norm_rows(h + 1, 1 - i)
            wait(e2, h)
            nc.vector.tensor_reduce(m2[:], c.rearrange("p n s -> p s n"), axis=AX.X, op=ALU.max).then_inc(max2, 1)
            sums(J - 1, 4 * i + 2, 1 - p)
            wait(exp1, h + 1)
            steps.link(nc.vector.tensor_reduce(s1[:], d, axis=AX.X, op=ALU.add))
            wait(D_ready, h)
            nc.vector.reciprocal(r1[:], s1[:]).then_inc(inv1, 1)
            sums(J - 1, 4 * i + 3, 1 - p)
            more = not (known(h) and h + 2 >= B)
            if more:
                gate_squares(h + 2 if known(h) else (h + 2, J + 2), i)
                gate_norm(h + 2)
            wait(exp2, h + 1)
            steps.link(nc.vector.tensor_reduce(s2[:], c.rearrange("p n s -> p s n"), axis=AX.X, op=ALU.add))
            wait(C_ready, h)
            nc.vector.reciprocal(r2[:], s2[:]).then_inc(inv2, 1)

        all_steps(dve, first, step, summing, steps.restart)


def experts(nc, a, m, acc, answers, ident, banks, we, w_loaded):
    eb = m.sb("eb", [128, ST, D])
    stats, mv, rstd = m.sb("estats", [128, ST, 6]), m.sb("emv", [128, ST, 2]), m.sb("erstd", [128, ST])
    th = [m.sb(f"th{i}", [128, D]) for i in range(2)]
    thT = [m.sb(f"thT{i}", [128, 2, 128]) for i in range(2)]
    b_loaded = m.sem("eb_loaded")
    moments, rstds, normed, th_ready, thT_ps, thT_ready, y_ps, y_sb = (
        m.sem(n) for n in ("e_moments", "e_rstds", "e_normed", "th_ready", "thT_ps", "thT_ready", "ans_ps", "ans_sb"))
    act_steps, dve_steps, passed = m.sem("e_act_steps"), m.sem("e_dve_steps"), m.sem("e_passed")
    block = m.ctx.enter_context(nc.Block())

    @block.sync
    def _(sp):
        for e in range(4):
            sp.dma_start(eb[32 * e:32 * e + 32], a.expert_b.rearrange("(s e) h -> e s h", e=4)[e].partition_broadcast(32)).then_inc(b_loaded, 16)
        with sp.Fori(0, ST // WS - 1) as j:
            for slot in range(WS):
                hold(sp, y_ps, WS * j + slot + 1, passed)
                load_expert_weights(sp, a, we, w_loaded, WS * (j + 1) + slot, slot)

    @block.vector
    def _(dve):
        steps = Steps(dve, dve_steps)
        steps.link(nc.vector.tensor_scalar(acc[:], acc[:], -33000.0, 65000.0, ALU.max, ALU.min))
        for s in range(ST):
            steps.mark(nc.vector.bn_stats(stats[:, s], acc[:, s]))
        steps.wait()
        for s in range(ST):
            nc.vector.bn_aggr(mv[:, s], stats[:, s]).then_inc(moments, 1)
        dve.wait_ge(rstds, 1)
        for s in range(ST):
            nc.vector.tensor_scalar(acc[:, s], acc[:, s], mv[:, s, 0:1], rstd[:, s:s + 1], ALU.subtract, ALU.mult).then_inc(normed, 1)
        dve.wait_ge(b_loaded, 64)
        with dve.Fori(0, ST // WS) as j:
            for slot in range(WS):
                n, i = WS * j + slot, slot % 2
                dve.wait_ge(y_ps, n + 1)
                nc.vector.tensor_tensor(answers[:, n, :], banks[2 + i][:, 0:D], eb[:, n, :], ALU.add).then_inc(y_sb, 1)

    @block.scalar
    def _(act):
        steps = Steps(act, act_steps)
        nc.scalar.preload_act_table_set(LN_EXP)
        act.wait_ge(moments, ST)
        inverse_root(nc, steps, rstd[:], mv[:, :, 1], LN_EPS).then_inc(rstds, 1)
        nc.scalar.preload_act_table_set(SILU)
        with act.Fori(0, ST // WS) as j:
            for slot in range(WS):
                n, i = WS * j + slot, slot % 2
                act.wait_ge(normed, n + 1)
                act.wait_ge(thT_ps, n)
                nc.scalar.activation(th[i][:], acc[:, n, :], ACT.Tanh).then_inc(th_ready, 1)
                act.wait_ge(thT_ps, n + 1)
                act.wait_ge(y_ps, n)
                nc.scalar.activation(thT[i][:], banks[i][:, 0:D].rearrange("p (t n) -> p t n", t=2), ACT.Copy).then_inc(thT_ready, 1)

    @block.tensor
    def _(pe):
        with pe.Fori(0, ST // WS) as j:
            for slot in range(WS):
                n, i = WS * j + slot, slot % 2
                hold(pe, th_ready, n + 1, passed)
                hold(pe, thT_ready, n, passed)
                for t in range(2):
                    last = nc.tensor.transpose(banks[i][:, 128 * t:128 * t + 128], th[i][:, 128 * t:128 * t + 128], ident[:])
                last.then_inc(thT_ps, 1)
                hold(pe, thT_ready, n + 1, passed)
                hold(pe, w_loaded[slot], 64 * (j + 1), passed)
                hold(pe, y_sb, WS * j + max(0, slot - 1), passed)
                for e in range(4):
                    for t in range(2):
                        last = nc.tensor.matmul(banks[2 + i][32 * e:32 * e + 32, 0:D], thT[i][:, t, 32 * e:32 * e + 32], we[slot][:, e, t, :], start=t == 0, stop=t == 1)
                last.then_inc(y_ps, 1)


def combine(nc, a, scratch, m, answers, banks):
    cT = [m.sb(f"ccT{i}", [128, ST, N]) for i in range(2)]
    h = [m.sb(f"ch{i}", [N, D]) for i in range(2)]
    o = [m.sb(f"co{i}", [N, D]) for i in range(2)]
    loaded, stored = [m.sem("c_loaded0"), m.sem("c_loaded1")], [m.sem("c_stored0"), m.sem("c_stored1")]
    summed, added, passed = [m.sem("c_summed0"), m.sem("c_summed1")], [m.sem("c_added0"), m.sem("c_added1")], m.sem("c_passed")
    block = m.ctx.enter_context(nc.Block())

    @block.sync
    def _(sp):
        with sp.Fori(0, B // 2) as j:
            for i in range(2):
                b = 2 * j + i
                hold(sp, summed[i], j, passed)
                sp.dma_start(cT[i][:].rearrange("p s n -> p (s n)"), scratch.cT[b]).then_inc(loaded[i], 16)
                hold(sp, added[i], j, passed)
                sp.dma_start(h[i][:], scratch.h[b]).then_inc(loaded[i], 16)

    @block.tensor
    def _(pe):
        with pe.Fori(0, B // 2) as j:
            for i in range(2):
                hold(pe, loaded[i], 32 * (j + 1), passed)
                hold(pe, added[i], j, passed)
                for s in range(ST):
                    last = nc.tensor.matmul(banks[i][0:N, 0:D], cT[i][:, s, :], answers[:, s, :], start=s == 0, stop=s == ST - 1)
                last.then_inc(summed[i], 1)

    @block.vector
    def _(dve):
        with dve.Fori(0, B // 2) as j:
            for i in range(2):
                dve.wait_ge(summed[i], j + 1)
                dve.wait_ge(loaded[i], 32 * (j + 1))
                dve.wait_ge(stored[i], 16 * j)
                nc.vector.tensor_tensor(o[i][:], banks[i][0:N, 0:D], h[i][:], ALU.add).then_inc(added[i], 1)

    @block.scalar
    def _(act):
        with act.Fori(0, B // 2) as j:
            for i in range(2):
                hold(act, added[i], j + 1, passed)
                act.dma_start(a.out[2 * j + i], o[i][:]).then_inc(stored[i], 16)
        for i in range(2):
            act.wait_ge(stored[i], 16 * (B // 2))


class _Arrays:
    pass


def build(nc, arrays):
    scratch = _Arrays()
    scratch.z = nc.dram_tensor("scratch_z", (B, 1 + NPOS, D), F32, kind="Internal").ap()
    scratch.v = nc.dram_tensor("scratch_v", (B + 1, 2, NT, D // 2), F32, kind="Internal").ap()
    scratch.gate = nc.dram_tensor("scratch_gate", (B + 1, NT, D), F32, kind="Internal").ap()
    scratch.slab = nc.dram_tensor("scratch_slab", (NC, 128, B + 1, SLAB), F32, kind="Internal").ap()
    scratch.o = nc.dram_tensor("scratch_o", (B, 2, NT, D // 2), F32, kind="Internal").ap()
    scratch.h = nc.dram_tensor("scratch_h", (B, N, D), F32, kind="Internal").ap()
    scratch.cT = nc.dram_tensor("scratch_cT", (B, 128, ST * N), F32, kind="Internal").ap()
    for part in (tokenizer, attention, mixture):
        part(nc, arrays, scratch)


def lay_out(inputs):
    import numpy as np
    x = {n: np.ascontiguousarray(v) for n, v in inputs.items()}
    p = x["x"].reshape(B, 3, GRID, 16, GRID, 16).transpose(2, 4, 0, 3, 5, 1).reshape(B * NPOS // 128, 128, PD)
    level = np.zeros((LV, V, 2 * T), np.int32)
    for l in range(LV):
        up = [(t, kind) for t in range(T) for kind in range(3)
              if ((kind > 0) if l == 0 else (2 * t) >> l & 1)]
        for at, (t, kind) in enumerate(up):
            q = 2 * t + min(kind, 1)
            for key in range(V):
                level[l, key, at] = key < q and key >> l != q >> l and key >> (l + 1) == q >> (l + 1)
                if kind == 2 and l == 0 and key == q:
                    level[l, key, at] = 1
    return {
        "patches": p,
        "txt": x["txt"],
        "ln1_g": x["L0_tok_ln1_g"].reshape(6, 128).T, "ln1_b": x["L0_tok_ln1_b"].reshape(6, 128).T,
        "W_proj": x["L0_tok_W_proj"], "b_proj": x["L0_tok_b_proj"],
        "ln2_g": x["L0_tok_ln2_g"], "ln2_b": x["L0_tok_ln2_b"],
        "cls_token": x["L0_tok_cls_token"].reshape(D), "pos_emb": x["L0_tok_pos_emb"][0],
        "Wq": x["L0_attn_Wq"], "Wk": x["L0_attn_Wk"], "Wv": x["L0_attn_Wv"],
        "Wf1": x["L0_attn_Wf1"], "Wf2": x["L0_attn_Wf2"], "Wbeta": x["L0_attn_Wbeta"],
        "Wog1": x["L0_attn_Wog1"], "Wog2": x["L0_attn_Wog2"],
        "norm_w": x["L0_attn_norm_w"].reshape(2, 128).T, "Wo": x["L0_attn_Wo"],
        "phi_wT": x["L0_ffn_phi_w"].T, "phi_b": x["L0_ffn_phi_b"],
        "expert_w": x["L0_ffn_expert_w"], "expert_b": x["L0_ffn_expert_b"],
        "ident": np.eye(128, dtype=np.float32),
        "head_ones": np.kron(np.eye(4, dtype=np.float32), np.ones((HD, HD), np.float32)),
        "levels": np.tile(level.transpose(1, 0, 2), (4, 1, 1)).reshape(128, LV * 2 * T),
        "in_chunk": np.tile((np.arange(NC * 2 * V) % V > 0).astype(np.float32), (128, 1)),
    }


def kernel(**inputs):
    import numpy as np
    import concourse.bacc as bacc
    from concourse.bass_utils import run_bass_kernel_spmd

    nc = bacc.Bacc("TRN2", target_bir_lowering=False, num_devices=1)
    data = {name: np.ascontiguousarray(v) for name, v in lay_out(inputs).items()}
    arrays = _Arrays()
    for name, v in data.items():
        arrays.__dict__[name] = nc.dram_tensor(f"in_{name}", v.shape, mybir.dt.from_np(v.dtype), kind="ExternalInput").ap()
    arrays.out = nc.dram_tensor("out", (B, N, D), F32, kind="ExternalOutput").ap()
    build(nc, arrays)
    result = run_bass_kernel_spmd(nc, [{f"in_{name}": v for name, v in data.items()}], core_ids=[0])
    return result.results[0]["out"]
```

```python
import concourse.bass as bass
from concourse import mybir
from contextlib import ExitStack

F32 = mybir.dt.float32
BF16 = mybir.dt.bfloat16
I32 = mybir.dt.int32
ALU = mybir.AluOpType
ACT = mybir.ActivationFunctionType
AX = mybir.AxisListType

B, NTXT, D = 32, 77, 256
GRID, NPOS = 6, 36
PD = 768
N = 1 + NPOS + NTXT
H, HD = 8, 32
T = 16
NC = 8
NT = NC * T
LAST = N - (NC - 1) * T
V = 2 * T
GB = 8
NG = B // GB
LV = 5
W = V + T
NEXP, PS = 64, 32
NS = NEXP * PS
ST = NS // 128
WS = 4
LN_EPS, QK_EPS = 1e-5, 1e-6
UP = [2 * T] + [W // 2] * (LV - 1)
KIN, KOUT, Q_E, A_T = 0, 2 * V, 4 * V, 4 * V + 2 * T
SLAB = 4 * V + 4 * T
LN_EXP, SILU = "natural_log_exp_and_others", "silu_and_others"


class Steps:

    def __init__(self, engine, sem):
        self.engine, self.sem, self.n = engine, sem, 0

    def mark(self, ins):
        self.n += 1
        ins.then_inc(self.sem, 1)
        return self.n

    def wait(self, n=None):
        self.engine.wait_ge(self.sem, self.n if n is None else n)

    def link(self, ins):
        self.mark(ins)
        self.wait()

    def restart(self):
        self.wait()
        self.engine.sem_clear(self.sem)
        self.n = 0


class Memory:
    def __init__(self, nc, ctx):
        self.nc, self.ctx = nc, ctx

    def sb(self, name, shape, dt=F32):
        return self.ctx.enter_context(self.nc.sbuf_tensor(name, shape, dt))

    def ps(self, name, shape=(128, 512), dt=F32):
        return self.ctx.enter_context(self.nc.psum_tensor(name, list(shape), dt))

    def sem(self, name):
        return self.ctx.enter_context(self.nc.semaphore(name))


def hold(engine, sem, value, passed):
    engine.wait_ge(sem, value)
    engine.sem_inc(passed, 1)


def from_one(engine, *sems):
    for sem in sems:
        engine.sem_inc(sem, 1)


def inverse_root(nc, steps, out, x, eps):
    steps.link(nc.scalar.activation(out, x, ACT.Ln, bias=eps))
    return nc.scalar.activation(out, out, ACT.Exp, scale=-0.5)


def tokenizer(nc, a, scratch):
    TILES = B * NPOS // 128
    KT = PD // 128
    with ExitStack() as ctx:
        m = Memory(nc, ctx)

        def two(kind, name, *shape):
            return [kind(f"{name}{p}", *shape) for p in range(2)]

        wp = m.sb("wp", [128, KT, D])
        g1, b1 = m.sb("g1", [128, KT]), m.sb("b1", [128, KT])
        bproj, g2, b2 = m.sb("bproj", [128, D]), m.sb("g2", [128, D]), m.sb("b2", [128, D])
        pos = m.sb("pos", [128, TILES, D])
        cls, pos0 = m.sb("cls", [32, D]), m.sb("pos0", [32, D])
        ident = m.sb("ident_tok", [128, 128])
        patch, xn, xnT = two(m.sb, "patch", [128, PD]), two(m.sb, "tok_xn", [128, PD]), two(m.sb, "tok_xnT", [128, KT, 128])
        stats, mv, rstd = two(m.sb, "tok_stats", [128, 12]), two(m.sb, "tok_mv", [128, 2]), two(m.sb, "tok_rstd", [128, 1])
        stats2, mv2, rstd2 = m.sb("tok_stats2", [128, 6]), m.sb("tok_mv2", [128, 2]), m.sb("tok_rstd2", [128, 1])
        z, zo = two(m.sb, "tok_z", [128, D]), two(m.sb, "tok_zo", [128, D])
        pT = [two(m.ps, f"pT{p}") for p in range(2)]
        pZ = two(m.ps, "pZ")
        weights, offsets, dve_steps, act_steps, passed = (m.sem(n) for n in ("tok_weights", "tok_offsets", "tok_dve_steps", "tok_act_steps", "tok_passed"))
        loaded, moments, rstds, normed, transposed, evacuated, projected, z_ready, stored = (
            two(m.sem, n) for n in ("tok_loaded", "tok_moments", "tok_rstds", "tok_normed", "tok_transposed", "tok_evacuated", "tok_projected", "z_ready", "tok_stored"))
        moments2, rstds2, cls_ready, cls_stored = (m.sem(n) for n in ("tok_moments2", "tok_rstds2", "cls_ready", "cls_stored"))
        block = ctx.enter_context(nc.Block())

        def tiles(engine, step):
            with engine.Fori(0, (TILES - 3) // 2) as q:
                for p in range(2):
                    step(2 * q + p, p, q, 3)
            for j in range(TILES - 3, TILES):
                step(j, j % 2, j // 2, TILES - 1 - j)

        @block.sync
        def _(sp):
            from_one(sp, stored[0], stored[1])
            def load(j, p, k):
                hold(sp, normed[p], k, passed)
                sp.dma_start(patch[p][:], a.patches[j]).then_inc(loaded[p], 16)

            load(0, 0, 0)
            sp.dma_start(ident[:], a.ident).then_inc(weights, 16)
            sp.dma_start(g1[:], a.ln1_g).then_inc(weights, 16)
            sp.dma_start(b1[:], a.ln1_b).then_inc(weights, 16)
            sp.dma_start(wp[:], a.W_proj.rearrange("(k p) e -> p k e", p=128)).then_inc(weights, 16)
            load(1, 1, 0)
            sp.dma_start(bproj[:], a.b_proj.partition_broadcast(128)).then_inc(offsets, 16)
            sp.dma_start(g2[:], a.ln2_g.partition_broadcast(128)).then_inc(offsets, 16)
            sp.dma_start(b2[:], a.ln2_b.partition_broadcast(128)).then_inc(offsets, 16)
            by_tile = a.pos_emb[1:1 + NPOS].rearrange("(j q) e -> q j e", q=4)
            for q in range(4):
                sp.dma_start(pos[32 * q:32 * q + 32], by_tile[q].partition_broadcast(32)).then_inc(offsets, 16)
            load(2, 0, 1)
            sp.dma_start(cls[:], a.cls_token.partition_broadcast(32)).then_inc(offsets, 16)
            sp.dma_start(pos0[:], a.pos_emb[0].partition_broadcast(32)).then_inc(offsets, 16)

            def step(j, p, k, more):
                if more > 2:
                    load(j + 3, 1 - p, k + p + 1)
                hold(sp, z_ready[p], 1 + k + 1, passed)
                for q in range(4):
                    sp.dma_start(scratch.z[:, 1 + 4 * j + q, :], zo[p][32 * q:32 * q + 32]).then_inc(stored[p], 16)

            tiles(sp, step)
            sp.wait_ge(cls_ready, 1)
            sp.dma_start(scratch.z[:, 0, :], cls[:]).then_inc(cls_stored, 16)
            sp.wait_ge(cls_stored, 16)
            for p in range(2):
                sp.wait_ge(stored[p], 1 + 64 * ((TILES + 1 - p) // 2))

        @block.vector
        def _(dve):
            from_one(dve, z_ready[0], z_ready[1])
            steps = Steps(dve, dve_steps)

            def patches(p, k):
                dve.wait_ge(loaded[p], 16 * (k + 1))
                for i in range(2):
                    steps.mark(nc.vector.bn_stats(stats[p][:, 6 * i:6 * i + 6], patch[p][:, 384 * i:384 * i + 384]))
                steps.wait()
                nc.vector.bn_aggr(mv[p][:], stats[p][:]).then_inc(moments[p], 1)
                dve.wait_ge(rstds[p], k + 1)
                dve.wait_ge(transposed[p], k)
                nc.vector.tensor_scalar(xn[p][:], patch[p][:], mv[p][:, 0:1], rstd[p][:], ALU.subtract, ALU.mult).then_inc(normed[p], 1)

            patches(0, 0)
            patches(1, 0)
            dve.wait_ge(offsets, 16 * 9)
            nc.vector.tensor_tensor(cls[:], cls[:], pos0[:], ALU.add).then_inc(cls_ready, 1)
            steps.link(nc.vector.tensor_tensor(pos[:], pos[:], b2[:].unsqueeze(1).to_broadcast([128, TILES, D]), ALU.add))

            steps.restart()

            def step(j, p, k, more):
                if more > 1:
                    patches(p, k + 1)
                dve.wait_ge(projected[p], 1 + k + 1)
                steps.link(nc.vector.tensor_tensor(z[p][:], pZ[p][:, 0:D], bproj[:], ALU.add))
                steps.link(nc.vector.bn_stats(stats2[:], z[p][:]))
                nc.vector.bn_aggr(mv2[:], stats2[:]).then_inc(moments2, 1)
                dve.wait_ge(rstds2, j + 1)
                steps.link(nc.vector.tensor_scalar(z[p][:], z[p][:], mv2[:, 0:1], rstd2[:], ALU.subtract, ALU.mult))
                steps.link(nc.vector.tensor_tensor(z[p][:], z[p][:], g2[:], ALU.mult))
                dve.wait_ge(stored[p], 1 + 64 * k)
                nc.vector.tensor_tensor(zo[p][:], z[p][:], pos[:, j, :], ALU.add).then_inc(z_ready[p], 1)
                steps.restart()

            tiles(dve, step)

        @block.tensor
        def _(pe):
            from_one(pe, projected[0], projected[1])
            def transposes(p, k):
                hold(pe, normed[p], k + 1, passed)
                hold(pe, evacuated[p], 1 + k, passed)
                for t in range(KT):
                    last = nc.tensor.transpose(pT[p][t // 4][:, 128 * (t % 4):128 * (t % 4) + 128], xn[p][:, 128 * t:128 * t + 128], ident[:])
                last.then_inc(transposed[p], 1)

            def step(j, p, k, more):
                if more:
                    transposes(1 - p, k + p)
                hold(pe, evacuated[p], 1 + k + 1, passed)
                hold(pe, z_ready[p], 1 + k, passed)
                for t in range(KT):
                    last = nc.tensor.matmul(pZ[p][:, 0:D], xnT[p][:, t, :], wp[:, t, :], start=t == 0, stop=t == KT - 1)
                last.then_inc(projected[p], 1)

            pe.wait_ge(weights, 16 * 4)
            transposes(0, 0)
            tiles(pe, step)

        @block.scalar
        def _(act):
            from_one(act, evacuated[0], evacuated[1])
            steps = Steps(act, act_steps)

            def root(p, k):
                act.wait_ge(moments[p], k + 1)
                inverse_root(nc, steps, rstd[p][:], mv[p][:, 1:2], LN_EPS).then_inc(rstds[p], 1)

            def evacuate(p, k):
                act.wait_ge(transposed[p], k + 1)
                act.wait_ge(projected[p], 1 + k)
                for t in range(KT):
                    last = nc.scalar.activation(xnT[p][:, t, :], pT[p][t // 4][:, 128 * (t % 4):128 * (t % 4) + 128],
                                                ACT.Identity, bias=b1[:, t:t + 1], scale=g1[:, t:t + 1])
                last.then_inc(evacuated[p], 1)

            def step(j, p, k, more):
                if more > 1:
                    root(p, k + 1)
                if more:
                    evacuate(1 - p, k + p)
                act.wait_ge(moments2, j + 1)
                inverse_root(nc, steps, rstd2[:], mv2[:, 1:2], LN_EPS).then_inc(rstds2, 1)
                steps.restart()

            nc.scalar.preload_act_table_set(LN_EXP)
            root(0, 0)
            root(1, 0)
            steps.restart()
            act.wait_ge(weights, 16 * 4)
            evacuate(0, 0)
            tiles(act, step)


def attention(nc, a, scratch):
    with ExitStack() as ctx:
        m = Memory(nc, ctx)
        wq, wk, wv = m.sb("wq", [128, 2, D]), m.sb("wk", [128, 2, D]), m.sb("wv", [128, 2, D])
        wfg = m.sb("wfg", [128, 2, 2 * HD])
        wf2, wog2 = m.sb("wf2", [HD, D]), m.sb("wog2", [HD, D])
        wb8, wb = m.sb("wb8", [128, 2, H]), m.sb("wb", [128, 2, D])
        ident, head_ones = m.sb("ident_att", [128, 128]), m.sb("head_ones", [128, 128])
        levels = m.sb("levels", [128, LV, 2 * T], I32)
        in_chunk = m.sb("in_chunk", [128, 2 * NC * V])
        hx = m.sb("hx", [128, D])
        stats, mv, rstd = m.sb("stats", [128, 6]), m.sb("mv", [128, 2]), m.sb("rstd", [128, 1])
        xn, xT = m.sb("xn", [128, D]), m.sb("xT", [128, 2, NT])
        fg = m.sb("fg", [HD, 2, NT])
        q, kraw, k2, k = m.sb("q", [128, D]), m.sb("kraw", [128, D]), m.sb("k2", [128, D]), m.sb("k", [128, D])
        kr, vt, gate = m.sb("kr", [128, D]), m.sb("vt", [128, D]), m.sb("gate", [128, D])
        tanh_beta, tanh_gate = m.sb("tanh_beta", [128, D]), m.sb("tanh_gate", [128, D])
        nbeta, nbk = m.sb("nbeta", [128, D]), m.sb("nbk", [128, D])
        fabs, flog = m.sb("fabs", [128, D]), m.sb("flog", [128, D])
        decay = m.sb("decay", [128, 2 * NC * V])
        L = m.sb("L", [128, 2 * NC * V])
        fac, facin = m.sb("fac", [128, LV + 1, 2 * NC * V]), m.sb("facin", [128, 2 * NC * V])
        diff = fac
        lower = m.sb("lower", [128, LV, 2 * NC, V])
        above = [m.sb(f"above{l}", [128, 2 * NC * UP[l]]) for l in range(LV)]
        kout, koutT = m.sb("kout", [128, 2 * NC * V]), m.sb("koutT", [128, 2 * NC * V])
        PA = m.sb("PA", [128, 2, NC, W])
        kiq, at = m.sb("kiq", [128, NC, A_T]), m.sb("at", [128, NC, SLAB - A_T])
        Pb = m.sb("Pb", [128, V, 128])
        LP = Pb
        X = m.sb("X", [128, V, 128])
        XT = m.sb("XT", [128, NC, 2 * GB * V])
        tmp = m.sb("tmp", [128, 4 * (V - 1) ** 2])
        eg = m.sb("eg", [128, NC, 2 * (B + 1)])
        stage = [m.sb(f"stage{i}", [128, GB, SLAB]) for i in range(2)]
        xst = [m.sb(f"xst{i}", [128, 2 * GB * V]) for i in range(2)]
        vst = [m.sb(f"vst{i}", [128, 512]) for i in range(2)]
        S = [m.sb(f"S{i}", [128, 512]) for i in range(2)]
        tS, R, U, O = m.sb("tS", [128, 512]), m.sb("R", [128, 512]), m.sb("U", [128, 512]), m.sb("O", [128, 512])
        bank = [m.ps(f"bank{i}") for i in range(8)]
        b_x, b_qk, b_vb, b_fg = bank[4:8]
        ring = bank[0:4]

        consts, wb_ready, zeroed, unit_diagonal = m.sem("consts"), m.sem("wb_ready"), m.sem("zeroed"), m.sem("unit_diagonal")
        loaded, moments, rstds, normed = m.sem("loaded"), m.sem("moments"), m.sem("rstds"), m.sem("normed")
        pe_x, x_ready, pe_fg, fg_ready = m.sem("pe_x"), m.sem("x_ready"), m.sem("pe_fg"), m.sem("fg_ready")
        pe_proj, pe_qk, pe_f, act_proj, k2_ready, pe_ss = m.sem("pe_proj"), m.sem("pe_qk"), m.sem("pe_f"), m.sem("act_proj"), m.sem("k2_ready"), m.sem("pe_ss")
        k_ready, kr_ready, flog_ready = m.sem("k_ready"), m.sem("kr_ready"), m.sem("flog_ready")
        diff_ready, fac_ready, kq_ready = m.sem("diff_ready"), m.sem("fac_ready"), m.sem("kq_ready")
        scores, taken = m.sem("scores"), m.sem("taken")
        v_out, gate_out, kiq_out, at_out = m.sem("v_out"), m.sem("gate_out"), m.sem("kiq_out"), m.sem("at_out")
        gate_ready, nb_ready, pool_done = m.sem("gate_ready"), m.sem("nb_ready"), m.sem("pool_done")
        pa_ready, at_copied, kout_ready, kout_copied = m.sem("pa_ready"), m.sem("at_copied"), m.sem("kout_ready"), m.sem("kout_copied")
        lane_ps, lane_sb, inverted = m.sem("lane_ps"), m.sem("lane_sb"), m.sem("inverted")
        xt_ps, xt_sb = m.sem("xt_ps"), m.sem("xt_sb")
        staged, v_staged = [m.sem("staged0"), m.sem("staged1")], [m.sem("v_staged0"), m.sem("v_staged1")]
        R_ps, R_sb, U_ps, U_sb = m.sem("R_ps"), m.sem("R_sb"), m.sem("U_ps"), m.sem("U_sb")
        S_ps, S_sb, O_ps, O_sb, o_out = m.sem("S_ps"), m.sem("S_sb"), m.sem("O_ps"), m.sem("O_sb"), m.sem("o_out")
        tS_ready, R_copied, S_copied = m.sem("tS_ready"), m.sem("R_copied"), m.sem("S_copied")
        act_steps, dve_steps, pool_steps, passed = m.sem("act_steps"), m.sem("dve_steps"), m.sem("pool_steps"), m.sem("passed")
        block = ctx.enter_context(nc.Block())

        def chunks(x):
            return x.rearrange("p (g c w) -> p g c w", g=2, c=NC)

        def tokens(x):
            return x.rearrange("p (n t) -> p n t", t=T)

        def upper(x, l):
            if l == 0:
                return x.rearrange("p c (t k) -> p c t k", k=3)[:, :, :, 1:]
            return x.rearrange("p c (s u k) -> p c s u k", u=2, k=3 << (l - 1))[:, :, :, 1]

        def chunks_at(l):
            return NC if 1 << l < 2 * LAST else NC - 1

        def fronts(g):
            return GB * (g + 1) + 1

        def groups(first, project, invert, finish, sweep):
            first()
            project(0)
            invert(0)
            finish(0)
            with block_engine[0].Fori(0, NG - 1) as g:
                project(g + 1)
                invert(g + 1)
                sweep(g)
                finish(g + 1)
            sweep(NG - 1)

        block_engine = [None]

        @block.sync
        def _(sp):
            from_one(sp, at_out, o_out)
            block_engine[0] = sp
            def load(y, at_batch):
                if not (isinstance(y, int) and y == 0):
                    hold(sp, normed, y, passed)
                sp.dma_start(hx[0:1 + NPOS], scratch.z[at_batch]).then_inc(loaded, 16)
                sp.dma_start(hx[1 + NPOS:N], a.txt[at_batch]).then_inc(loaded, 16)

            load(0, 0)
            for dst, src in ((wq, a.Wq), (wk, a.Wk), (wv, a.Wv), (wb8, a.Wbeta)):
                sp.dma_start(dst[:], src.rearrange("(t p) n -> p t n", p=128)).then_inc(consts, 16)
            sp.dma_start(wfg[:, :, 0:HD], a.Wf1.rearrange("(t p) n -> p t n", p=128)).then_inc(consts, 16)
            sp.dma_start(wfg[:, :, HD:], a.Wog1.rearrange("(t p) n -> p t n", p=128)).then_inc(consts, 16)
            sp.dma_start(wf2[:], a.Wf2).then_inc(consts, 16)
            sp.dma_start(wog2[:], a.Wog2).then_inc(consts, 16)
            sp.dma_start(ident[:], a.ident).then_inc(consts, 16)
            sp.dma_start(head_ones[:], a.head_ones).then_inc(consts, 16)
            sp.dma_start(levels[:], a.levels.rearrange("p (l w) -> p l w", l=LV)).then_inc(consts, 16)
            sp.dma_start(in_chunk[:], a.in_chunk).then_inc(consts, 16)
            load(1, 1)
            load(2, 2)

            def store_front(x, load_next=lambda: None):
                hold(sp, gate_ready, x + 1, passed)
                hold(sp, act_proj, 3 * x + 3, passed)
                sp.dma_start(scratch.v[x].rearrange("g t w -> t g w"), vt[:].rearrange("p (g w) -> p g w", g=2)).then_inc(v_out, 16)
                sp.dma_start(scratch.gate[x], gate[:]).then_inc(gate_out, 16)
                load_next()
                hold(sp, pool_done, 5 * (x + 1), passed)
                hold(sp, kout_copied, x + 1, passed)
                sp.dma_start(scratch.slab[:, :, x, 0:A_T].rearrange("c p w -> p c w"), kiq[:]).then_inc(kiq_out, 16)

            def first():
                store_front(0)
                sp.wait_ge(zeroed, 6)

            def project(g):
                if not isinstance(g, int):
                    preload(g - 1)
                with sp.Fori(0, GB // 2) as b2:
                    for b in (b2 * 2, b2 * 2 + 1):
                        it = g * GB + b
                        store_front(it + 1, lambda: load(it + 3, (it + 3) % B))
                        hold(sp, at_copied, 1 + it + 1, passed)
                        sp.dma_start(scratch.slab[:, :, it, A_T:].rearrange("c p w -> p c w"), at[:]).then_inc(at_out, 16)

            values = scratch.v.rearrange("b g (c t) (h w) -> h c t (b g) w", c=NC, h=4)
            outs = scratch.o.rearrange("b g (c t) (h w) -> h c t (b g) w", c=NC, h=4)

            def load_chunk(g, c, i):
                sp.dma_start(stage[i][:], scratch.slab[c, :, bass.ds(g * GB, GB), :]).then_inc(staged[i], 16)
                sp.dma_start(xst[i][:], XT[:, c, :]).then_inc(staged[i], 16)
                for h in range(4):
                    sp.dma_start(vst[i][32 * h + 1:32 * h + 32:2].rearrange("p (y w) -> p y w", y=2 * GB),
                                 values[h, c, :, bass.ds(g * (2 * GB), 2 * GB), :]).then_inc(v_staged[i], 16)

            def preload(g):
                hold(sp, v_out, 16 * fronts(g), passed)
                hold(sp, kiq_out, 16 * fronts(g), passed)
                hold(sp, at_out, 1 + 16 * GB * (g + 1), passed)
                hold(sp, xt_sb, 8 * (g + 1), passed)
                hold(sp, O_ps, 2 * NC * g + 2, passed)
                load_chunk(g, 0, 0)
                load_chunk(g, 1, 1)

            def store_chunk(g, c):
                hold(sp, O_sb, 1 + 2 * (g * NC + c) + 2, passed)
                for h in range(4):
                    sp.dma_start(outs[h, c, :, bass.ds(g * (2 * GB), 2 * GB), :],
                                 O[32 * h:32 * h + T].rearrange("p (y w) -> p y w", y=2 * GB)).then_inc(o_out, 16)

            def sweep(g):
                if isinstance(g, int):
                    preload(g)
                with sp.Fori(0, NC // 2 - 1) as c2:
                    for i in range(2):
                        c = c2 * 2 + i
                        store_chunk(g, c)
                        hold(sp, O_ps, 2 * (g * NC + c) + 4, passed)
                        load_chunk(g, c + 2, i)
                store_chunk(g, NC - 2)
                store_chunk(g, NC - 1)

            groups(first, project, lambda g: None, lambda g: None, sweep)
            sp.wait_ge(o_out, 1 + 64 * NG * NC)
            sp.wait_ge(loaded, 32 * (B + 3))
            sp.wait_ge(gate_out, 16 * (B + 1))
            sp.wait_ge(v_out, 16 * (B + 1))
            sp.wait_ge(kiq_out, 16 * (B + 1))
            sp.wait_ge(at_out, 1 + 16 * B)

        @block.tensor
        def _(pe):
            from_one(pe, U_ps)
            block_engine[0] = pe

            def wait(sem, value):
                if not (isinstance(value, int) and value <= 0):
                    hold(pe, sem, value, passed)

            pe.wait_ge(consts, 16 * 12)
            pe.wait_ge(wb_ready, 1)
            pe.wait_ge(zeroed, 6)
            pe.sem_inc(O_ps, 2)

            def transposes(y):
                wait(normed, y + 1)
                for t in range(2):
                    last = nc.tensor.transpose(b_x[:, 128 * t:128 * t + N], xn[0:N, 128 * t:128 * t + 128], ident[0:N, 0:N])
                last.then_inc(pe_x, 1)

            def project_qk(x):
                wait(x_ready, x + 1)
                for j in range(2):
                    for t in range(2):
                        last = nc.tensor.matmul(b_x[0:HD, 256 + 128 * j:384 + 128 * j], wfg[:, t, HD * j:HD * j + HD], xT[:, t, :], start=t == 0, stop=t == 1)
                last.then_inc(pe_fg, 1)
                for w, at_col in ((wk, D), (wq, 0)):
                    for hg in range(2):
                        for t in range(2):
                            last = nc.tensor.matmul(b_qk[:, at_col + 128 * hg:at_col + 128 * hg + 128], w[:, t, 128 * hg:128 * hg + 128], xT[:, t, :], start=t == 0, stop=t == 1)
                last.then_inc(pe_qk, 1)
                factors_out(x)

            def factors_out(x):
                wait(fg_ready, x + 1)
                for hg in range(2):
                    nc.tensor.matmul(b_fg[:, 128 * hg:128 * hg + 128], wf2[:, 128 * hg:128 * hg + 128], fg[:, 0, :], start=True, stop=True)
                nc.tensor.matmul(b_fg[:, D:], fg[:, 1, :], wog2[:], start=True, stop=True).then_inc(pe_f, 1)

            def project_rest(x):
                for t in range(2):
                    nc.tensor.matmul(b_vb[:, 0:D], xT[:, t, :], wv[:, t, :], start=t == 0, stop=t == 1)
                for hg in range(2):
                    for t in range(2):
                        last = nc.tensor.matmul(b_vb[:, D + 128 * hg:D + 128 * hg + 128], wb[:, t, 128 * hg:128 * hg + 128], xT[:, t, :], start=t == 0, stop=t == 1)
                last.then_inc(pe_proj, 1)

            def squares(x):
                wait(k2_ready, x + 1)
                nc.tensor.matmul(b_x[:, 0:D], head_ones[:], k2[:], start=True, stop=True).then_inc(pe_ss, 1)

            def score(it, n):
                l, hg = n // 2, n % 2
                if hg == 0:
                    wait(kq_ready, 3 * (LV * it + l + 1))
                if n == 0 or n > 3:
                    wait(taken, 1 + 2 * LV * it + max(0, n - 3))
                for c in range(chunks_at(l)):
                    for h in range(4):
                        r = slice(32 * h, 32 * h + 32)
                        last = nc.tensor.matmul(ring[n % 4][r, 32 * c:32 * c + UP[l]], lower[r, l, hg * NC + c, :], above[l][r, UP[l] * (hg * NC + c):UP[l] * (hg * NC + c) + UP[l]], start=True, stop=True)
                last.then_inc(scores, 1)

            def first():
                transposes(0)
                project_qk(0)
                project_rest(0)
                squares(0)
                transposes(1)

            def project(g):
                wait(O_sb, 1 + 2 * NC * (g - 1 if not isinstance(g, int) else 0))
                wait(S_sb, 1 + 18 * (g - 1 if not isinstance(g, int) else 0))
                wait(xt_sb, 8 * g)
                with pe.Fori(0, GB // 2) as b2:
                    for b in (b2 * 2, b2 * 2 + 1):
                        it = g * GB + b
                        project_qk(it + 1)
                        project_rest(it + 1)
                        score(it, 0)
                        score(it, 1)
                        squares(it + 1)
                        for n in range(2, 6):
                            score(it, n)
                        transposes(it + 2)
                        for n in range(6, 2 * LV):
                            score(it, n)
                wait(pa_ready, 2 * GB * (g + 1))
                wait(taken, 1 + 2 * LV * GB * (g + 1))
                for n in range(V // 4):
                    if n >= 4:
                        wait(lane_sb, 8 * g + n - 3)
                    for i in range(4):
                        last = nc.tensor.transpose(ring[n % 4][:, 128 * i:128 * i + 128], Pb[:, 4 * n + i, :], ident[:])
                    last.then_inc(lane_ps, 1)

            def finish(g):
                wait(inverted, g + 1)
                wait(lane_sb, 8 * (g + 1))
                wait(R_sb, 2 * NC * g)
                wait(U_sb, 2 * NC * g)
                for n in range(V // 4):
                    if n >= 4:
                        wait(xt_sb, 8 * g + n - 3)
                    for i in range(4):
                        last = nc.tensor.transpose(ring[n % 4][:, 128 * i:128 * i + 128], X[:, 4 * n + i, :], ident[:])
                    last.then_inc(xt_ps, 1)

            def sweep(g):
                wait(xt_sb, 8 * (g + 1))
                wait(lane_sb, 8 * (g + 2 if not isinstance(g, int) else NG))
                x1 = fronts(g + 1) if not isinstance(g, int) else fronts(g)
                wait(act_proj, 3 * x1)
                wait(flog_ready, x1)
                wait(kr_ready, x1)
                wait(x_ready, x1 + 1)
                with pe.Fori(0, NC // 2 - 1) as c2:
                    for i in range(2):
                        chunk(g, c2 * 2 + i, i, c2, V, T)
                chunk(g, NC - 2, 0, NC // 2 - 1, V, T)
                chunk(g, NC - 1, 1, NC // 2 - 1, 2 * LAST, LAST)
                pe.sem_inc(S_ps, 2)

            def chunk(g, c, i, uses, v, t):
                n = g * NC + c
                st = stage[i]

                def chain(p, h, at, w, rows, some):
                    return st[32 * h:32 * h + rows, p // 2, at + w * (p % 2):at + w * (p % 2) + some]

                wait(staged[i], 32 * (g * (NC // 2) + uses + 1))
                for half in range(2):
                    wait(S_sb, 1 + 18 * g + 2 * c + half + 1)
                    for p in range(8 * half, 8 * half + 8):
                        for h in range(4):
                            last = nc.tensor.matmul(bank[half][32 * h:32 * h + v, 32 * p:32 * p + 32], chain(p, h, KIN, V, 32, v), S[i][32 * h:32 * h + 32, 32 * p:32 * p + 32], start=True, stop=True)
                    last.then_inc(R_ps, 1)
                for half in range(2):
                    wait(R_sb, 2 * n + half + 1)
                    for p in range(8 * half, 8 * half + 8):
                        for h in range(4):
                            r = slice(32 * h, 32 * h + v)
                            last = nc.tensor.matmul(bank[2 + half][r, 32 * p:32 * p + 32], xst[i][r, 32 * p:32 * p + v], R[r, 32 * p:32 * p + 32], start=True, stop=True)
                    last.then_inc(U_ps, 1)
                for half in range(2):
                    wait(U_sb, 2 * n + half + 1)
                    if v < V:
                        continue
                    for p in range(8 * half, 8 * half + 8):
                        for h in range(4):
                            r = slice(32 * h, 32 * h + 32)
                            last = nc.tensor.matmul(bank[4 + half][r, 32 * p:32 * p + 32], chain(p, h, KOUT, V, V, 32), U[r, 32 * p:32 * p + 32], start=True, stop=True)
                    last.then_inc(S_ps, 1)
                wait(O_sb, 1 + 2 * n)
                for half in range(2):
                    for p in range(8 * half, 8 * half + 8):
                        for h in range(4):
                            o = bank[6 + half][32 * h:32 * h + t, 32 * p:32 * p + 32]
                            nc.tensor.matmul(o, chain(p, h, Q_E, T, 32, t), S[i][32 * h:32 * h + 32, 32 * p:32 * p + 32], start=True, stop=False)
                            last = nc.tensor.matmul(o, chain(p, h, A_T, T, v, t), U[32 * h:32 * h + v, 32 * p:32 * p + 32], start=False, stop=True)
                    last.then_inc(O_ps, 1)

            groups(first, project, lambda g: None, finish, sweep)

        @block.scalar
        def _(act):
            from_one(act, O_sb, at_copied)
            block_engine[0] = act
            steps = Steps(act, act_steps)

            def wait(sem, value):
                if not (isinstance(value, int) and value <= 0):
                    act.wait_ge(sem, value)

            def rows_root(y):
                wait(moments, y + 1)
                inverse_root(nc, steps, rstd[0:N], mv[0:N, 1:2], LN_EPS).then_inc(rstds, 1)

            def rows_copy(y):
                wait(pe_x, y + 1)
                wait(pe_proj, y)
                nc.scalar.activation(xT[:, :, 0:N], b_x[:, 0:256].rearrange("p (t n) -> p t n", t=2)[:, :, 0:N], ACT.Copy).then_inc(x_ready, 1)

            def front(x, y):
                wait(pe_fg, x + 1)
                wait(pe_f, x)
                nc.scalar.activation(fg[:], b_x[0:HD, 256:512].rearrange("p (t n) -> p t n", t=2), ACT.Copy).then_inc(fg_ready, 1)
                wait(pe_f, x + 1)
                wait(flog_ready, x)
                steps.link(nc.scalar.activation(fabs[:], b_fg[:, 0:D], ACT.Abs))
                steps.link(nc.scalar.activation(fabs[:], fabs[:], ACT.Exp, scale=-1.0))
                nc.scalar.activation(flog[:], fabs[:], ACT.Ln, bias=1.0).then_inc(act_proj, 1)
                nc.scalar.preload_act_table_set(SILU)
                wait(pe_qk, x + 1)
                wait(k_ready, x)
                wait(pe_ss, x)
                wait(kq_ready, 3 * LV * x)
                steps.link(nc.scalar.activation(kraw[:], b_qk[:, D:], ACT.Silu))
                nc.scalar.activation(k2[:], kraw[:], ACT.Square).then_inc(k2_ready, 1)
                wait(pool_done, 5 * x)
                steps.mark(nc.scalar.activation(q[:], b_qk[:, 0:D], ACT.Silu))
                wait(gate_ready, x)
                wait(flog_ready, x + 1)
                nc.scalar.activation(tanh_gate[:], b_fg[:, D:], ACT.Tanh, scale=0.5).then_inc(act_proj, 1)
                wait(pe_proj, x + 1)
                wait(v_out, 16 * x)
                steps.mark(nc.scalar.activation(vt[:], b_vb[:, 0:D], ACT.Silu))
                wait(nb_ready, x)
                steps.link(nc.scalar.activation(tanh_beta[:], b_vb[:, D:], ACT.Tanh, scale=0.5))
                act.sem_inc(act_proj, 1)
                nc.scalar.preload_act_table_set(LN_EXP)
                wait(pe_ss, x + 1)
                steps.link(nc.scalar.activation(kr[:], b_x[:, 0:D], ACT.Ln, bias=QK_EPS))
                nc.scalar.activation(kr[:], kr[:], ACT.Exp, scale=-0.5).then_inc(kr_ready, 1)
                rows_root(y)
                wait(diff_ready, x + 1)
                steps.mark(nc.scalar.activation(facin[:], L[:], ACT.Exp))
                nc.scalar.activation(fac[:], diff[:], ACT.Exp).then_inc(fac_ready, 1)

            def kout_section(x):
                wait(kout_ready, x + 1)
                wait(kiq_out, 16 * x)
                kt = chunks(koutT[:])
                nc.scalar.activation(kiq[:, :, KOUT:KOUT + 2 * V].rearrange("p c (g w) -> p g c w", g=2), kt, ACT.Copy).then_inc(kout_copied, 1)

            def first():
                nc.scalar.preload_act_table_set(LN_EXP)
                wait(zeroed, 6)
                rows_root(0)
                rows_copy(0)
                front(0, 1)
                rows_copy(1)
                kout_section(0)
                steps.restart()

            def project(g):
                with act.Fori(0, GB // 2) as b2:
                    for b in (b2 * 2, b2 * 2 + 1):
                        it = g * GB + b
                        front(it + 1, it + 2)
                        rows_copy(it + 2)
                        wait(at_out, 1 + 16 * it)
                        wait(pa_ready, 2 * it + 2)
                        nc.scalar.activation(at[:].rearrange("p c (g t) -> p g c t", g=2), PA[:].rearrange("p g c (t k) -> p g c t k", k=3)[:, :, :, :, 2], ACT.Copy).then_inc(at_copied, 1)
                        kout_section(it + 1)
                        steps.restart()
                for n in range(V // 4):
                    act.wait_ge(lane_ps, 8 * g + n + 1)
                    nc.scalar.activation(LP[:, 4 * n:4 * n + 4, :], ring[n % 4][:].rearrange("p (v x) -> p v x", v=4), ACT.Copy).then_inc(lane_sb, 1)

            def finish(g):
                for i in range(2):
                    wait(staged[i], 32 * (NC // 2) * g)
                for n in range(V // 4):
                    act.wait_ge(xt_ps, 8 * g + n + 1)
                    for i in range(4):
                        last = nc.scalar.activation(XT[:, :, 4 * n + i::V], ring[n % 4][:, 128 * i:128 * i + 128].rearrange("p (c x) -> p c x", c=NC), ACT.Copy)
                    last.then_inc(xt_sb, 1)

            def sweep(g):
                act.wait_ge(S_sb, 1 + 18 * g + 2)
                with act.Fori(0, NC // 2) as c2:
                    for i in range(2):
                        c = c2 * 2 + i
                        n = g * NC + c
                        parts = (slice(0, 256), slice(256, 512))
                        for half, cols in enumerate(parts):
                            act.wait_ge(R_ps, 2 * n + half + 1)
                            if half == 0:
                                act.wait_ge(U_ps, 1 + 2 * n)
                            nc.scalar.activation(R[:, cols], bank[half][:, cols], ACT.Copy).then_inc(R_copied, 1)
                        for half, cols in enumerate(parts):
                            act.wait_ge(U_ps, 1 + 2 * n + half + 1)
                            if half == 0:
                                act.wait_ge(O_ps, 2 * n + 2)
                            nc.scalar.activation(U[:, cols], bank[2 + half][:, cols], ACT.Copy).then_inc(U_sb, 1)
                        for half, cols in enumerate(parts):
                            act.wait_ge(S_ps, 2 * n + half + 1)
                            if half == 0:
                                act.wait_ge(tS_ready, 1 + n)
                            nc.scalar.activation(S[1 - i][:, cols], bank[4 + half][:, cols], ACT.Copy).then_inc(S_copied, 1)
                        for half, cols in enumerate(parts):
                            act.wait_ge(O_ps, 2 * n + half + 3)
                            if half == 0:
                                act.wait_ge(o_out, 1 + 64 * n)
                            nc.scalar.activation(O[:, cols], bank[6 + half][:, cols], ACT.Copy).then_inc(O_sb, 1)

            groups(first, project, lambda g: None, finish, sweep)

        @block.gpsimd
        def _(pool):
            from_one(pool, S_sb, tS_ready)
            block_engine[0] = pool

            def wait(sem, value):
                if not (isinstance(value, int) and value <= 0):
                    pool.wait_ge(sem, value)

            def front(x):
                wait(fac_ready, x + 1)
                wait(nb_ready, x + 1)
                wait(kiq_out, 16 * x)
                fin = chunks(facin[:])
                for hg in range(2):
                    kk = nbk[:, 128 * hg:128 * hg + 128].rearrange("p (c t) -> p c t", c=NC).unsqueeze(3).to_broadcast([128, NC, T, 2])
                    pool.tensor_tensor(kiq[:, :, KIN + V * hg:KIN + V * hg + V].rearrange("p c (t a) -> p c t a", a=2),
                                       fin[:, hg].rearrange("p c (t a) -> p c t a", a=2), kk, ALU.mult).then_inc(pool_done, 1)
                    pool.tensor_tensor(kiq[:, :, Q_E + T * hg:Q_E + T * hg + T], fin[:, hg, :, 1:V:2],
                                       q[:, 128 * hg:128 * hg + 128].rearrange("p (c t) -> p c t", c=NC), ALU.mult).then_inc(pool_done, 1)
                pool.tensor_copy(eg[:, :, bass.ds(2 * x, 2)], fin[:, :, :, V - 1].rearrange("p g c -> p c g")).then_inc(pool_done, 1)

            def project(g):
                with pool.Fori(0, GB // 2) as b2:
                    for b in (b2 * 2, b2 * 2 + 1):
                        front(g * GB + b + 1)

            def sweep(g):
                hold(pool, pool_done, 5 * (fronts(g + 1) if not isinstance(g, int) else fronts(g)), passed)
                hold(pool, S_sb, 1 + 18 * g, passed)
                nc.gpsimd.memset(S[0][:, 0:256], 0.0).then_inc(S_sb, 1)
                nc.gpsimd.memset(S[0][:, 256:512], 0.0).then_inc(S_sb, 1)
                with pool.Fori(0, NC // 2) as c2:
                    for i in range(2):
                        c = c2 * 2 + i
                        n = g * NC + c
                        pool.wait_ge(S_sb, 1 + 18 * g + 2 * c + 2)
                        pool.tensor_tensor(tS[:].rearrange("p (x w) -> p x w", w=HD), S[i][:].rearrange("p (x w) -> p x w", w=HD),
                                           eg[:, c, bass.ds(g * (2 * GB), 2 * GB)].unsqueeze(2).to_broadcast([128, 2 * GB, HD]), ALU.mult).then_inc(tS_ready, 1)
                        pool.wait_ge(v_staged[i], 64 * (g * (NC // 2) + c2 + 1))
                        for half in range(2):
                            cols = slice(256 * half, 256 * half + 256)
                            pool.wait_ge(R_copied, 2 * n + half + 1)
                            pool.tensor_tensor(R[:, cols], R[:, cols], vst[i][:, cols], ALU.add).then_inc(R_sb, 1)
                        pool.wait_ge(tS_ready, 1 + n + 1)
                        for half in range(2):
                            cols = slice(256 * half, 256 * half + 256)
                            pool.wait_ge(S_copied, 2 * n + half + 1)
                            pool.tensor_tensor(S[1 - i][:, cols], S[1 - i][:, cols], tS[:, cols], ALU.add).then_inc(S_sb, 1)

            for x in (xT, decay, lower, PA, vst[0], vst[1]):
                nc.gpsimd.memset(x[:], 0.0).then_inc(zeroed, 1)
            nc.gpsimd.memset(X[:], 0.0).then_inc(pool_steps, 1)
            pool.wait_ge(pool_steps, 1)
            for v in range(V):
                nc.gpsimd.memset(X[:, v, v:128:V], 1.0).then_inc(unit_diagonal, 1)
            groups(lambda: front(0), project, lambda g: None, lambda g: None, sweep)

        @block.vector
        def _(dve):
            from_one(dve, taken)
            block_engine[0] = dve
            steps = Steps(dve, dve_steps)

            def wait(sem, value):
                if not (isinstance(value, int) and value <= 0):
                    dve.wait_ge(sem, value)

            dve.wait_ge(consts, 16 * 12)
            nc.vector.tensor_copy(wb[:].rearrange("p t (h w) -> p t h w", h=H), wb8[:].unsqueeze(3).to_broadcast([128, 2, H, HD])).then_inc(wb_ready, 1)
            dve.wait_ge(zeroed, 6)

            def rows_stats(y):
                wait(rstds, y)
                wait(loaded, 32 * (y + 1))
                steps.link(nc.vector.bn_stats(stats[0:N], hx[0:N]))
                nc.vector.bn_aggr(mv[0:N], stats[0:N]).then_inc(moments, 1)

            def rows_norm(y):
                wait(rstds, y + 1)
                wait(pe_x, y)
                nc.vector.tensor_scalar(xn[0:N], hx[0:N], mv[0:N, 0:1], rstd[0:N], ALU.subtract, ALU.mult).then_inc(normed, 1)

            def decays(x):
                wait(act_proj, 3 * x + 1)
                wait(fac_ready, x)
                nc.vector.scalar_tensor_tensor(out=decay[:, 1::2], in0=b_fg[:, 0:D], scalar=0.0, in1=flog[:], op0=ALU.min, op1=ALU.subtract).then_inc(flog_ready, 1)
                wait(flog_ready, x + 1)
                steps.link(nc.vector.tensor_tensor_scan(L[:], in_chunk[:], decay[:], 0.0, ALU.mult, ALU.add))
                for l in range(LV):
                    w = 1 << l
                    s = L[:].rearrange("p (n s w) -> p n s w", s=2, w=w)
                    d = diff[:, l].rearrange("p (n s w) -> p n s w", s=2, w=w)
                    top = s[:, :, 1, 0:1].to_broadcast([128, 2 * NC * V // (2 * w), w])
                    steps.mark(nc.vector.tensor_tensor(d[:, :, 1], s[:, :, 1], top, ALU.subtract))
                    steps.mark(nc.vector.tensor_tensor(d[:, :, 0], top, s[:, :, 0], ALU.subtract))
                s = L[:].rearrange("p (n w) -> p n w", w=V)
                steps.mark(nc.vector.tensor_tensor(diff[:, LV].rearrange("p (n w) -> p n w", w=V), s[:, :, V - 1:V].to_broadcast([128, 2 * NC, V]), s, ALU.subtract))
                steps.wait()
                dve.sem_inc(diff_ready, 1)

            def gates(x):
                wait(act_proj, 3 * x + 2)
                wait(gate_out, 16 * x)
                nc.vector.tensor_scalar(gate[:], tanh_gate[:], 0.5, 0.5, ALU.mult, ALU.add).then_inc(gate_ready, 1)

            def keys(x):
                gates(x)
                wait(kr_ready, x + 1)
                nc.vector.tensor_tensor(k[:], kraw[:], kr[:], ALU.mult).then_inc(k_ready, 1)
                wait(k_ready, x + 1)
                wait(fac_ready, x + 1)

            def pairs_of_keys():
                return tokens(k[:]).unsqueeze(3).to_broadcast([128, 2 * NC, T, 2])

            def factors(x, l):
                wait(scores, 2 * LV * (x - 1) + 2 * l + 2 if not isinstance(x, int) else 0)
                if l == 0:
                    f, up = tokens(fac[:, 0, 1::2]), above[0][:].rearrange("p (n t k) -> p n t k", t=T, k=2)
                    nc.vector.tensor_tensor(lower[:, 0].rearrange("p n (t a) -> p n t a", a=2), fac[:, 0].rearrange("p (n t a) -> p n t a", t=T, a=2),
                                            pairs_of_keys(), ALU.mult).then_inc(kq_ready, 1)
                    nc.vector.tensor_tensor(up[:, :, :, 0], f, tokens(k[:]), ALU.mult).then_inc(kq_ready, 1)
                    nc.vector.tensor_tensor(up[:, :, :, 1], f, tokens(q[:]), ALU.mult).then_inc(kq_ready, 1)
                    return
                w = 1 << (l - 1)
                kb = k[:].rearrange("p (s u w) -> p s u w", u=2, w=w)
                qb = q[:].rearrange("p (s u w) -> p s u w", u=2, w=w)
                f = fac[:, l].rearrange("p (s u w a) -> p s u w a", u=2, w=w, a=2)
                low = lower[:, l].rearrange("p n v -> p (n v)").rearrange("p (s u w a) -> p s u w a", u=2, w=w, a=2)
                up = above[l][:].rearrange("p (s w k) -> p s w k", w=w, k=3)
                both = [128, D // (2 * w), w, 2]
                nc.vector.tensor_tensor(low[:, :, 0], f[:, :, 0], kb[:, :, 0].unsqueeze(3).to_broadcast(both), ALU.mult).then_inc(kq_ready, 1)
                nc.vector.tensor_tensor(up[:, :, :, 0:2], f[:, :, 1], kb[:, :, 1].unsqueeze(3).to_broadcast(both), ALU.mult).then_inc(kq_ready, 1)
                nc.vector.tensor_tensor(up[:, :, :, 2], f[:, :, 1, :, 1], qb[:, :, 1], ALU.mult).then_inc(kq_ready, 1)

            def writes(x):
                steps.link(nc.vector.tensor_tensor(kout[:].rearrange("p (n t a) -> p n t a", t=T, a=2), fac[:, LV].rearrange("p (n t a) -> p n t a", t=T, a=2), pairs_of_keys(), ALU.mult))
                wait(kout_copied, x)
                nc.vector.transpose(koutT[:], kout[:]).then_inc(kout_ready, 1)
                wait(act_proj, 3 * x + 3)
                steps.link(nc.vector.tensor_scalar(nbeta[:], tanh_beta[:], -1.0, -1.0, ALU.mult, ALU.add))
                wait(pool_done, 5 * x)
                nc.vector.tensor_tensor(nbk[:], k[:], nbeta[:], ALU.mult).then_inc(nb_ready, 1)

            def take(it, n):
                l, hg = n // 2, n % 2
                hold(dve, scores, 2 * LV * it + n + 1, passed)
                some = chunks_at(l)
                dst = upper(PA[:, hg, 0:some], l)
                k1, k0 = dst.shape[-2:]
                mask = levels[:, l, 0:UP[l]].rearrange("p (s k) -> p s k", s=k1).unsqueeze(1).to_broadcast([128, some, k1, k0])
                src = ring[n % 4][:, 0:some * 32].rearrange("p (c w) -> p c w", w=32)[:, :, 0:UP[l]].rearrange("p c (s k) -> p c s k", s=k1)
                nc.vector.copy_predicated(dst, mask, src).then_inc(taken, 1)
                hold(dve, taken, 1 + 2 * LV * it + n + 1, passed)

            def times_beta(b, it):
                pbv = Pb[:].rearrange("p (t a) (c y) -> p c t a y", a=2, c=NC)
                for hg in range(2):
                    nb = nbeta[:, 128 * hg:128 * hg + 128].rearrange("p (c t) -> p c t", c=NC).unsqueeze(3).to_broadcast([128, NC, T, 2])
                    nc.vector.tensor_tensor(pbv[:, :, :, :, 2 * b + hg], PA[:, hg].rearrange("p c (t k) -> p c t k", k=3)[:, :, :, 0:2], nb, ALU.mult).then_inc(pa_ready, 1)

            def first():
                rows_stats(0)
                rows_norm(0)
                rows_stats(1)
                decays(0)
                rows_norm(1)
                keys(0)
                for l in range(LV):
                    factors(0, l)
                writes(0)
                steps.restart()

            def project(g):
                with dve.Fori(0, GB // 2) as b2:
                    for b in (b2 * 2, b2 * 2 + 1):
                        it = g * GB + b
                        dve.wait_ge(nb_ready, it + 1)
                        dve.wait_ge(at_copied, 1 + it)
                        rows_stats(it + 2)
                        decays(it + 1)
                        for n in range(3):
                            take(it, n)
                        rows_norm(it + 2)
                        for n in range(3, 6):
                            take(it, n)
                        keys(it + 1)
                        factors(it + 1, 0)
                        factors(it + 1, 1)
                        take(it, 6)
                        factors(it + 1, 2)
                        take(it, 7)
                        take(it, 8)
                        factors(it + 1, 3)
                        take(it, 9)
                        times_beta(b, it)
                        factors(it + 1, 4)
                        writes(it + 1)
                        steps.restart()

            def invert(g):
                dve.wait_ge(unit_diagonal, V)
                dve.wait_ge(lane_sb, 8 * (g + 1))
                for v in range(1, V):
                    parts = 1 if v < V // 4 else 2 if v < V // 2 else 4
                    cuts = [v * n // parts for n in range(parts + 1)]
                    at, products = 0, []
                    for lo, hi in zip(cuts, cuts[1:]):
                        cols, rows = hi - lo, v - lo
                        lp = LP[:, v].rearrange("p (h m) -> p h m", h=4)[:, :, lo:v].unsqueeze(2).to_broadcast([128, 4, cols, rows])
                        x = X[:, lo:v].rearrange("p m (h c) -> p h c m", h=4)[:, :, lo:hi, :]
                        product = tmp[:, at:at + 4 * cols * rows].rearrange("p (h c m) -> p h c m", h=4, c=cols)
                        steps.mark(nc.vector.tensor_tensor(product, lp, x, ALU.mult))
                        products.append((lo, hi, product))
                        at += 4 * cols * rows
                    steps.wait()
                    for lo, hi, product in products:
                        ins = nc.vector.tensor_reduce(X[:, v].rearrange("p (h c) -> p h c", h=4)[:, :, lo:hi], product, axis=AX.X, op=ALU.add)
                        steps.mark(ins)
                    steps.wait()
                dve.sem_inc(inverted, 1)
                steps.restart()

            groups(first, project, invert, lambda g: None, lambda g: None)


def mixture(nc, a, scratch):
    with ExitStack() as ctx:
        m = Memory(nc, ctx)
        acc = m.sb("acc", [128, ST, D])
        ident = m.sb("ident_mix", [128, 128])
        we = [m.sb(f"we{i}", [128, 4, 2, D]) for i in range(WS)]
        w_loaded = [m.sem(f"we_loaded{i}") for i in range(WS)]
        bank = [m.ps(f"mbank{i}") for i in range(4, 8)]
        passed = m.sem("mix_passed")
        with ExitStack() as inner:
            dispatch(nc, a, scratch, Memory(nc, inner), acc, ident, bank, we, w_loaded)
        with ExitStack() as inner:
            answers = m.sb("answers", [128, ST, D])
            cT = [m.sb(f"ccT{i}", [128, ST, N]) for i in range(2)]
            h = [m.sb(f"ch{i}", [N, D]) for i in range(2)]
            c_loaded = [m.sem(f"c_loaded{i}") for i in range(2)]

            def load_batch(sp, b, i, before_h=lambda: None):
                sp.dma_start(cT[i][:].rearrange("p s n -> p (s n)"), scratch.cT[b]).then_inc(c_loaded[i], 16)
                before_h()
                sp.dma_start(h[i][:], scratch.h[b]).then_inc(c_loaded[i], 16)

            experts(nc, a, Memory(nc, inner), acc, answers, ident, bank, we, w_loaded, load_batch, passed)
        with ExitStack() as inner:
            combine(nc, a, Memory(nc, inner), cT, h, c_loaded, load_batch, answers, bank, passed)


def load_expert_weights(sp, a, we, w_loaded, tile, slot):
    w = a.expert_w.rearrange("(s e) (t p) h -> s p e t h", e=4, p=128)
    for e in range(4):
        sp.dma_start(we[slot][:, e], w[tile, :, e]).then_inc(w_loaded[slot], 16)


def dispatch(nc, a, scratch, m, acc, ident, banks, we, w_loaded):
    by_misc, ring = banks[0], banks[1:4]
    logits = m.ps("logits", [128, NS])
    wo, norm_w = m.sb("wo", [128, 2, D]), m.sb("norm_w", [128, 2])
    phi = m.sb("phi", [128, 2, NS])
    bias, rest, parts = m.sb("bias", [128, ST]), m.sb("rest", [128, ST]), m.sb("parts", [128, 3, ST], BF16)
    bias3, ones3 = m.sb("bias3", [3, NS], BF16), m.sb("ones3", [3, N], BF16)
    ot = [m.sb(f"ot{i}", [N, D]) for i in range(2)]
    gt = [m.sb(f"gt{i}", [N, D]) for i in range(2)]
    hx = [m.sb(f"mhx{i}", [N, D]) for i in range(2)]
    h2 = [m.sb(f"h2{i}", [N, D]) for i in range(2)]
    fresh = [m.sb(f"fresh{i}", [N, D]) for i in range(2)]
    x = [m.sb(f"mx{i}", [N, D]) for i in range(4)]
    xT = [m.sb(f"mxT{i}", [128, 2, N]) for i in range(2)]
    y, y2, yn, yT = m.sb("y", [N, D]), m.sb("y2", [N, D]), m.sb("yn", [N, D]), m.sb("yT", [128, 2, N])
    ms, rr = m.sb("ms", [N, H]), m.sb("rr", [N, H])
    stats, mv, rstd = m.sb("mstats", [N, 6]), m.sb("mmv", [N, 2]), m.sb("mrstd", [N, 1])
    Dx = [m.sb(f"Dx{i}", [N, NS]) for i in range(4)]
    Cx = [m.sb(f"Cx{i}", [N, NS]) for i in range(4)]
    m1, s1 = m.sb("m1", [N, NEXP]), m.sb("s1", [N, NEXP])
    m2, s2 = m.sb("m2", [N, PS]), m.sb("s2", [N, PS])
    r1, r2 = m.sb("r1", [N, NEXP]), m.sb("r2", [N, PS])
    cT = [m.sb(f"cT{i}", [128, ST, N]) for i in range(2)]
    bias_loaded, phi_loaded = m.sem("bias_loaded"), m.sem("phi_loaded")
    consts, split, bias_ready, acc_zero = m.sem("mconsts"), m.sem("bias_split"), m.sem("bias_ready"), m.sem("acc_zero")
    loaded = [m.sem("mloaded0"), m.sem("mloaded1")]
    squares, roots, yn_ready, yT_ps, yT_ready, projected = (m.sem(n) for n in ("squares", "roots", "yn_ready", "yT_ps", "yT_ready", "wo_done"))
    h2_ready, moments, rstds, x_ready, x_kept, xT_ps, xT_ready = (
        m.sem(n) for n in ("h2_ready", "mmoments", "mrstds", "mx_ready", "mx_kept", "mxT_ps", "mxT_ready"))
    l_ps, l_copied, e1, max2, e2, exp1, exp2, inv1, inv2, D_ready, C_ready = (
        m.sem(n) for n in ("l_ps", "l_copied", "e1_ready", "max2", "e2_ready", "exp1", "exp2", "inv1", "inv2", "D_ready", "C_ready"))
    cT_ps, cT_sb, acc_ps, acc_added = (m.sem(n) for n in ("cT_ps", "cT_sb", "acc_ps", "acc_added"))
    h_out = [m.sem("h_out0"), m.sem("h_out1")]
    cT_out = [m.sem("cT_out0"), m.sem("cT_out1")]
    dve_steps, act_steps, passed = m.sem("mdve_steps"), m.sem("mact_steps"), m.sem("mpassed")
    PAIRS = B // 2

    def known(h):
        return isinstance(h, int)

    def all_steps(engine, first, step, summing, end):
        first()
        for i in range(2):
            step(0, i, 0)
        end()
        with engine.Fori(0, PAIRS // 2 - 1) as q:
            for p in (1, 0):
                for i in range(2):
                    step(2 * q + 2 - p, i, p)
            end()
        for i in range(2):
            step(PAIRS - 1, i, 1)
        for n in range(8):
            summing(PAIRS - 1, n, 1)
        end()

    def nothing(*_):
        return None

    block = m.ctx.enter_context(nc.Block())

    @block.sync
    def _(sp):
        from_one(sp, cT_out[0], cT_out[1])
        def load(f, i):
            sp.dma_start(ot[i][:].rearrange("p (g w) -> p g w", g=2), scratch.o[f, :, 0:N, :].rearrange("g t w -> t g w")).then_inc(loaded[i], 16)
            sp.dma_start(gt[i][:], scratch.gate[f, 0:N, :]).then_inc(loaded[i], 16)
            sp.dma_start(hx[i][0:1 + NPOS], scratch.z[f]).then_inc(loaded[i], 16)
            sp.dma_start(hx[i][1 + NPOS:N], a.txt[f]).then_inc(loaded[i], 16)

        def store_h(f, i):
            hold(sp, h2_ready, f + 1, passed)
            sp.dma_start(scratch.h[f], h2[i][:]).then_inc(h_out[i], 16)

        def first():
            load(0, 0)
            sp.dma_start(ident[:], a.ident).then_inc(consts, 16)
            sp.dma_start(wo[:], a.Wo.rearrange("(t p) n -> p t n", p=128)).then_inc(consts, 16)
            sp.dma_start(norm_w[:], a.norm_w).then_inc(consts, 16)
            sp.dma_start(bias[:], a.phi_b.rearrange("(p c) -> p c", p=128)).then_inc(bias_loaded, 16)
            sp.dma_start(phi[:], a.phi_wT.rearrange("(t p) n -> p t n", p=128)).then_inc(phi_loaded, 16)
            load(1, 1)
            store_h(0, 0)
            sp.wait_ge(split, 5)
            for r in range(3):
                sp.dma_start(bias3[r:r + 1, :].rearrange("o (p c) -> o p c", p=128), parts[:, r, :]).then_inc(bias_ready, 16)
            for tile in range(WS):
                load_expert_weights(sp, a, we, w_loaded, tile, tile)

        def store_weights(J, i):
            hold(sp, cT_sb, 1 + 8 * J + 4 * i + 4, passed)
            sp.dma_start(scratch.cT[2 * J + i], cT[i][:].rearrange("p s n -> p (s n)")).then_inc(cT_out[i], 16)

        def step(J, i, p):
            h = 2 * J + i
            if not (known(h) and h + 2 >= B):
                load(h + 2, i)
            if not (known(h) and h + 1 >= B):
                store_h(h + 1, 1 - i)
            if not (known(J) and J == 0):
                store_weights(J - 1, i)

        def summing(J, n, p):
            if n % 4 == 3:
                store_weights(J, n // 4)

        all_steps(sp, first, step, summing, nothing)
        for i in range(2):
            sp.wait_ge(h_out[i], 16 * PAIRS)
            sp.wait_ge(cT_out[i], 1 + 16 * PAIRS)

    @block.tensor
    def _(pe):
        from_one(pe, cT_ps, acc_ps)
        def wait(sem, value):
            if not (isinstance(value, int) and value <= 0):
                hold(pe, sem, value, passed)

        def gated(f):
            wait(yn_ready, f + 1)
            wait(xT_ready, f)
            wait(h2_ready, f)
            for t in range(2):
                last = nc.tensor.transpose(by_misc[:, 128 * t:128 * t + N], yn[:, 128 * t:128 * t + 128], ident[0:N, 0:N])
            last.then_inc(yT_ps, 1)

        def project(f):
            wait(yT_ready, f + 1)
            for t in range(2):
                last = nc.tensor.matmul(by_misc[0:N, D:], yT[:, t, :], wo[:, t, :], start=t == 0, stop=t == 1)
            last.then_inc(projected, 1)

        def rows(f, i):
            wait(x_ready, f + 1)
            for t in range(2):
                last = nc.tensor.transpose(by_misc[:, 128 * t:128 * t + N], fresh[i][:, 128 * t:128 * t + 128], ident[0:N, 0:N])
            last.then_inc(xT_ps, 1)

        def summing(J, n, p):
            for kind in range(2):
                turn = 2 * n + kind
                if turn < 3:
                    wait(cT_sb, 1 + 8 * J)
                    wait(acc_added, 1 + 8 * J)
                elif kind == 0:
                    wait(acc_added, 1 + 8 * J + (turn - 3) // 2 + 1)
                else:
                    wait(cT_sb, 1 + 8 * J + (turn - 3) // 2 + 1)
                out = ring[turn % 3]
                if kind == 0:
                    i, s0 = n // 4, 4 * (n % 4)
                    wait(C_ready, 2 * J + i + 1)
                    for s in range(4):
                        last = nc.tensor.transpose(out[:, 128 * s:128 * s + N], Cx[2 * p + i][:, 128 * (s0 + s):128 * (s0 + s) + 128], ident[0:N, 0:N])
                    last.then_inc(cT_ps, 1)
                else:
                    wait(D_ready, 2 * J + 2)
                    wait(x_kept, 2 * J + 2)
                    for s in range(2):
                        st = 2 * n + s
                        for i in range(2):
                            last = nc.tensor.matmul(out[:, D * s:D * s + D], Dx[2 * p + i][:, 128 * st:128 * st + 128], x[2 * p + i][:], start=i == 0, stop=i == 1)
                    last.then_inc(acc_ps, 1)

        def first():
            gated(0)
            project(0)
            rows(0, 0)
            pe.wait_ge(phi_loaded, 16)
            pe.wait_ge(bias_ready, 48)

        def step(J, i, p):
            h = 2 * J + i
            wait(xT_ready, h + 1)
            wait(l_copied, h)
            for s in range(4):
                cols = slice(512 * s, 512 * s + 512)
                for t in range(2):
                    nc.tensor.matmul(logits[0:N, cols], xT[i][:, t, :], phi[:, t, cols], start=t == 0, stop=False)
                last = nc.tensor.matmul(logits[0:N, cols], ones3[:], bias3[:, cols], start=False, stop=True)
            last.then_inc(l_ps, 1)
            sums = summing if not (known(J) and J == 0) else nothing
            front = not (known(h) and h + 1 >= B)
            if front:
                gated(h + 1)
            sums(J - 1, 4 * i, 1 - p)
            if front:
                project(h + 1)
            sums(J - 1, 4 * i + 1, 1 - p)
            sums(J - 1, 4 * i + 2, 1 - p)
            if front:
                rows(h + 1, 1 - i)
            sums(J - 1, 4 * i + 3, 1 - p)

        pe.wait_ge(consts, 16 * 3)
        all_steps(pe, first, step, summing, nothing)

    @block.scalar
    def _(act):
        from_one(act, cT_sb)
        steps = Steps(act, act_steps)

        def wait(sem, value):
            if not (isinstance(value, int) and value <= 0):
                act.wait_ge(sem, value)

        def gate_roots(f):
            wait(squares, f + 1)
            wait(yn_ready, f)
            steps.link(nc.scalar.activation(rr[:], ms[:], ACT.Ln, bias=QK_EPS, scale=1.0 / HD))
            nc.scalar.activation(rr[:], rr[:], ACT.Exp, scale=-0.5).then_inc(roots, 1)

        def gated(f):
            wait(yT_ps, f + 1)
            wait(projected, f)
            for t in range(2):
                last = nc.scalar.activation(yT[:, t, :], by_misc[:, 128 * t:128 * t + N], ACT.Copy, scale=norm_w[:, t:t + 1])
            last.then_inc(yT_ready, 1)

        def row_roots(f):
            wait(moments, f + 1)
            wait(x_kept, f)
            inverse_root(nc, steps, rstd[:], mv[:, 1:2], LN_EPS).then_inc(rstds, 1)

        def rows(f, i):
            wait(xT_ps, f + 1)
            wait(l_ps, f - 1)
            nc.scalar.activation(xT[i][:], by_misc[:, 0:256].rearrange("p (t n) -> p t n", t=2)[:, :, 0:N], ACT.Copy).then_inc(xT_ready, 1)

        def summing(J, n, p):
            i, s0 = n // 4, 4 * (n % 4)
            if n % 4 == 0:
                wait(cT_out[i], 1 + 16 * J)
            wait(cT_ps, 1 + 8 * J + n + 1)
            nc.scalar.activation(cT[i][:, s0:s0 + 4, :], ring[(2 * n) % 3][:].rearrange("p (s n) -> p s n", s=4)[:, :, 0:N], ACT.Copy).then_inc(cT_sb, 1)

        def first():
            gate_roots(0)
            gated(0)
            row_roots(0)
            rows(0, 0)
            gate_roots(1)

        def step(J, i, p):
            h = 2 * J + i
            slot = 2 * p + i
            wait(l_ps, h + 1)
            wait(cT_ps, 1 + 8 * (J - 1) if not (known(J) and J == 0) else 0)
            nc.scalar.activation(Cx[slot][:], logits[0:N, :], ACT.Copy).then_inc(l_copied, 1)
            sums = summing if not (known(J) and J == 0) else nothing
            front = not (known(h) and h + 1 >= B)
            if front:
                gated(h + 1)
            sums(J - 1, 4 * i, 1 - p)
            sums(J - 1, 4 * i + 1, 1 - p)
            if front:
                row_roots(h + 1)
            sums(J - 1, 4 * i + 2, 1 - p)
            wait(e1, h + 1)
            nc.scalar.activation(Dx[slot][:], Dx[slot][:], ACT.Exp).then_inc(exp1, 1)
            if front:
                rows(h + 1, 1 - i)
            sums(J - 1, 4 * i + 3, 1 - p)
            if not (known(h) and h + 2 >= B):
                gate_roots(h + 2)
            wait(e2, h + 1)
            nc.scalar.activation(Cx[slot][:], Cx[slot][:], ACT.Exp).then_inc(exp2, 1)

        act.wait_ge(consts, 16 * 3)
        nc.scalar.preload_act_table_set(LN_EXP)
        all_steps(act, first, step, summing, steps.restart)

    @block.gpsimd
    def _(pool):
        def by_expert(t, r):
            return t[:].rearrange("p (n s) -> p n s", n=NEXP), r[:].unsqueeze(2).to_broadcast([N, NEXP, PS])

        def by_slot(t, r):
            return t[:].rearrange("p (n s) -> p n s", n=NEXP), r[:].unsqueeze(1).to_broadcast([N, NEXP, PS])

        def step(J, i, p):
            h = 2 * J + i
            pool.wait_ge(e1, h + 1)
            pool.wait_ge(max2, h + 1)
            c, r = by_slot(Cx[2 * p + i], m2)
            pool.tensor_tensor(c, c, r, ALU.subtract).then_inc(e2, 1)
            pool.wait_ge(inv1, h + 1)
            d, r = by_expert(Dx[2 * p + i], r1)
            pool.tensor_tensor(d, d, r, ALU.mult).then_inc(D_ready, 1)
            pool.wait_ge(inv2, h + 1)
            c, r = by_slot(Cx[2 * p + i], r2)
            pool.tensor_tensor(c, c, r, ALU.mult).then_inc(C_ready, 1)

        nc.gpsimd.memset(acc[:], 0.0).then_inc(acc_zero, 1)
        all_steps(pool, nothing, step, nothing, nothing)

    @block.vector
    def _(dve):
        from_one(dve, acc_added)
        steps = Steps(dve, dve_steps)

        def wait(sem, value):
            if not (isinstance(value, int) and value <= 0):
                dve.wait_ge(sem, value)

        def gate_squares(f, i):
            wait(loaded[i], 64 * (f // 2 + 1) if known(f) else 64 * f[1])
            f = f if known(f) else f[0]
            steps.link(nc.vector.tensor_tensor(y[:], ot[i][:], gt[i][:], ALU.mult))
            steps.link(nc.vector.tensor_tensor(y2[:], y[:], y[:], ALU.mult))
            wait(roots, f)
            nc.vector.tensor_reduce(ms[:], y2[:].rearrange("p (h w) -> p h w", h=H), axis=AX.X, op=ALU.add).then_inc(squares, 1)

        def gate_norm(f):
            wait(roots, f + 1)
            wait(yT_ps, f)
            nc.vector.tensor_tensor(yn[:].rearrange("p (h w) -> p h w", h=H), y[:].rearrange("p (h w) -> p h w", h=H),
                                    rr[:].unsqueeze(2).to_broadcast([N, H, HD]), ALU.mult).then_inc(yn_ready, 1)

        def add_rows(f, i, before):
            wait(projected, f + 1)
            wait(h_out[i], 16 * before)
            nc.vector.tensor_tensor(h2[i][:], by_misc[0:N, D:], hx[i][:], ALU.add).then_inc(h2_ready, 1)
            wait(h2_ready, f + 1)
            steps.link(nc.vector.bn_stats(stats[:], h2[i][:]))
            nc.vector.bn_aggr(mv[:], stats[:]).then_inc(moments, 1)

        def norm_rows(f, i):
            wait(rstds, f + 1)
            wait(xT_ps, f - 1)
            nc.vector.tensor_scalar(fresh[i][:], h2[i][:], mv[:, 0:1], rstd[:], ALU.subtract, ALU.mult).then_inc(x_ready, 1)

        def summing(J, n, p):
            wait(acc_ps, 1 + 8 * J + n + 1)
            part = acc[:, 2 * n:2 * n + 2, :].rearrange("p s d -> p (s d)")
            wait(acc_added, 1 + 8 * J)
            nc.vector.tensor_tensor(part, ring[(2 * n + 1) % 3][:], part, ALU.add).then_inc(acc_added, 1)

        def first():
            gate_squares(0, 0)
            gate_norm(0)
            add_rows(0, 0, 0)
            norm_rows(0, 0)
            dve.wait_ge(bias_loaded, 16)
            nc.vector.memset(ones3[:], 1.0).then_inc(split, 1)
            steps.link(nc.vector.tensor_copy(parts[:, 0, :], bias[:]))
            steps.link(nc.vector.tensor_tensor(rest[:], bias[:], parts[:, 0, :], ALU.subtract))
            steps.link(nc.vector.tensor_copy(parts[:, 1, :], rest[:]))
            steps.link(nc.vector.tensor_tensor(rest[:], rest[:], parts[:, 1, :], ALU.subtract))
            steps.link(nc.vector.tensor_copy(parts[:, 2, :], rest[:]))
            dve.sem_inc(split, 4)
            gate_squares(1, 1)
            gate_norm(1)
            dve.wait_ge(acc_zero, 1)

        def step(J, i, p):
            h = 2 * J + i
            slot = 2 * p + i
            d, c = (t[slot][:].rearrange("p (n s) -> p n s", n=NEXP) for t in (Dx, Cx))
            sums = summing if not (known(J) and J == 0) else nothing
            front = not (known(h) and h + 1 >= B)
            done = 8 * (J - 1) if not (known(J) and J == 0) else 0
            wait(acc_ps, 1 + done)
            nc.vector.tensor_scalar(x[slot][:], h2[i][:], mv[:, 0:1], rstd[:], ALU.subtract, ALU.mult).then_inc(x_kept, 1)
            wait(l_copied, h + 1)
            steps.link(nc.vector.tensor_reduce(m1[:], c, axis=AX.X, op=ALU.max))
            sums(J - 1, 4 * i, 1 - p)
            if front:
                add_rows(h + 1, 1 - i, J + i)
            nc.vector.tensor_tensor(d, c, m1[:].unsqueeze(2).to_broadcast([N, NEXP, PS]), ALU.subtract).then_inc(e1, 1)
            sums(J - 1, 4 * i + 1, 1 - p)
            if front:
                norm_rows(h + 1, 1 - i)
            wait(e2, h)
            nc.vector.tensor_reduce(m2[:], c.rearrange("p n s -> p s n"), axis=AX.X, op=ALU.max).then_inc(max2, 1)
            sums(J - 1, 4 * i + 2, 1 - p)
            wait(exp1, h + 1)
            steps.link(nc.vector.tensor_reduce(s1[:], d, axis=AX.X, op=ALU.add))
            wait(D_ready, h)
            nc.vector.reciprocal(r1[:], s1[:]).then_inc(inv1, 1)
            sums(J - 1, 4 * i + 3, 1 - p)
            more = not (known(h) and h + 2 >= B)
            if more:
                gate_squares(h + 2 if known(h) else (h + 2, J + 2), i)
                gate_norm(h + 2)
            wait(exp2, h + 1)
            steps.link(nc.vector.tensor_reduce(s2[:], c.rearrange("p n s -> p s n"), axis=AX.X, op=ALU.add))
            wait(C_ready, h)
            nc.vector.reciprocal(r2[:], s2[:]).then_inc(inv2, 1)

        all_steps(dve, first, step, summing, steps.restart)


def experts(nc, a, m, acc, answers, ident, banks, we, w_loaded, load_batch, passed):
    CLIP = 3 * ST // 4
    eb = m.sb("eb", [128, ST, D])
    stats, mv, rstd = m.sb("estats", [128, ST, 6]), m.sb("emv", [128, ST, 2]), m.sb("erstd", [128, ST])
    th = [m.sb(f"th{i}", [128, D]) for i in range(2)]
    thT = [m.sb(f"thT{i}", [128, 2, 128]) for i in range(2)]
    b_loaded = m.sem("eb_loaded")
    moments, rstds, normed, th_ready, thT_ps, thT_ready, y_ps, y_sb = (
        m.sem(n) for n in ("e_moments", "e_rstds", "e_normed", "th_ready", "thT_ps", "thT_ready", "ans_ps", "ans_sb"))
    act_steps, dve_steps, clipped = (m.sem(n) for n in ("e_act_steps", "e_dve_steps", "e_clipped"))
    block = m.ctx.enter_context(nc.Block())

    @block.sync
    def _(sp):
        for e in range(4):
            sp.dma_start(eb[32 * e:32 * e + 32], a.expert_b.rearrange("(s e) h -> e s h", e=4)[e].partition_broadcast(32)).then_inc(b_loaded, 16)
        with sp.Fori(0, ST // WS - 1) as j:
            for slot in range(WS):
                hold(sp, y_ps, 1 + WS * j + slot + 1, passed)
                load_expert_weights(sp, a, we, w_loaded, WS * (j + 1) + slot, slot)
        for i in range(2):
            load_batch(sp, i, i)

    @block.gpsimd
    def _(pool):
        pool.tensor_scalar(acc[:, CLIP:], acc[:, CLIP:], -33000.0, 65000.0, ALU.max, ALU.min).then_inc(clipped, 1)

    @block.vector
    def _(dve):
        from_one(dve, y_sb)
        steps = Steps(dve, dve_steps)
        steps.link(nc.vector.tensor_scalar(acc[:, 0:CLIP], acc[:, 0:CLIP], -33000.0, 65000.0, ALU.max, ALU.min))
        for s in range(ST):
            if s == CLIP:
                dve.wait_ge(clipped, 1)
            steps.mark(nc.vector.bn_stats(stats[:, s], acc[:, s]))
        steps.wait()
        for s in range(ST):
            nc.vector.bn_aggr(mv[:, s], stats[:, s]).then_inc(moments, 1)
        dve.wait_ge(rstds, 1)
        for s in range(ST):
            nc.vector.tensor_scalar(acc[:, s], acc[:, s], mv[:, s, 0:1], rstd[:, s:s + 1], ALU.subtract, ALU.mult).then_inc(normed, 1)
        dve.wait_ge(b_loaded, 64)
        with dve.Fori(0, ST // WS) as j:
            for slot in range(WS):
                n, i = WS * j + slot, slot % 2
                dve.wait_ge(y_ps, 1 + n + 1)
                nc.vector.tensor_tensor(answers[:, n, :], banks[2 + i][:, 0:D], eb[:, n, :], ALU.add).then_inc(y_sb, 1)

    @block.scalar
    def _(act):
        from_one(act, thT_ready)
        steps = Steps(act, act_steps)
        nc.scalar.preload_act_table_set(LN_EXP)
        act.wait_ge(moments, ST)
        inverse_root(nc, steps, rstd[:], mv[:, :, 1], LN_EPS).then_inc(rstds, 1)
        nc.scalar.preload_act_table_set(SILU)
        with act.Fori(0, ST // WS) as j:
            for slot in range(WS):
                n, i = WS * j + slot, slot % 2
                act.wait_ge(normed, n + 1)
                act.wait_ge(thT_ps, 1 + n)
                nc.scalar.activation(th[i][:], acc[:, n, :], ACT.Tanh).then_inc(th_ready, 1)
                act.wait_ge(thT_ps, 1 + n + 1)
                act.wait_ge(y_ps, 1 + n)
                nc.scalar.activation(thT[i][:], banks[i][:, 0:D].rearrange("p (t n) -> p t n", t=2), ACT.Copy).then_inc(thT_ready, 1)

    @block.tensor
    def _(pe):
        from_one(pe, thT_ps, y_ps)
        with pe.Fori(0, ST // WS) as j:
            for slot in range(WS):
                n, i = WS * j + slot, slot % 2
                hold(pe, th_ready, n + 1, passed)
                hold(pe, thT_ready, 1 + n, passed)
                for t in range(2):
                    last = nc.tensor.transpose(banks[i][:, 128 * t:128 * t + 128], th[i][:, 128 * t:128 * t + 128], ident[:])
                last.then_inc(thT_ps, 1)
                hold(pe, thT_ready, 1 + n + 1, passed)
                hold(pe, w_loaded[slot], 64 * (j + 1), passed)
                hold(pe, y_sb, 1 + WS * j + max(0, slot - 1), passed)
                for e in range(4):
                    for t in range(2):
                        last = nc.tensor.matmul(banks[2 + i][32 * e:32 * e + 32, 0:D], thT[i][:, t, 32 * e:32 * e + 32], we[slot][:, e, t, :], start=t == 0, stop=t == 1)
                last.then_inc(y_ps, 1)


def combine(nc, a, m, cT, h, loaded, load_batch, answers, banks, passed):
    o = [m.sb(f"co{i}", [N, D]) for i in range(2)]
    stored = [m.sem("c_stored0"), m.sem("c_stored1")]
    summed, added = [m.sem("c_summed0"), m.sem("c_summed1")], [m.sem("c_added0"), m.sem("c_added1")]
    block = m.ctx.enter_context(nc.Block())

    @block.sync
    def _(sp):
        with sp.Fori(0, B // 2 - 1) as j:
            for i in range(2):
                hold(sp, summed[i], 1 + j + 1, passed)
                load_batch(sp, 2 * j + 2 + i, i, lambda: hold(sp, added[i], 1 + j + 1, passed))

    @block.tensor
    def _(pe):
        from_one(pe, summed[0], summed[1])
        with pe.Fori(0, B // 2) as j:
            for i in range(2):
                hold(pe, loaded[i], 32 * (j + 1), passed)
                hold(pe, added[i], 1 + j, passed)
                for s in range(ST):
                    last = nc.tensor.matmul(banks[i][0:N, 0:D], cT[i][:, s, :], answers[:, s, :], start=s == 0, stop=s == ST - 1)
                last.then_inc(summed[i], 1)

    @block.vector
    def _(dve):
        from_one(dve, added[0], added[1])
        with dve.Fori(0, B // 2) as j:
            for i in range(2):
                dve.wait_ge(summed[i], 1 + j + 1)
                dve.wait_ge(loaded[i], 32 * (j + 1))
                dve.wait_ge(stored[i], 1 + 16 * j)
                nc.vector.tensor_tensor(o[i][:], banks[i][0:N, 0:D], h[i][:], ALU.add).then_inc(added[i], 1)

    @block.scalar
    def _(act):
        from_one(act, stored[0], stored[1])
        with act.Fori(0, B // 2) as j:
            for i in range(2):
                hold(act, added[i], 1 + j + 1, passed)
                act.dma_start(a.out[2 * j + i], o[i][:]).then_inc(stored[i], 16)
        for i in range(2):
            act.wait_ge(stored[i], 1 + 16 * (B // 2))


class _Arrays:
    pass


def build(nc, arrays):
    scratch = _Arrays()
    scratch.z = nc.dram_tensor("scratch_z", (B, 1 + NPOS, D), F32, kind="Internal").ap()
    scratch.v = nc.dram_tensor("scratch_v", (B + 1, 2, NT, D // 2), F32, kind="Internal").ap()
    scratch.gate = nc.dram_tensor("scratch_gate", (B + 1, NT, D), F32, kind="Internal").ap()
    scratch.slab = nc.dram_tensor("scratch_slab", (NC, 128, B + 1, SLAB), F32, kind="Internal").ap()
    scratch.o = nc.dram_tensor("scratch_o", (B, 2, NT, D // 2), F32, kind="Internal").ap()
    scratch.h = nc.dram_tensor("scratch_h", (B, N, D), F32, kind="Internal").ap()
    scratch.cT = nc.dram_tensor("scratch_cT", (B, 128, ST * N), F32, kind="Internal").ap()
    for part in (tokenizer, attention, mixture):
        part(nc, arrays, scratch)


def lay_out(inputs):
    import numpy as np
    x = {n: np.ascontiguousarray(v) for n, v in inputs.items()}
    p = x["x"].reshape(B, 3, GRID, 16, GRID, 16).transpose(2, 4, 0, 3, 5, 1).reshape(B * NPOS // 128, 128, PD)
    level = np.zeros((LV, V, 2 * T), np.int32)
    for l in range(LV):
        up = [(t, kind) for t in range(T) for kind in range(3)
              if ((kind > 0) if l == 0 else (2 * t) >> l & 1)]
        for at, (t, kind) in enumerate(up):
            q = 2 * t + min(kind, 1)
            for key in range(V):
                level[l, key, at] = key < q and key >> l != q >> l and key >> (l + 1) == q >> (l + 1)
                if kind == 2 and l == 0 and key == q:
                    level[l, key, at] = 1
    return {
        "patches": p,
        "txt": x["txt"],
        "ln1_g": x["L0_tok_ln1_g"].reshape(6, 128).T, "ln1_b": x["L0_tok_ln1_b"].reshape(6, 128).T,
        "W_proj": x["L0_tok_W_proj"], "b_proj": x["L0_tok_b_proj"],
        "ln2_g": x["L0_tok_ln2_g"], "ln2_b": x["L0_tok_ln2_b"],
        "cls_token": x["L0_tok_cls_token"].reshape(D), "pos_emb": x["L0_tok_pos_emb"][0],
        "Wq": x["L0_attn_Wq"], "Wk": x["L0_attn_Wk"], "Wv": x["L0_attn_Wv"],
        "Wf1": x["L0_attn_Wf1"], "Wf2": x["L0_attn_Wf2"], "Wbeta": x["L0_attn_Wbeta"],
        "Wog1": x["L0_attn_Wog1"], "Wog2": x["L0_attn_Wog2"],
        "norm_w": x["L0_attn_norm_w"].reshape(2, 128).T, "Wo": x["L0_attn_Wo"],
        "phi_wT": x["L0_ffn_phi_w"].T, "phi_b": x["L0_ffn_phi_b"],
        "expert_w": x["L0_ffn_expert_w"], "expert_b": x["L0_ffn_expert_b"],
        "ident": np.eye(128, dtype=np.float32),
        "head_ones": np.kron(np.eye(4, dtype=np.float32), np.ones((HD, HD), np.float32)),
        "levels": np.tile(level.transpose(1, 0, 2), (4, 1, 1)).reshape(128, LV * 2 * T),
        "in_chunk": np.tile((np.arange(NC * 2 * V) % V > 0).astype(np.float32), (128, 1)),
    }


def kernel(**inputs):
    import numpy as np
    import concourse.bacc as bacc
    from concourse.bass_utils import run_bass_kernel_spmd

    nc = bacc.Bacc("TRN2", target_bir_lowering=False, num_devices=1)
    data = {name: np.ascontiguousarray(v) for name, v in lay_out(inputs).items()}
    arrays = _Arrays()
    for name, v in data.items():
        arrays.__dict__[name] = nc.dram_tensor(f"in_{name}", v.shape, mybir.dt.from_np(v.dtype), kind="ExternalInput").ap()
    arrays.out = nc.dram_tensor("out", (B, N, D), F32, kind="ExternalOutput").ap()
    build(nc, arrays)
    result = run_bass_kernel_spmd(nc, [{f"in_{name}": v for name, v in data.items()}], core_ids=[0])
    return result.results[0]["out"]
```
